# Optimizing a Trainium2 kernel written in Bass

```python
import numpy as np
import jax
import jax.numpy as jnp

def _softmax(x, axis=-1):
    return jax.nn.softmax(x, axis=axis)

def _gelu(x):
    return jax.nn.gelu(x, approximate=True)

def _silu(x):
    return jax.nn.silu(x)

def _sigmoid(x):
    return jax.nn.sigmoid(x)

def _layernorm(x, axis=-1, eps=1e-05):
    m = jnp.mean(x, axis=axis, keepdims=True)
    v = jnp.var(x, axis=axis, keepdims=True)
    return (x - m) / jnp.sqrt(v + eps)

def _scatter_add(tgt, idx, src, axis=0):
    return tgt.at[idx].add(src)

def _segment_sum(src, seg, n):
    return jax.ops.segment_sum(src, seg, n)
kernel_name = 'mk_sandwich_d1_jaxref_r8_9b399d'

def setup_inputs(seed: int=0):
    np.random.seed(seed)
    _w = jnp.asarray

    def _L0_attn_setup():
        import jax, jax.numpy as jnp
        import numpy as np
        EMB, HEADS = (128, 16)
        S = EMB // HEADS
        key = jax.random.key(seed)
        ks = jax.random.split(key, 7)
        b, t = (2, 256)
        sc = 0.02
        return {'x': jax.random.normal(ks[0], (b, t, EMB), jnp.float32), 'W_down': jax.random.normal(ks[1], (EMB, EMB), jnp.float32) * sc, 'tokeys': jax.random.normal(ks[2], (HEADS, S, S), jnp.float32) * sc, 'toqueries': jax.random.normal(ks[3], (HEADS, S, S), jnp.float32) * sc, 'tovalues': jax.random.normal(ks[4], (HEADS, S, S), jnp.float32) * sc, 'W_unify': jax.random.normal(ks[5], (EMB, EMB), jnp.float32) * sc, 'b_unify': jax.random.normal(ks[6], (EMB,), jnp.float32) * sc}
    _L0_attn_in = _L0_attn_setup()

    def _L0_ffn_setup():
        import jax, jax.numpy as jnp
        import numpy as np
        DIM = 128
        DEPTH = 6
        HEADS = 16
        DIM_HEAD = 64
        WINDOW = 32
        INNER = HEADS * DIM_HEAD
        DIM_INNER = int(DIM * 4 * 2 / 3)
        QK_SCALE = 8.0

        def shift_tokens(t):
            a, s = jnp.split(t, 2, -1)
            s = jnp.pad(s, ((0, 0), (1, 0), (0, 0)))[:, :-1]
            return jnp.concatenate([a, s], -1)

        def l2norm(t):
            return t / jnp.maximum(jnp.linalg.norm(t, axis=-1, keepdims=True), 1e-12)

        def rotate_half(x):
            x1, x2 = jnp.split(x, 2, -1)
            return jnp.concatenate([-x2, x1], -1)

        def rotary_tables(n):
            half = jnp.arange(0, DIM_HEAD, 2, dtype=jnp.float32)
            inv_freq = 1.0 / 10000.0 ** (half / DIM_HEAD)
            t = jnp.arange(n, dtype=jnp.float32)
            freqs = t[:, None] * inv_freq[None, :]
            freqs = jnp.concatenate([freqs, freqs], -1)
            base_scale = (half + 0.4 * DIM_HEAD) / (1.4 * DIM_HEAD)
            power = (t - n // 2) / (WINDOW // 2)
            scale = base_scale[None, :] ** power[:, None]
            scale = jnp.concatenate([scale, scale], -1)
            return (freqs, scale)

        def local_attention(q, k, v):
            b, h, n, d = q.shape
            w = WINDOW
            nw = n // w
            bq = q.reshape(b, h, nw, w, d)
            bk = k.reshape(b, h, nw, w, d)
            bv = v.reshape(b, h, nw, w, d)

            def look(t):
                p = jnp.pad(t, ((0, 0), (0, 0), (1, 0), (0, 0), (0, 0)))
                return jnp.concatenate([p[:, :, :nw], p[:, :, 1:]], axis=3)
            bk2, bv2 = (look(bk), look(bv))
            seq = jnp.arange(n).reshape(nw, w)
            seq_p = jnp.pad(seq, ((1, 0), (0, 0)), constant_values=-1)
            jt = jnp.concatenate([seq_p[:nw], seq_p[1:]], axis=1)
            it = seq[:, :, None]
            jb = jt[:, None, :]
            mask = (it < jb) | (it > jb + w) | (jb == -1)
            sim = jnp.einsum('bhwie,bhwje->bhwij', bq, bk2) * QK_SCALE
            sim = jnp.where(mask, -jnp.finfo(sim.dtype).max, sim)
            attn = jax.nn.softmax(sim, -1)
            out = jnp.einsum('bhwij,bhwje->bhwie', attn, bv2)
            return out.reshape(b, h, n, d)

        def attn_layer(x, Wqkv, qs, ksc, Wo):
            b, n, _ = x.shape
            qkv = x @ Wqkv
            q, k, v = jnp.split(qkv, 3, -1)
            sh = lambda t: t.reshape(b, n, HEADS, DIM_HEAD).transpose(0, 2, 1, 3)
            q, k, v = (sh(q), sh(k), sh(v))
            q = l2norm(q) * qs
            k = l2norm(k) * ksc
            freqs, scale = rotary_tables(n)
            cos, sin = (jnp.cos(freqs), jnp.sin(freqs))
            q = q * cos * scale + rotate_half(q) * sin * scale
            inv = 1.0 / scale
            k = k * cos * inv + rotate_half(k) * sin * inv
            out = local_attention(q, k, v)
            out = out.transpose(0, 2, 1, 3).reshape(b, n, INNER)
            return out @ Wo

        def ffn_layer(x, g, bln, W1, b1, W2, b2):
            mu = x.mean(-1, keepdims=True)
            var = ((x - mu) ** 2).mean(-1, keepdims=True)
            xn = (x - mu) / jnp.sqrt(var + 1e-05) * g + bln
            hg = xn @ W1 + b1
            a, gate = jnp.split(hg, 2, -1)
            return a * jax.nn.gelu(gate, approximate=False) @ W2 + b2
        key = jax.random.key(seed)
        ks = jax.random.split(key, 8)
        B, N = (2, 256)
        init = lambda k, shape: jax.random.normal(k, shape, jnp.float32) * 0.02
        return {'x': jax.random.normal(ks[0], (B, N, DIM), jnp.float32), 'Wqkv': init(ks[1], (DEPTH, DIM, 3 * INNER)), 'q_scale': jnp.ones((DEPTH, DIM_HEAD), jnp.float32), 'k_scale': jnp.ones((DEPTH, DIM_HEAD), jnp.float32), 'Wo': init(ks[2], (DEPTH, INNER, DIM)), 'ln_g': jnp.ones((DEPTH, DIM), jnp.float32), 'ln_b': jnp.zeros((DEPTH, DIM), jnp.float32), 'W1': init(ks[3], (DEPTH, DIM, 2 * DIM_INNER)), 'b1': jnp.zeros((DEPTH, 2 * DIM_INNER), jnp.float32), 'W2': init(ks[4], (DEPTH, DIM_INNER, DIM)), 'b2': jnp.zeros((DEPTH, DIM), jnp.float32)}
    _L0_ffn_in = _L0_ffn_setup()
    _d = {'L0_attn_x': _L0_attn_in['x'], 'L0_attn_W_down': _L0_attn_in['W_down'], 'L0_attn_tokeys': _L0_attn_in['tokeys'], 'L0_attn_toqueries': _L0_attn_in['toqueries'], 'L0_attn_tovalues': _L0_attn_in['tovalues'], 'L0_attn_W_unify': _L0_attn_in['W_unify'], 'L0_attn_b_unify': _L0_attn_in['b_unify'], 'L0_ffn_Wqkv': _L0_ffn_in['Wqkv'], 'L0_ffn_q_scale': _L0_ffn_in['q_scale'], 'L0_ffn_k_scale': _L0_ffn_in['k_scale'], 'L0_ffn_Wo': _L0_ffn_in['Wo'], 'L0_ffn_ln_g': _L0_ffn_in['ln_g'], 'L0_ffn_ln_b': _L0_ffn_in['ln_b'], 'L0_ffn_W1': _L0_ffn_in['W1'], 'L0_ffn_b1': _L0_ffn_in['b1'], 'L0_ffn_W2': _L0_ffn_in['W2'], 'L0_ffn_b2': _L0_ffn_in['b2']}
    _x0 = _d['L0_attn_x']
    _d['L0_attn_x'] = jax.random.normal(jax.random.fold_in(jax.random.key(seed), 1), (16, 256, 128), dtype=_x0.dtype)
    del _x0
    return _d

def reference(L0_attn_x, L0_attn_W_down, L0_attn_tokeys, L0_attn_toqueries, L0_attn_tovalues, L0_attn_W_unify, L0_attn_b_unify, L0_ffn_Wqkv, L0_ffn_q_scale, L0_ffn_k_scale, L0_ffn_Wo, L0_ffn_ln_g, L0_ffn_ln_b, L0_ffn_W1, L0_ffn_b1, L0_ffn_W2, L0_ffn_b2):

    def _L0_attn_ref(x, W_down, tokeys, toqueries, tovalues, W_unify, b_unify):
        import jax, jax.numpy as jnp
        import numpy as np
        EMB, HEADS = (128, 16)
        S = EMB // HEADS
        b, t, e = x.shape
        h, s = (HEADS, S)
        scale = s ** (-0.25)
        xd = (x @ W_down).reshape(b, t, h, s)
        keys = jnp.einsum('bthk,hik->bthi', xd, tokeys) * scale
        queries = jnp.einsum('bthk,hik->bthi', xd, toqueries) * scale
        values = jnp.einsum('bthk,hik->bthi', xd, tovalues)
        dot = jnp.einsum('bqhs,bkhs->bhqk', queries, keys)
        attn = jax.nn.softmax(dot, axis=-1)
        out = jnp.einsum('bhqk,bkhs->bqhs', attn, values).reshape(b, t, e)
        return out @ W_unify + b_unify

    def _L0_ffn_ref(x, Wqkv, q_scale, k_scale, Wo, ln_g, ln_b, W1, b1, W2, b2):
        import jax, jax.numpy as jnp
        import numpy as np
        DIM = 128
        DEPTH = 6
        HEADS = 16
        DIM_HEAD = 64
        WINDOW = 32
        INNER = HEADS * DIM_HEAD
        DIM_INNER = int(DIM * 4 * 2 / 3)
        QK_SCALE = 8.0

        def shift_tokens(t):
            a, s = jnp.split(t, 2, -1)
            s = jnp.pad(s, ((0, 0), (1, 0), (0, 0)))[:, :-1]
            return jnp.concatenate([a, s], -1)

        def l2norm(t):
            return t / jnp.maximum(jnp.linalg.norm(t, axis=-1, keepdims=True), 1e-12)

        def rotate_half(x):
            x1, x2 = jnp.split(x, 2, -1)
            return jnp.concatenate([-x2, x1], -1)

        def rotary_tables(n):
            half = jnp.arange(0, DIM_HEAD, 2, dtype=jnp.float32)
            inv_freq = 1.0 / 10000.0 ** (half / DIM_HEAD)
            t = jnp.arange(n, dtype=jnp.float32)
            freqs = t[:, None] * inv_freq[None, :]
            freqs = jnp.concatenate([freqs, freqs], -1)
            base_scale = (half + 0.4 * DIM_HEAD) / (1.4 * DIM_HEAD)
            power = (t - n // 2) / (WINDOW // 2)
            scale = base_scale[None, :] ** power[:, None]
            scale = jnp.concatenate([scale, scale], -1)
            return (freqs, scale)

        def local_attention(q, k, v):
            b, h, n, d = q.shape
            w = WINDOW
            nw = n // w
            bq = q.reshape(b, h, nw, w, d)
            bk = k.reshape(b, h, nw, w, d)
            bv = v.reshape(b, h, nw, w, d)

            def look(t):
                p = jnp.pad(t, ((0, 0), (0, 0), (1, 0), (0, 0), (0, 0)))
                return jnp.concatenate([p[:, :, :nw], p[:, :, 1:]], axis=3)
            bk2, bv2 = (look(bk), look(bv))
            seq = jnp.arange(n).reshape(nw, w)
            seq_p = jnp.pad(seq, ((1, 0), (0, 0)), constant_values=-1)
            jt = jnp.concatenate([seq_p[:nw], seq_p[1:]], axis=1)
            it = seq[:, :, None]
            jb = jt[:, None, :]
            mask = (it < jb) | (it > jb + w) | (jb == -1)
            sim = jnp.einsum('bhwie,bhwje->bhwij', bq, bk2) * QK_SCALE
            sim = jnp.where(mask, -jnp.finfo(sim.dtype).max, sim)
            attn = jax.nn.softmax(sim, -1)
            out = jnp.einsum('bhwij,bhwje->bhwie', attn, bv2)
            return out.reshape(b, h, n, d)

        def attn_layer(x, Wqkv, qs, ksc, Wo):
            b, n, _ = x.shape
            qkv = x @ Wqkv
            q, k, v = jnp.split(qkv, 3, -1)
            sh = lambda t: t.reshape(b, n, HEADS, DIM_HEAD).transpose(0, 2, 1, 3)
            q, k, v = (sh(q), sh(k), sh(v))
            q = l2norm(q) * qs
            k = l2norm(k) * ksc
            freqs, scale = rotary_tables(n)
            cos, sin = (jnp.cos(freqs), jnp.sin(freqs))
            q = q * cos * scale + rotate_half(q) * sin * scale
            inv = 1.0 / scale
            k = k * cos * inv + rotate_half(k) * sin * inv
            out = local_attention(q, k, v)
            out = out.transpose(0, 2, 1, 3).reshape(b, n, INNER)
            return out @ Wo

        def ffn_layer(x, g, bln, W1, b1, W2, b2):
            mu = x.mean(-1, keepdims=True)
            var = ((x - mu) ** 2).mean(-1, keepdims=True)
            xn = (x - mu) / jnp.sqrt(var + 1e-05) * g + bln
            hg = xn @ W1 + b1
            a, gate = jnp.split(hg, 2, -1)
            return a * jax.nn.gelu(gate, approximate=False) @ W2 + b2
        for i in range(DEPTH):
            x = attn_layer(shift_tokens(x), Wqkv[i], q_scale[i], k_scale[i], Wo[i]) + x
            x = ffn_layer(shift_tokens(x), ln_g[i], ln_b[i], W1[i], b1[i], W2[i], b2[i]) + x
        return x
    x = L0_attn_x
    x = x + _layernorm(_L0_attn_ref(_layernorm(x, axis=-1), L0_attn_W_down, L0_attn_tokeys, L0_attn_toqueries, L0_attn_tovalues, L0_attn_W_unify, L0_attn_b_unify), axis=-1)
    x = x + _layernorm(_L0_ffn_ref(_layernorm(x, axis=-1), L0_ffn_Wqkv, L0_ffn_q_scale, L0_ffn_k_scale, L0_ffn_Wo, L0_ffn_ln_g, L0_ffn_ln_b, L0_ffn_W1, L0_ffn_b1, L0_ffn_W2, L0_ffn_b2), axis=-1)
    return x

_drawn_inputs = setup_inputs


def setup_inputs(seed=0):
    import zlib

    import numpy as np

    out = dict(_drawn_inputs(seed))
    spreads = {'L0_ffn_q_scale': (1.0, 0.6),
     'L0_ffn_k_scale': (1.0, 0.6),
     'L0_ffn_ln_g': (1.0, 0.6),
     'L0_ffn_ln_b': (0.0, 0.8),
     'L0_ffn_b1': (0.0, 0.8),
     'L0_ffn_b2': (0.0, 0.385)}
    factors = {'L0_attn_W_down': 8.0,
     'L0_attn_tokeys': 8.0,
     'L0_attn_toqueries': 8.0,
     'L0_attn_tovalues': 8.0,
     'L0_attn_W_unify': 8.0,
     'L0_ffn_W1': 4.898,
     'L0_ffn_W2': 4.604}
    for name, (base, spread) in spreads.items():
        noise = np.random.default_rng([zlib.crc32(name.encode()), seed]).standard_normal(out[name].shape)
        drawn = base * np.exp(spread * noise) if base else spread * noise
        out[name] = jnp.asarray(drawn.astype(out[name].dtype))
    for name, factor in factors.items():
        out[name] = (out[name] * factor).astype(out[name].dtype)
    return out
```

```python
import concourse.bass as bass
from concourse import mybir
from contextlib import ExitStack

SEQS, TOKENS, DIM = 16, 256, 128
P = 128
TILES = TOKENS // P
A_HEADS, A_DIM = 16, 8
A_ROWS = 32
A_PER_GROUP = P // A_ROWS
A_GROUPS = A_HEADS // A_PER_GROUP
DEPTH, HEADS, HEAD_DIM, WINDOW = 6, 16, 64, 32
INNER = HEADS * HEAD_DIM
PAIRS = HEADS // 2
WINDOWS = TOKENS // WINDOW
TILE_WINDOWS = P // WINDOW
CHUNK = 512
CHUNK_HEADS = CHUNK // HEAD_DIM
UNITS = TILES * 2 * INNER // CHUNK
V_UNITS = TILES * INNER // CHUNK
FF = DIM * 4 * 2 // 3
FF_BLOCKS = -(-FF // P)
FF_LAST = FF - (FF_BLOCKS - 1) * P
FF_SEQS = 2
FF_COLS = FF_SEQS * TOKENS
FF_STEPS = SEQS // FF_SEQS
EPS = 1e-5
QK_SCALE = 8.0
LEAST_NORM = 1e-12
MASKED = -float(2 ** 100)


def nth(n, per_iteration, j):
    return n * per_iteration + (j + 1)


def nth_of_used(n, per_iteration, j):
    return nth(n, per_iteration, j) + 1


def build(nc, x, w_down, qk_pad, v_block, w_unify, b_unify, w_qkv, w_o, scales, w1, w2, columns,
          rope, ident, mask, spread, out):
    f32, bf16 = mybir.dt.float32, mybir.dt.bfloat16
    ALU = mybir.AluOpType
    ACT = mybir.ActivationFunctionType
    X = mybir.AxisListType.X

    ctx = ExitStack()
    with ctx:
        def sb(name, shape, dt=f32):
            return ctx.enter_context(nc.sbuf_tensor(name, shape, dt))

        def sem(name):
            return ctx.enter_context(nc.semaphore(name))

        resid = sb("resid", [P, SEQS * TILES, DIM])
        stream = sb("stream", [P, SEQS + FF_SEQS, TOKENS + 1])
        ident_f = sb("ident_f", [P, P])
        ident_b = sb("ident_b", [P, P], bf16)
        mask_f = sb("mask_f", [P, 2, HEAD_DIM])
        mask_b = sb("mask_b", [P, 2, CHUNK_HEADS, HEAD_DIM], bf16)
        mean_w = sb("mean_w", [P, P])
        ones_w = sb("ones_w", [P, P])
        neg_half = sb("neg_half", [P, 1])
        spread_sb = sb("spread_sb", [P, P])
        stat_sum = sb("stat_sum", [P, SEQS * TILES])
        stat_mean = sb("stat_mean", [P, SEQS * TILES])
        stat_ss = sb("stat_ss", [P, SEQS * TILES])
        stat_var = sb("stat_var", [P, SEQS * TILES])
        stat_rstd = sb("stat_rstd", [P, SEQS * TILES])
        w_down_sb = sb("w_down_sb", [P, P])
        qk_pad_sb = sb("qk_pad_sb", [P, 2, A_GROUPS, P])
        v_block_sb = sb("v_block_sb", [P, P])
        w_unify_sb = sb("w_unify_sb", [P, A_GROUPS, P])
        b_unify_sb = sb("b_unify_sb", [P, DIM])
        w_qkv_sb = sb("w_qkv_sb", [P, 3 * INNER])
        w_o_sb = sb("w_o_sb", [P, PAIRS, DIM])
        w1_sb = sb("w1_sb", [P, 2 * FF])
        w2_sb = sb("w2_sb", [P, FF_BLOCKS, DIM])
        cols_sb = sb("cols_sb", [P, 2 * FF_BLOCKS + 3])
        rope_sb = sb("rope_sb", [P, TILES, 4, HEAD_DIM])
        scales_sb = sb("scales_sb", [P, 4, HEAD_DIM])
        table = sb("table", [P, TILES, 4, HEAD_DIM])
        shifted = sb("shifted", [P, TOKENS])
        squares = sb("squares", [P, 2, CHUNK])
        sumsq = sb("sumsq", [P, UNITS, CHUNK_HEADS])
        clamped = sb("clamped", [P, UNITS, CHUNK_HEADS])
        rnorm = sb("rnorm", [P, UNITS, CHUNK_HEADS])
        normed = sb("normed", [P, 2, CHUNK])
        by_cos = sb("by_cos", [P, 2, CHUNK])
        by_sin = sb("by_sin", [P, 2, CHUNK])
        k_t = sb("k_t", [P, PAIRS, WINDOW + TOKENS])
        row_max = sb("row_max", [P, TILES, HEADS])
        row_sum = sb("row_sum", [P, TILES, HEADS])
        row_inv = sb("row_inv", [P, TILES, HEADS])
        area_a = sb("area_a", [P, 2 * TILES * INNER])
        area_b = sb("area_b", [P, 2 * TILES * INNER])
        area_c = sb("area_c", [P, 2 * TILES * INNER])
        half = TILES * INNER
        probs = area_a[:, 0:half].rearrange("p (t n) -> p t n", t=TILES)
        exps = area_a[:, half:].rearrange("p (t n) -> p t n", t=TILES)
        v_sb = area_b[:, 0:half].rearrange("p (t n) -> p t n", t=TILES)
        att_t = area_b[:, half:].rearrange("p (c n) -> p c n", c=PAIRS)
        q_t = area_c[:, 0:half].rearrange("p (c n) -> p c n", c=PAIRS)
        probs_t = area_c[:, half:].rearrange("p (t b n) -> p t b n", t=TILES, b=2)
        band = sb("band", [P, 2 * TILE_WINDOWS + 1, HEADS * WINDOW])
        ff_x = sb("ff_x", [P, FF_COLS])
        ff_xc = sb("ff_xc", [P, FF_COLS])
        ff_sq = sb("ff_sq", [P, FF_COLS])
        ff_var = sb("ff_var", [P, FF_COLS // P])
        ff_rstd = sb("ff_rstd", [P, FF_COLS // P])
        ff_diag = sb("ff_diag", [P, FF_COLS // P, P])
        ff_x0 = sb("ff_x0", [P, FF_COLS])
        ff_xn = sb("ff_xn", [P, FF_COLS])
        ff_gate = sb("ff_gate", [P, FF_BLOCKS, FF_COLS])
        ff_h = sb("ff_h", [P, FF_BLOCKS, FF_COLS])
        ln_sq = area_a[:, :].rearrange("p (n d) -> p n d", d=DIM)
        ln_xc = area_b[:, :].rearrange("p (n d) -> p n d", d=DIM)
        y_all = area_c[:, :].rearrange("p (n d) -> p n d", d=DIM)
        flat = band[:, :, :].rearrange("p a b -> p (a b)")
        side = A_GROUPS * TOKENS
        a_q = flat[:, 0:side].rearrange("p (g n) -> p g n", g=A_GROUPS)
        a_k = flat[:, side:2 * side].rearrange("p (g n) -> p g n", g=A_GROUPS)
        a_v = flat[:, 2 * side:3 * side].rearrange("p (t h r) -> p t h r", t=TILES, h=A_HEADS)
        a_on = flat[:, 3 * side:4 * side].rearrange("p (g n) -> p g n", g=A_GROUPS)
        a_x = sb("a_x", [P, TILES, DIM])
        a_xt = sb("a_xt", [P, TOKENS])
        a_xd = sb("a_xd", [P, TOKENS])
        a_nmax = sb("a_nmax", [P, A_HEADS, TILES])
        a_p = sb("a_p", [P, 2, TILES, TOKENS])
        a_pt = sb("a_pt", [P, 2, TILES, TOKENS])
        a_os = sb("a_os", [P, 2, TOKENS])
        a_inv = sb("a_inv", [P, 2, TOKENS])

        bank = [ctx.enter_context(nc.psum_tensor(f"bank{i}", [P, CHUNK], f32)) for i in range(6)]
        wide = ctx.enter_context(nc.psum_tensor("wide", [P, 2 * CHUNK], f32))
        proj = bank[0:2]
        turn = bank[2]
        att_o = bank[3:5]
        wo_ps = bank[5]
        score = wide[:, :].rearrange("p (h j) -> p h j", j=2 * WINDOW)
        wide_half = [wide[:, 0:CHUNK], wide[:, CHUNK:2 * CHUNK]]
        ff_mean_ps, ff_var_ps = bank[0], bank[1]
        ff_ps = [bank[2][:, :], bank[3][:, :], wide_half[0], wide_half[1]]
        ff_rstd_ps = bank[4]
        ff_y_ps = bank[5]
        a_s_ps = bank[0:3]
        a_pt_ps = bank[3:5]
        a_o_ps = [wide_half[0], wide_half[1]]
        a_m_ps = bank[5]

        in_x, in_const, in_first = sem("in_x"), sem("in_const"), sem("in_first")
        in_attn, in_ff = sem("in_attn"), sem("in_ff")
        const_ready, zero_ready, dve_step = sem("const_ready"), sem("zero_ready"), sem("dve_step")
        ln_centred, ln_squared, ln_var = sem("ln_centred"), sem("ln_squared"), sem("ln_var")
        ln_rstd, ln_scaled, ln_eps = sem("ln_rstd"), sem("ln_scaled"), sem("ln_eps")
        x_turned, stream_ready = sem("x_turned"), sem("stream_ready")
        out_turned, out_copied, out_stored = sem("out_turned"), sem("out_copied"), sem("out_stored")
        a_x_ready, a_xt_ps, a_xt_sb = sem("a_x_ready"), sem("a_xt_ps"), sem("a_xt_sb")
        a_xd_ps, a_xd_sb, a_qk_ps = sem("a_xd_ps"), sem("a_xd_sb"), sem("a_qk_ps")
        a_qk_sb, a_v_ps, a_v_sb = sem("a_qk_sb"), sem("a_v_ps"), sem("a_v_sb")
        a_scored, a_maxed, a_exped = sem("a_scored"), sem("a_maxed"), sem("a_exped")
        a_turned, a_pt_act, a_pt_dve = sem("a_turned"), sem("a_pt_act"), sem("a_pt_dve")
        a_mixed, a_o_sb, a_spread = sem("a_mixed"), sem("a_o_sb"), sem("a_spread")
        a_inv_ready, a_on_ready = sem("a_inv_ready"), sem("a_on_ready")
        a_y_ps, a_y_sb = sem("a_y_ps"), sem("a_y_sb")
        table_ready, shift_ready = sem("table_ready"), sem("shift_ready")
        projected, squared, summed = sem("projected"), sem("squared"), sem("summed")
        clamp_done, rnorm_ready, normed_ready = sem("clamp_done"), sem("rnorm_ready"), sem("normed_ready")
        cos_done, sin_done, turned = sem("cos_done"), sem("sin_done"), sem("turned")
        qk_ready, v_projected, v_ready = sem("qk_ready"), sem("v_projected"), sem("v_ready")
        scored, maxed, lowered = sem("scored"), sem("maxed"), sem("lowered")
        exped, row_summed, inv_ready = sem("exped"), sem("row_summed"), sem("inv_ready")
        probs_ready, probs_turned, band_ready = sem("probs_ready"), sem("probs_turned"), sem("band_ready")
        mixed, att_ready, unified = sem("mixed"), sem("att_ready"), sem("unified")
        attn_added = sem("attn_added")
        ff_shifted, ff_mean, ff_centred = sem("ff_shifted"), sem("ff_mean"), sem("ff_centred")
        ff_squared, ff_var_done, ff_eps = sem("ff_squared"), sem("ff_var_done"), sem("ff_eps")
        ff_rstd_done, ff_diag_ready, ff_rstd_wide = sem("ff_rstd_done"), sem("ff_diag_ready"), sem("ff_rstd_wide")
        ff_scaled, ff_xn_ready = sem("ff_scaled"), sem("ff_xn_ready")
        ff_up, ff_gelu, ff_gated = sem("ff_up"), sem("ff_gelu"), sem("ff_gated")
        ff_down, ff_added = sem("ff_down"), sem("ff_added")

        ATTN_LOADS, FF_LOADS, CONST_LOADS, FIRST_LOADS = 3, 3, 4, 5
        BAND_COPIES = WINDOWS + WINDOWS - 1
        DONE_ATTN = SEQS
        HALF_ROWS = P // 2

        block = ctx.enter_context(nc.Block())

        @block.sync
        def _(sp):
            sp.dma_start(resid[:, :, :], x.rearrange("(n p) d -> p n d", p=P)).then_inc(in_x, 16)
            sp.dma_start(ident_f[:, :], ident).then_inc(in_const, 16)
            sp.dma_start(mask_f[:, :, :], mask).then_inc(in_const, 16)
            sp.dma_start(rope_sb[:, :, :, :], rope).then_inc(in_const, 16)
            sp.dma_start(spread_sb[:, :], spread).then_inc(in_const, 16)
            sp.dma_start(w_down_sb[:, :], w_down).then_inc(in_first, 16)
            sp.dma_start(qk_pad_sb[:, :, :, :], qk_pad).then_inc(in_first, 16)
            sp.dma_start(v_block_sb[:, :], v_block).then_inc(in_first, 16)
            sp.dma_start(w_unify_sb[:, :, :], w_unify).then_inc(in_first, 16)
            sp.dma_start(b_unify_sb[:, :], b_unify.partition_broadcast(P)).then_inc(in_first, 16)

            def spread_band(tile):
                for w in range(TILE_WINDOWS):
                    wq = tile * TILE_WINDOWS + w
                    src = slice(w * WINDOW, (w + 1) * WINDOW)
                    sp.dma_start(band[src, wq + tile, :], probs_t[src, tile, 1, :]).then_inc(band_ready, 16)
                    if wq > 0:
                        key_tile, key_w = divmod(wq - 1, TILE_WINDOWS)
                        dst = slice(key_w * WINDOW, (key_w + 1) * WINDOW)
                        sp.dma_start(band[dst, wq + key_tile, :], probs_t[src, tile, 0, :])\
                          .then_inc(band_ready, 16)

            with sp.Fori(0, DEPTH) as layer:
                sp.wait_ge(attn_added, layer * DONE_ATTN + 1)
                sp.dma_start(w_qkv_sb[:, :], w_qkv[bass.ds(layer, 1), :, :].rearrange("a p n -> (a p) n"))\
                  .then_inc(in_attn, 16)
                sp.dma_start(w_o_sb[:, :, :], w_o[bass.ds(layer, 1), :, :].rearrange("a (c p) n -> p (a c) n", p=P))\
                  .then_inc(in_attn, 16)
                sp.wait_ge(table_ready, layer * TILES + 1)
                sp.dma_start(scales_sb[:, :, :], scales[bass.ds(layer, 1), :, :].rearrange("a c d -> a (c d)")
                             .broadcast_to([P, 4 * HEAD_DIM]).rearrange("p (c d) -> p c d", c=4)).then_inc(in_attn, 16)
                sp.wait_ge(ff_added, layer * FF_STEPS + 1)
                sp.dma_start(w1_sb[:, :], w1[bass.ds(layer, 1), :, :].rearrange("a p n -> (a p) n")).then_inc(in_ff, 16)
                sp.dma_start(w2_sb[:, :, :], w2[bass.ds(layer, 1), :, :].rearrange("a (c p) n -> p (a c) n", p=P))\
                  .then_inc(in_ff, 16)
                sp.wait_ge(ff_xn_ready, layer * (FF_STEPS + 1) + 1)
                sp.dma_start(cols_sb[:, :], columns[bass.ds(layer, 1), :, :].rearrange("a p n -> (a p) n"))\
                  .then_inc(in_ff, 16)
                with sp.Fori(0, SEQS) as seq:
                    n = layer * SEQS + seq
                    for tile in range(TILES):
                        sp.wait_ge(probs_turned, nth(n, TILES, tile))
                        spread_band(tile)

            for c in range(4):
                sp.wait_ge(out_copied, c + 1)
                rows = slice(c * 8, (c + 1) * 8)
                sp.dma_start(out.rearrange("(n p) d -> p n d", p=P)[:, rows, :], resid[:, rows, :])\
                  .then_inc(out_stored, 16)
            sp.wait_ge(out_stored, 4 * 16)

        @block.tensor
        def _(pe):
            mm = nc.tensor.matmul

            pe.wait_ge(in_first, 16 * FIRST_LOADS)
            pe.wait_ge(in_const, 16 * CONST_LOADS)

            def a_scores(n, h):
                g, j = divmod(h, A_PER_GROUP)
                rows = slice(j * A_ROWS, (j + 1) * A_ROWS)
                if h >= 3:
                    pe.wait_ge(a_exped, nth(n, A_HEADS, h - 3))
                for t in range(TILES):
                    last = mm(a_s_ps[h % 3][:, t * TOKENS:(t + 1) * TOKENS], a_q[rows, g, t * P:(t + 1) * P],
                              a_k[rows, g, :], start=True, stop=True)
                last.then_inc(a_scored, 1)

            def a_spread_sums(n, g):
                pe.wait_ge(a_o_sb, nth(n, A_GROUPS, g))
                if g > 0:
                    pe.wait_ge(a_inv_ready, nth(n, A_GROUPS, g - 1))
                mm(a_m_ps[:, 0:TOKENS], spread_sb[:, :], a_os[:, g % 2, :], start=True, stop=True)\
                    .then_inc(a_spread, 1)

            with pe.Fori(0, SEQS) as n:
                pe.wait_ge(a_x_ready, nth(n, 1, 0))
                pe.wait_ge(a_y_sb, nth_of_used(n, 1, -1))
                for t in range(TILES):
                    last = mm(a_m_ps[:, t * P:(t + 1) * P], a_x[:, t, :], ident_f[:, :], start=True, stop=True,
                              is_transpose=True)
                last.then_inc(a_xt_ps, 1)
                pe.wait_ge(a_xt_sb, nth(n, 1, 0))
                mm(a_m_ps[:, 0:TOKENS], w_down_sb[:, :], a_xt[:, :], start=True, stop=True).then_inc(a_xd_ps, 1)
                pe.wait_ge(a_xd_sb, nth(n, 1, 0))
                qk_banks = [a_s_ps[0], a_s_ps[1], a_s_ps[2], a_m_ps]
                for r in range(4):
                    side_no, g0 = divmod(2 * r, A_GROUPS)
                    for i in range(2):
                        last = mm(qk_banks[r][:, i * TOKENS:(i + 1) * TOKENS], qk_pad_sb[:, side_no, g0 + i, :],
                                  a_xd[:, :], start=True, stop=True)
                    last.then_inc(a_qk_ps, 1)
                for t in range(TILES):
                    last = mm(a_pt_ps[0][:, t * P:(t + 1) * P], a_xd[:, t * P:(t + 1) * P], v_block_sb[:, :],
                              start=True, stop=True)
                last.then_inc(a_v_ps, 1)
                pe.wait_ge(a_qk_sb, nth(n, 4, 3))
                a_scores(n, 0)
                a_scores(n, 1)
                pe.wait_ge(a_v_sb, nth(n, 1, 0))
                for h in range(A_HEADS):
                    g, j = divmod(h, A_PER_GROUP)
                    if h + 2 < A_HEADS:
                        a_scores(n, h + 2)
                    pe.wait_ge(a_exped, nth(n, A_HEADS, h))
                    if h >= 2:
                        pe.wait_ge(a_pt_dve if h % 2 == 0 else a_pt_act, nth(n, A_HEADS // 2, h // 2 - 1))
                    for kb in range(TILES):
                        for t in range(TILES):
                            at = kb * TOKENS + t * P
                            last = mm(a_pt_ps[h % 2][:, at:at + P], a_p[:, h % 2, t, kb * P:(kb + 1) * P],
                                      ident_f[:, :], start=True, stop=True, is_transpose=True)
                    last.then_inc(a_turned, 1)
                    if h % A_PER_GROUP == 0 and g > 0:
                        a_spread_sums(n, g - 1)
                    pe.wait_ge(a_pt_dve if h % 2 == 0 else a_pt_act, nth(n, A_HEADS // 2, h // 2))
                    if g >= 2 and j == 0:
                        pe.wait_ge(a_on_ready, nth(n, A_GROUPS, g - 2))
                    rows = slice(j * A_ROWS, (j + 1) * A_ROWS)
                    for kb in range(TILES):
                        last = mm(a_o_ps[g % 2][rows, 0:TOKENS], a_v[:, kb, h, :], a_pt[:, h % 2, kb, :],
                                  start=kb == 0, stop=kb == TILES - 1)
                    last.then_inc(a_mixed, 1)
                a_spread_sums(n, A_GROUPS - 1)
                pe.wait_ge(a_on_ready, nth(n, A_GROUPS, A_GROUPS - 1))
                for t in range(TILES):
                    for g in range(A_GROUPS):
                        last = mm(a_m_ps[:, t * P:(t + 1) * P], a_on[:, g, t * P:(t + 1) * P], w_unify_sb[:, g, :],
                                  start=g == 0, stop=g == A_GROUPS - 1)
                last.then_inc(a_y_ps, 1)

            pe.wait_ge(ln_scaled, 3)
            for c in range(SEQS * TILES // 4):
                if c >= 2:
                    pe.wait_ge(stream_ready, c - 1)
                for i in range(4):
                    last = mm(proj[c % 2][:, i * P:(i + 1) * P], ln_xc[:, 4 * c + i, :], ident_f[:, :],
                              start=True, stop=True, is_transpose=True)
                last.then_inc(x_turned, 1)

            def project(n, u, first, shifts):
                tile, c = divmod(u, UNITS // TILES)
                if u == 0:
                    pe.wait_ge(shift_ready, nth_of_used(shifts, 1, 0))
                if u >= 2:
                    pe.wait_ge(normed_ready, nth(n, UNITS, u - 2))
                elif not first:
                    pe.wait_ge(v_ready, nth(n, V_UNITS, u + 2 - V_UNITS))
                mm(proj[u % 2][:, :], shifted[:, tile * P:(tile + 1) * P], w_qkv_sb[:, c * CHUNK:(c + 1) * CHUNK],
                   start=True, stop=True).then_inc(projected, 1)

            def project_v(n, j):
                tile, c = divmod(j, V_UNITS // TILES)
                if j < 2:
                    pe.wait_ge(normed_ready, nth(n, UNITS, UNITS - 2 + j))
                else:
                    pe.wait_ge(v_ready, nth(n, V_UNITS, j - 2))
                at = 2 * INNER + c * CHUNK
                mm(proj[j % 2][:, :], shifted[:, tile * P:(tile + 1) * P], w_qkv_sb[:, at:at + CHUNK],
                   start=True, stop=True).then_inc(v_projected, 1)

            def scores(n, tile):
                if tile == 0:
                    pe.wait_ge(qk_ready, nth(n, UNITS, UNITS - 1))
                else:
                    pe.wait_ge(lowered, nth(n, TILES, tile - 1))
                for odd in range(2):
                    mm(wide_half[odd], ident_b[:, :], mask_b[:, 0 if tile == 0 else 1, :, :]
                       .rearrange("p h j -> p (h j)"), start=True, stop=False, skip_group_check=True)
                for pair in range(PAIRS):
                    for w in range(TILE_WINDOWS):
                        for odd in range(2):
                            rows = slice(odd * HEAD_DIM, (odd + 1) * HEAD_DIM)
                            at = tile * P + w * WINDOW
                            last = mm(score[w * WINDOW:(w + 1) * WINDOW, odd * PAIRS + pair, :],
                                      q_t[rows, pair, at:at + WINDOW], k_t[rows, pair, at:at + 2 * WINDOW],
                                      start=False, stop=True, skip_group_check=True)
                last.then_inc(scored, 1)

            def turn_unit(n, u, first):
                pe.wait_ge(cos_done, nth(n, UNITS, u))
                pe.wait_ge(sin_done, nth(n, UNITS, u))
                if u > 0:
                    pe.wait_ge(qk_ready, nth(n, UNITS, u - 1))
                for i in range(CHUNK // P):
                    at = slice(i * P, (i + 1) * P)
                    mm(turn[:, at], by_cos[:, u % 2, at], ident_f[:, :], start=True, stop=False, is_transpose=True)
                    last = mm(turn[:, at], by_sin[:, u % 2, at], ident_f[:, :], start=False, stop=True,
                              is_transpose=True)
                last.then_inc(turned, 1)

            def mix(n, j):
                if j == 0:
                    pe.wait_ge(band_ready, n * (16 * BAND_COPIES) + 16 * BAND_COPIES)
                    pe.wait_ge(v_ready, nth(n, V_UNITS, V_UNITS - 1))
                if j >= 2:
                    pe.wait_ge(att_ready, nth(n, PAIRS // 2, j - 2))
                cut = (TILE_WINDOWS + 1) * WINDOW
                for i in range(2):
                    pair = 2 * j + i
                    for odd in range(2):
                        rows = slice(odd * HEAD_DIM, (odd + 1) * HEAD_DIM)
                        at = (odd * PAIRS + pair) * WINDOW
                        feats = slice((2 * pair + odd) * HEAD_DIM, (2 * pair + odd + 1) * HEAD_DIM)
                        mm(att_o[j % 2][rows, i * TOKENS:i * TOKENS + cut], v_sb[:, 0, feats],
                           band[:, 0:TILE_WINDOWS + 1, at:at + WINDOW], start=True, stop=False, skip_group_check=True)
                        last = mm(att_o[j % 2][rows, i * TOKENS + P:(i + 1) * TOKENS], v_sb[:, 1, feats],
                                  band[:, TILE_WINDOWS + 1:, at:at + WINDOW], start=False, stop=True,
                                  skip_group_check=True)
                last.then_inc(mixed, 1)

            def unify(n):
                pe.wait_ge(att_ready, nth(n, PAIRS // 2, PAIRS // 2 - 1))
                pe.wait_ge(attn_added, nth_of_used(n, 1, -1))
                for pair in range(PAIRS):
                    last = mm(wo_ps[:, 0:TOKENS], w_o_sb[:, pair, :], att_t[:, pair, :], start=pair == 0,
                              stop=pair == PAIRS - 1)
                last.then_inc(unified, 1)

            def attention_step(n, shifts, first=False, last=False):
                old = n - 1
                if not last:
                    project(n, 0, first, shifts)
                    project(n, 1, first, shifts)
                if not first:
                    scores(old, 0)
                if not last:
                    project(n, 2, first, shifts)
                    turn_unit(n, 0, first)
                if not first:
                    scores(old, 1)
                if not last:
                    for u in range(3, UNITS):
                        project(n, u, first, shifts)
                        turn_unit(n, u - 2, first)
                    turn_unit(n, UNITS - 2, first)
                if not first:
                    mix(old, 0)
                if not last:
                    turn_unit(n, UNITS - 1, first)
                if not first:
                    for j in range(1, PAIRS // 2):
                        mix(old, j)
                if not last:
                    for j in range(V_UNITS):
                        project_v(n, j)
                if not first:
                    unify(old)

            def ff_mean_of(e):
                pe.wait_ge(ff_shifted, nth(e, 1, 0))
                mm(ff_mean_ps[:, :], mean_w[:, :], ff_x[:, :], start=True, stop=True).then_inc(ff_mean, 1)

            def ff_var_of(e):
                pe.wait_ge(ff_squared, nth(e, 1, 0))
                for i in range(FF_COLS // P):
                    last = mm(ff_var_ps[:, i:i + 1], ff_sq[:, i * P:(i + 1) * P], mean_w[:, 0:1], start=True, stop=True)
                last.then_inc(ff_var_done, 1)

            def ff_rstd_of(e):
                pe.wait_ge(ff_diag_ready, nth(e, 1, 0))
                mm(ff_rstd_ps[:, :], ones_w[:, :], ff_diag[:, :, :].rearrange("p c n -> p (c n)"), start=True,
                   stop=True).then_inc(ff_rstd_wide, 1)

            def ff_up_of(f, k, wait=None):
                rows = P if k < FF_BLOCKS - 1 else FF_LAST
                for i, at in enumerate((FF + k * P, k * P)):
                    b = (2 * k + i) % 4
                    if k == 2:
                        if i == 0:
                            pe.wait_ge(ff_gelu, nth(f, FF_BLOCKS, 0))
                        else:
                            pe.wait_ge(ff_gated, nth_of_used(f, FF_BLOCKS, 0))
                    mm(ff_ps[b][0:rows, :], w1_sb[:, at:at + rows], ff_xn[:, :], start=True, stop=True)\
                        .then_inc(ff_up, 1)

            with pe.Fori(0, DEPTH) as layer:
                pe.wait_ge(in_attn, (layer + 1) * (16 * ATTN_LOADS))
                shifts = layer * (SEQS + 1)
                attention_step(layer * SEQS, shifts, first=True)
                with pe.Fori(1, SEQS) as seq:
                    attention_step(layer * SEQS + seq, shifts + seq)
                attention_step(layer * SEQS + SEQS, None, last=True)

                pe.wait_ge(in_ff, (layer + 1) * (16 * FF_LOADS))
                ff_mean_of(layer * (FF_STEPS + 1))
                ff_var_of(layer * (FF_STEPS + 1))
                ff_rstd_of(layer * (FF_STEPS + 1))
                with pe.Fori(0, FF_STEPS) as step:
                    f = layer * FF_STEPS + step
                    e = layer * (FF_STEPS + 1) + step
                    pe.wait_ge(ff_xn_ready, nth_of_used(e, 1, 0))
                    pe.wait_ge(ff_gated, nth_of_used(f, FF_BLOCKS, -1))
                    ff_up_of(f, 0)
                    ff_mean_of(e + 1)
                    ff_up_of(f, 1)
                    ff_var_of(e + 1)
                    ff_up_of(f, 2)
                    ff_rstd_of(e + 1)
                    pe.wait_ge(ff_added, nth_of_used(f, 1, -1))
                    for k in range(FF_BLOCKS):
                        rows = P if k < FF_BLOCKS - 1 else FF_LAST
                        pe.wait_ge(ff_gated, nth_of_used(f, FF_BLOCKS, k))
                        last = mm(ff_y_ps[:, :], w2_sb[0:rows, k, :], ff_h[0:rows, k, :], start=k == 0,
                                  stop=k == FF_BLOCKS - 1)
                    last.then_inc(ff_down, 1)

            pe.wait_ge(ff_added, DEPTH * FF_STEPS + 1)
            for c in range(SEQS * TILES // 4):
                if c >= 2:
                    pe.wait_ge(out_turned, c - 1)
                for i in range(4):
                    seq, tile = divmod(4 * c + i, TILES)
                    last = mm(proj[c % 2][:, i * P:(i + 1) * P], stream[:, seq, 1 + tile * P:1 + (tile + 1) * P],
                              ident_f[:, :], start=True, stop=True, is_transpose=True)
                last.then_inc(x_turned, 1)

        @block.scalar
        def _(act):
            av = nc.scalar.activation

            def ln_square(i):
                act.wait_ge(ln_centred, i)
                av(ln_sq, ln_xc, ACT.Square).then_inc(ln_squared, 1)

            for used in (ff_xn_ready, shift_ready):
                act.sem_inc(used, 1)
            ln_square(1)
            with act.Fori(0, SEQS) as n:
                act.wait_ge(a_xt_ps, nth(n, 1, 0))
                av(a_xt[:, :], a_m_ps[:, 0:TOKENS], ACT.Copy).then_inc(a_xt_sb, 1)
                act.wait_ge(a_xd_ps, nth(n, 1, 0))
                av(a_xd[:, :], a_m_ps[:, 0:TOKENS], ACT.Copy).then_inc(a_xd_sb, 1)
                qk_banks = [a_s_ps[0], a_s_ps[1], a_s_ps[2], a_m_ps]
                for r in range(4):
                    act.wait_ge(a_qk_ps, nth(n, 4, r))
                    side_no, g0 = divmod(2 * r, A_GROUPS)
                    av((a_q, a_k)[side_no][:, g0:g0 + 2, :], qk_banks[r][:, :].rearrange("p (g n) -> p g n", g=2),
                       ACT.Copy, scale=float(A_DIM) ** -0.25).then_inc(a_qk_sb, 1)
                for h in range(A_HEADS + 1):
                    if h < A_HEADS:
                        act.wait_ge(a_maxed, nth(n, A_HEADS, h))
                        if h >= 2:
                            act.wait_ge(a_turned, nth(n, A_HEADS, h - 2))
                        for t in range(TILES):
                            last = av(a_p[:, h % 2, t, :], a_s_ps[h % 3][:, t * TOKENS:(t + 1) * TOKENS], ACT.Exp,
                                      bias=a_nmax[:, h, t:t + 1])
                        last.then_inc(a_exped, 1)
                    if h >= 1:
                        g, j = divmod(h - 1, A_PER_GROUP)
                        if (h - 1) % 2 == 1:
                            act.wait_ge(a_turned, nth(n, A_HEADS, h - 1))
                            if h - 1 >= 2:
                                act.wait_ge(a_mixed, nth(n, A_HEADS, h - 3))
                            av(a_pt[:, 1, :, :], a_pt_ps[1][:, :].rearrange("p (t n) -> p t n", t=TILES), ACT.Copy)\
                                .then_inc(a_pt_act, 1)
                        if j == A_PER_GROUP - 1:
                            act.wait_ge(a_mixed, nth(n, A_HEADS, h - 1))
                            if g >= 2:
                                act.wait_ge(a_on_ready, nth(n, A_GROUPS, g - 2))
                            av(a_os[:, g % 2, :], a_o_ps[g % 2][:, 0:TOKENS], ACT.Copy).then_inc(a_o_sb, 1)

            ln_square(2)
            ln_square(3)
            for c in range(SEQS * TILES // 4):
                act.wait_ge(x_turned, c + 1)
                if c == 0:
                    act.wait_ge(zero_ready, 3)
                av(stream[:, 2 * c:2 * c + 2, 1:TOKENS + 1], proj[c % 2][:, :].rearrange("p (s n) -> p s n", s=2),
                   ACT.Copy).then_inc(stream_ready, 1)

            def shift(seq):
                av(shifted[0:HALF_ROWS, :], stream[0:HALF_ROWS, bass.ds(seq, 1), 1:TOKENS + 1]
                   .rearrange("p a n -> p (a n)"), ACT.Copy)
                av(shifted[HALF_ROWS:P, :], stream[HALF_ROWS:P, bass.ds(seq, 1), 0:TOKENS]
                   .rearrange("p a n -> p (a n)"), ACT.Copy).then_inc(shift_ready, 1)

            def square(n, u, first):
                act.wait_ge(projected, nth(n, UNITS, u))
                if u >= 2:
                    act.wait_ge(summed, nth(n, UNITS, u - 2))
                elif not first:
                    act.wait_ge(summed, nth(n, UNITS, u - 2))
                av(squares[:, u % 2, :], proj[u % 2][:, :], ACT.Square).then_inc(squared, 1)

            def take_unit(n, u):
                tile, c = divmod(u, UNITS // TILES)
                pairs = slice((c % 2) * (PAIRS // 2), (c % 2 + 1) * (PAIRS // 2))
                act.wait_ge(turned, nth(n, UNITS, u))
                dst = q_t[:, pairs, tile * P:(tile + 1) * P] if c < 2 else \
                    k_t[:, pairs, WINDOW + tile * P:WINDOW + (tile + 1) * P]
                av(dst, turn[:, :].rearrange("p (c n) -> p c n", c=PAIRS // 2), ACT.Copy).then_inc(qk_ready, 1)

            def take_v(n, j):
                tile, c = divmod(j, V_UNITS // TILES)
                act.wait_ge(v_projected, nth(n, V_UNITS, j))
                av(v_sb[:, tile, c * CHUNK:(c + 1) * CHUNK], proj[j % 2][:, :], ACT.Copy).then_inc(v_ready, 1)

            def exponentials(n, tile):
                act.wait_ge(lowered, nth(n, TILES, tile))
                av(exps[:, tile, :], probs[:, tile, :], ACT.Exp, scale=QK_SCALE).then_inc(exped, 1)

            def take_out(n, j):
                act.wait_ge(mixed, nth(n, PAIRS // 2, j))
                av(att_t[:, 2 * j:2 * j + 2, :], att_o[j % 2][:, :].rearrange("p (c n) -> p c n", c=2), ACT.Copy)\
                    .then_inc(att_ready, 1)

            def attention_step(n, seq, first=False, last=False):
                old = n - 1
                if not last:
                    square(n, 0, first)
                    square(n, 1, first)
                if not first:
                    exponentials(old, 0)
                if not last:
                    square(n, 2, first)
                    take_unit(n, 0)
                if not last:
                    square(n, 3, first)
                if not first:
                    exponentials(old, 1)
                if not last:
                    take_unit(n, 1)
                    for u in range(4, UNITS):
                        square(n, u, first)
                        take_unit(n, u - 2)
                    take_unit(n, UNITS - 2)
                if not first:
                    take_out(old, 0)
                if not last:
                    take_unit(n, UNITS - 1)
                if not first:
                    for j in range(1, PAIRS // 2):
                        take_out(old, j)
                if not last:
                    for j in range(V_UNITS):
                        take_v(n, j)
                    shift(seq + 1)

            def ff_shift(step):
                seqs = bass.ds(step * FF_SEQS, FF_SEQS)
                for rows, start in ((slice(0, HALF_ROWS), 1), (slice(HALF_ROWS, P), 0)):
                    last = av(ff_x[rows, :].rearrange("p (s n) -> p s n", s=FF_SEQS),
                              stream[rows, seqs, start:start + TOKENS], ACT.Copy)
                last.then_inc(ff_shifted, 1)

            def ff_square(e):
                act.wait_ge(ff_centred, nth(e, 1, 0))
                av(ff_sq[:, :], ff_xc[:, :], ACT.Square).then_inc(ff_squared, 1)

            def ff_affine(e):
                act.wait_ge(ff_scaled, nth(e, 1, 0))
                av(ff_xn[:, :], ff_x0[:, :], ACT.Identity, bias=cols_sb[:, 2 * FF_BLOCKS + 2:],
                   scale=cols_sb[:, 2 * FF_BLOCKS + 1:2 * FF_BLOCKS + 2]).then_inc(ff_xn_ready, 1)

            def ff_gelu_of(f, k):
                rows = P if k < FF_BLOCKS - 1 else FF_LAST
                act.wait_ge(ff_up, nth(f, 2 * FF_BLOCKS, 2 * k))
                av(ff_gate[0:rows, k, :], ff_ps[(2 * k) % 4][0:rows, :], ACT.Gelu,
                   bias=cols_sb[0:rows, FF_BLOCKS + k:FF_BLOCKS + k + 1]).then_inc(ff_gelu, 1)

            with act.Fori(0, DEPTH) as layer:
                n0 = layer * (SEQS + 1)
                act.wait_ge(ff_added, layer * FF_STEPS + 1)
                act.wait_ge(shift_ready, n0 + 1)
                act.wait_ge(stream_ready, SEQS * TILES // 4)
                shift(0)
                attention_step(layer * SEQS, 0, first=True)
                with act.Fori(1, SEQS) as seq:
                    attention_step(layer * SEQS + seq, seq)
                attention_step(layer * SEQS + SEQS, SEQS, last=True)

                act.wait_ge(attn_added, (layer + 1) * SEQS + 1)
                act.wait_ge(in_ff, (layer + 1) * (16 * FF_LOADS))
                e0 = layer * (FF_STEPS + 1)
                ff_shift(0)
                ff_square(e0)
                ff_affine(e0)
                with act.Fori(0, FF_STEPS) as step:
                    f = layer * FF_STEPS + step
                    e = layer * (FF_STEPS + 1) + step
                    act.wait_ge(ff_centred, nth(e, 1, 0))
                    ff_shift(step + 1)
                    ff_gelu_of(f, 0)
                    ff_square(e + 1)
                    ff_gelu_of(f, 1)
                    ff_gelu_of(f, 2)
                    act.wait_ge(ff_up, nth(f, 2 * FF_BLOCKS, 2 * FF_BLOCKS - 1))
                    ff_affine(e + 1)
            ln_square(4)

        @block.gpsimd
        def _(pool):
            tt = nc.gpsimd.tensor_tensor

            nc.gpsimd.memset(mean_w[:, :], 1.0 / DIM).then_inc(const_ready, 1)
            nc.gpsimd.memset(neg_half[:, :], -0.5).then_inc(const_ready, 1)
            nc.gpsimd.memset(ones_w[:, :], 1.0).then_inc(const_ready, 1)
            pool.wait_ge(const_ready, 3)

            def power(out_, in_, width):
                return tt(out_, in_, neg_half[:, 0:1].broadcast_to([P, width]), ALU.pow)

            def ln_power(i):
                pool.wait_ge(ln_var, i)
                power(stat_rstd[:, :], stat_var[:, :], SEQS * TILES).then_inc(ln_rstd, 1)

            for i in (1, 2, 3):
                ln_power(i)

            def rnorms(n, u):
                pool.wait_ge(clamp_done, nth(n, UNITS, u))
                power(rnorm[:, u, :], clamped[:, u, :], CHUNK_HEADS).then_inc(rnorm_ready, 1)

            def sines(n, u, first):
                tile, c = divmod(u, UNITS // TILES)
                pool.wait_ge(normed_ready, nth(n, UNITS, u))
                if u >= 2 or not first:
                    pool.wait_ge(turned, nth(n, UNITS, u - 2))
                src = normed[:, u % 2, :].rearrange("p (h b d) -> p h b d", h=CHUNK_HEADS, b=2)
                dst = by_sin[:, u % 2, :].rearrange("p (h b d) -> p h b d", h=CHUNK_HEADS, b=2)
                tab = table[:, tile, 2 * (c // 2) + 1, :].rearrange("p (b d) -> p b d", b=2)
                for b in range(2):
                    last = tt(dst[:, :, b, :], src[:, :, 1 - b, :],
                              tab[:, b, :].unsqueeze(1).broadcast_to([P, CHUNK_HEADS, HEAD_DIM // 2]), ALU.mult)
                last.then_inc(sin_done, 1)

            def normalise(n, tile):
                pool.wait_ge(inv_ready, nth(n, TILES, tile))
                tt(probs[:, tile, :].rearrange("p (h j) -> p h j", h=HEADS),
                   exps[:, tile, :].rearrange("p (h j) -> p h j", h=HEADS),
                   row_inv[:, tile, :].unsqueeze(2).broadcast_to([P, HEADS, 2 * WINDOW]), ALU.mult)\
                    .then_inc(probs_ready, 1)

            def attention_step(n, first=False, last=False):
                old = n - 1
                if not last:
                    for u in range(UNITS):
                        rnorms(n, u)
                        if u > 0:
                            sines(n, u - 1, first)
                        if not first and u == 3:
                            normalise(old, 0)
                        if not first and u == 4:
                            normalise(old, 1)
                    sines(n, UNITS - 1, first)
                else:
                    normalise(old, 0)
                    normalise(old, 1)

            def ff_power(e):
                pool.wait_ge(ff_eps, nth(e, 1, 0))
                power(ff_rstd[:, :], ff_var[:, :], FF_COLS // P).then_inc(ff_rstd_done, 1)

            with pool.Fori(0, DEPTH) as layer:
                pool.wait_ge(table_ready, (layer + 1) * TILES + 1)
                attention_step(layer * SEQS, first=True)
                with pool.Fori(1, SEQS) as seq:
                    attention_step(layer * SEQS + seq)
                attention_step(layer * SEQS + SEQS, last=True)
                with pool.Fori(0, FF_STEPS + 1) as step:
                    ff_power(layer * (FF_STEPS + 1) + step)
            ln_power(4)

        @block.vector
        def _(dve):
            tt, ts, red = nc.vector.tensor_tensor, nc.vector.tensor_scalar, nc.vector.tensor_reduce
            steps = [0]

            def then(ins):
                steps[0] += 1
                ins.then_inc(dve_step, 1)
                dve.wait_ge(dve_step, steps[0])

            def tiles_wide(stat):
                return stat[:, :].unsqueeze(2).broadcast_to([P, SEQS * TILES, DIM])

            def layernorm(i, src, dst=None):
                then(red(stat_sum[:, :], src, X, ALU.add))
                then(ts(stat_mean[:, :], stat_sum[:, :], 1.0 / DIM, None, ALU.mult))
                tt(ln_xc, src, tiles_wide(stat_mean), ALU.subtract).then_inc(ln_centred, 1)
                dve.wait_ge(ln_squared, i)
                then(red(stat_ss[:, :], ln_sq, X, ALU.add))
                ts(stat_var[:, :], stat_ss[:, :], 1.0 / DIM, EPS, ALU.mult, ALU.add).then_inc(ln_var, 1)
                dve.wait_ge(ln_rstd, i)
                if dst is not None:
                    dve.wait_ge(ln_centred, i)
                    tt(dst, ln_xc, tiles_wide(stat_rstd), ALU.mult).then_inc(ln_scaled, 1)
                    dve.wait_ge(ln_scaled, i)

            for used in (attn_added, table_ready, ff_added, ff_gated, a_y_sb):
                dve.sem_inc(used, 1)
            dve.wait_ge(in_x, 16)
            layernorm(1, resid[:, :, :])
            ts(ln_sq[:, 0, 0:1], stat_rstd[:, 0:1], 1.0, None, ALU.mult).then_inc(ln_scaled, 1)
            dve.wait_ge(ln_scaled, 1)
            then(nc.vector.memset(flat[:, :], 0.0))
            then(nc.vector.memset(a_v[:, :, :, A_DIM:A_DIM + 1], 1.0))
            dve.wait_ge(in_first, 16 * FIRST_LOADS)
            with dve.Fori(0, SEQS) as n:
                tt(a_x[:, :, :], ln_xc[:, bass.ds(n * TILES, TILES), :],
                   stat_rstd[:, bass.ds(n * TILES, TILES)].unsqueeze(2).broadcast_to([P, TILES, DIM]), ALU.mult)\
                    .then_inc(a_x_ready, 1)
                dve.wait_ge(a_v_ps, nth(n, 1, 0))
                nc.vector.tensor_copy(a_v[:, :, :, 0:A_DIM],
                                      a_pt_ps[0][:, 0:TOKENS].rearrange("p (t h d) -> p t h d", t=TILES, h=A_HEADS))\
                    .then_inc(a_v_sb, 1)

                def maximum(h):
                    dve.wait_ge(a_scored, nth(n, A_HEADS, h))
                    red(a_nmax[:, h, :], a_s_ps[h % 3][:, :].rearrange("p (t n) -> p t n", t=TILES), X, ALU.max,
                        negate=True).then_inc(a_maxed, 1)

                def divide(g):
                    dve.wait_ge(a_spread, nth(n, A_GROUPS, g))
                    nc.vector.reciprocal(a_inv[:, g % 2, :], a_m_ps[:, 0:TOKENS]).then_inc(a_inv_ready, 1)
                    dve.wait_ge(a_inv_ready, nth(n, A_GROUPS, g))
                    tt(a_on[:, g, :], a_os[:, g % 2, :], a_inv[:, g % 2, :], ALU.mult).then_inc(a_on_ready, 1)

                maximum(0)
                maximum(1)
                for h in range(A_HEADS):
                    if h + 2 < A_HEADS:
                        maximum(h + 2)
                    if h % 2 == 0:
                        dve.wait_ge(a_turned, nth(n, A_HEADS, h))
                        if h >= 2:
                            dve.wait_ge(a_mixed, nth(n, A_HEADS, h - 2))
                        nc.vector.tensor_copy(a_pt[:, 0, :, :],
                                              a_pt_ps[0][:, :].rearrange("p (t n) -> p t n", t=TILES))\
                            .then_inc(a_pt_dve, 1)
                    if h % A_PER_GROUP == 1 and h > 1:
                        divide(h // A_PER_GROUP - 1)
                divide(A_GROUPS - 1)
                dve.wait_ge(a_y_ps, nth(n, 1, 0))
                tt(y_all[:, bass.ds(n * TILES, TILES), :], a_m_ps[:, 0:TOKENS].rearrange("p (t d) -> p t d", t=TILES),
                   b_unify_sb[:, :].unsqueeze(1).broadcast_to([P, TILES, DIM]), ALU.add).then_inc(a_y_sb, 1)

            dve.wait_ge(a_y_sb, SEQS + 1)
            layernorm(2, y_all, dst=ln_xc)
            then(tt(resid[:, :, :], resid[:, :, :], ln_xc, ALU.add))
            layernorm(3, resid[:, :, :], dst=ln_xc)

            nc.vector.memset(stream[:, SEQS:, :], 0.0).then_inc(zero_ready, 1)
            nc.vector.memset(stream[:, 0:SEQS, 0:1], 0.0).then_inc(zero_ready, 1)
            nc.vector.memset(k_t[:, :, 0:WINDOW], 0.0).then_inc(zero_ready, 1)
            dve.wait_ge(in_const, 16 * CONST_LOADS)
            then(nc.vector.memset(band[:, :, :], 0.0))
            then(nc.vector.tensor_copy(ident_b[:, :], ident_f[:, :]))
            for i in range(2):
                then(nc.vector.tensor_copy(mask_b[:, i, :, :],
                                           mask_f[:, i, :].unsqueeze(1).broadcast_to([P, CHUNK_HEADS, HEAD_DIM])))

            def heads_of(ap):
                return ap.rearrange("p (h d) -> p h d", h=CHUNK_HEADS)

            def sum_squares(n, u):
                dve.wait_ge(squared, nth(n, UNITS, u))
                red(sumsq[:, u, :], heads_of(squares[:, u % 2, :]), X, ALU.add).then_inc(summed, 1)
                dve.wait_ge(summed, nth(n, UNITS, u))
                ts(clamped[:, u, :], sumsq[:, u, :], LEAST_NORM ** 2, None, ALU.max).then_inc(clamp_done, 1)

            def norm_and_cosines(n, u, first):
                tile, c = divmod(u, UNITS // TILES)
                dve.wait_ge(rnorm_ready, nth(n, UNITS, u))
                if u >= 2 or not first:
                    dve.wait_ge(sin_done, nth(n, UNITS, u - 2))
                    dve.wait_ge(cos_done, nth(n, UNITS, u - 2))
                tt(heads_of(normed[:, u % 2, :]), heads_of(proj[u % 2][:, :]),
                   rnorm[:, u, :].unsqueeze(2).broadcast_to([P, CHUNK_HEADS, HEAD_DIM]), ALU.mult)\
                    .then_inc(normed_ready, 1)
                dve.wait_ge(normed_ready, nth(n, UNITS, u))
                if u >= 2 or not first:
                    dve.wait_ge(turned, nth(n, UNITS, u - 2))
                tt(heads_of(by_cos[:, u % 2, :]), heads_of(normed[:, u % 2, :]),
                   table[:, tile, 2 * (c // 2), :].unsqueeze(1).broadcast_to([P, CHUNK_HEADS, HEAD_DIM]), ALU.mult)\
                    .then_inc(cos_done, 1)

            def lower(n, tile):
                dve.wait_ge(scored, nth(n, TILES, tile))
                red(row_max[:, tile, :], score, X, ALU.max).then_inc(maxed, 1)
                dve.wait_ge(maxed, nth(n, TILES, tile))
                tt(probs[:, tile, :].rearrange("p (h j) -> p h j", h=HEADS), score,
                   row_max[:, tile, :].unsqueeze(2).broadcast_to([P, HEADS, 2 * WINDOW]), ALU.subtract)\
                    .then_inc(lowered, 1)

            def row_sums(n, tile):
                dve.wait_ge(exped, nth(n, TILES, tile))
                red(row_sum[:, tile, :], exps[:, tile, :].rearrange("p (h j) -> p h j", h=HEADS), X, ALU.add)\
                    .then_inc(row_summed, 1)
                dve.wait_ge(row_summed, nth(n, TILES, tile))
                nc.vector.reciprocal(row_inv[:, tile, :], row_sum[:, tile, :]).then_inc(inv_ready, 1)

            def turn_probs(n, tile):
                dve.wait_ge(probs_ready, nth(n, TILES, tile))
                nc.vector.transpose(probs_t[:, tile, :, :].rearrange("p b (h i) -> p h b i", h=HEADS),
                                    probs[:, tile, :].rearrange("p (h b j) -> p h b j", h=HEADS, b=2))\
                    .then_inc(probs_turned, 1)

            def attention_step(n, seq, first=False, last=False):
                old = n - 1
                if not last:
                    sum_squares(n, 0)
                    sum_squares(n, 1)
                    norm_and_cosines(n, 0, first)
                if not first:
                    lower(old, 0)
                if not last:
                    norm_and_cosines(n, 1, first)
                    sum_squares(n, 2)
                if not first:
                    row_sums(old, 0)
                    lower(old, 1)
                if not last:
                    sum_squares(n, 3)
                    norm_and_cosines(n, 2, first)
                if not first:
                    row_sums(old, 1)
                for u in range(3, UNITS):
                    if not last:
                        if u + 1 < UNITS:
                            sum_squares(n, u + 1)
                        norm_and_cosines(n, u, first)
                    if not first and u == 4:
                        turn_probs(old, 0)
                    if not first and u == 5:
                        turn_probs(old, 1)
                if not first:
                    dve.wait_ge(unified, nth(old, 1, 0))
                    at = stream[:, bass.ds(seq - 1, 1), 1:TOKENS + 1].rearrange("p a n -> p (a n)")
                    tt(at, at, wo_ps[:, 0:TOKENS], ALU.add).then_inc(attn_added, 1)

            def ff_centre(e):
                dve.wait_ge(ff_mean, nth(e, 1, 0))
                tt(ff_xc[:, :], ff_x[:, :], ff_mean_ps[:, :], ALU.subtract).then_inc(ff_centred, 1)

            def ff_epsilon(e):
                dve.wait_ge(ff_var_done, nth(e, 1, 0))
                ts(ff_var[:, :], ff_var_ps[:, 0:FF_COLS // P], EPS, None, ALU.add).then_inc(ff_eps, 1)

            def ff_diagonals(e):
                dve.wait_ge(ff_rstd_done, nth(e, 1, 0))
                tt(ff_diag[:, :, :], ident_f[:, :].unsqueeze(1).broadcast_to([P, FF_COLS // P, P]),
                   ff_rstd[:, :].unsqueeze(2).broadcast_to([P, FF_COLS // P, P]), ALU.mult).then_inc(ff_diag_ready, 1)

            def ff_scale(e):
                dve.wait_ge(ff_rstd_wide, nth(e, 1, 0))
                tt(ff_x0[:, :], ff_xc[:, :], ff_rstd_ps[:, :], ALU.mult).then_inc(ff_scaled, 1)

            def ff_gate_of(f, k):
                rows = P if k < FF_BLOCKS - 1 else FF_LAST
                dve.wait_ge(ff_up, nth(f, 2 * FF_BLOCKS, 2 * k + 1))
                dve.wait_ge(ff_gelu, nth(f, FF_BLOCKS, k))
                nc.vector.scalar_tensor_tensor(ff_h[0:rows, k, :], ff_ps[(2 * k + 1) % 4][0:rows, :],
                                               cols_sb[0:rows, k:k + 1], ff_gate[0:rows, k, :], ALU.add, ALU.mult)\
                    .then_inc(ff_gated, 1)

            with dve.Fori(0, DEPTH) as layer:
                dve.wait_ge(in_attn, (layer + 1) * (16 * ATTN_LOADS))
                for tile in range(TILES):
                    tt(table[:, tile, :, :], rope_sb[:, tile, :, :], scales_sb[:, :, :], ALU.mult)\
                        .then_inc(table_ready, 1)
                dve.wait_ge(table_ready, (layer + 1) * TILES + 1)
                attention_step(layer * SEQS, 0, first=True)
                with dve.Fori(1, SEQS) as seq:
                    attention_step(layer * SEQS + seq, seq)
                attention_step(layer * SEQS + SEQS, SEQS, last=True)

                dve.wait_ge(in_ff, (layer + 1) * (16 * FF_LOADS))
                e0 = layer * (FF_STEPS + 1)
                ff_centre(e0)
                ff_epsilon(e0)
                ff_diagonals(e0)
                ff_scale(e0)
                with dve.Fori(0, FF_STEPS) as step:
                    f = layer * FF_STEPS + step
                    e = layer * (FF_STEPS + 1) + step
                    dve.wait_ge(ff_scaled, nth(e, 1, 0))
                    ff_centre(e + 1)
                    ff_gate_of(f, 0)
                    ff_epsilon(e + 1)
                    ff_gate_of(f, 1)
                    ff_diagonals(e + 1)
                    dve.wait_ge(ff_xn_ready, nth_of_used(e, 1, 0))
                    ff_gate_of(f, 2)
                    ff_scale(e + 1)
                    dve.wait_ge(ff_down, nth(f, 1, 0))
                    at = stream[:, bass.ds(step * FF_SEQS, FF_SEQS), 1:TOKENS + 1]
                    nc.vector.scalar_tensor_tensor(
                        at, ff_y_ps[:, :].rearrange("p (s n) -> p s n", s=FF_SEQS),
                        cols_sb[:, 2 * FF_BLOCKS:2 * FF_BLOCKS + 1], at, ALU.add, ALU.add).then_inc(ff_added, 1)

            for c in range(SEQS * TILES // 4):
                dve.wait_ge(x_turned, SEQS * TILES // 4 + c + 1)
                nc.vector.tensor_copy(y_all[:, 4 * c:4 * c + 4, :],
                                      proj[c % 2][:, :].rearrange("p (n d) -> p n d", n=4)).then_inc(out_turned, 1)
            dve.wait_ge(out_turned, SEQS * TILES // 4)
            layernorm(4, y_all, dst=ln_xc)
            for c in range(4):
                rows = slice(c * 8, (c + 1) * 8)
                tt(resid[:, rows, :], resid[:, rows, :], ln_xc[:, rows, :], ALU.add).then_inc(out_copied, 1)


def rope_tables(np):
    f = np.float32
    half = np.arange(0, HEAD_DIM, 2, dtype=f)
    inv_freq = f(1.0) / np.power(f(10000.0), half / f(HEAD_DIM))
    t = np.arange(TOKENS, dtype=f)
    freqs = t[:, None] * inv_freq[None, :]
    freqs = np.concatenate([freqs, freqs], -1)
    base = (half + f(0.4 * HEAD_DIM)) / f(1.4 * HEAD_DIM)
    power = (t - f(TOKENS // 2)) / f(WINDOW // 2)
    scale = np.power(base[None, :], power[:, None])
    scale = np.concatenate([scale, scale], -1)
    sign = np.where(np.arange(HEAD_DIM) < HEAD_DIM // 2, -1, 1).astype(f)
    cos, sin = np.cos(freqs), np.sin(freqs) * sign
    tables = np.stack([cos * scale, sin * scale, cos / scale, sin / scale], 1).astype(f)
    return np.ascontiguousarray(tables.reshape(TILES, P, 4, HEAD_DIM).transpose(1, 0, 2, 3))


def window_masks(np):
    i = np.arange(P) % WINDOW
    j = np.arange(2 * WINDOW)
    seen = (j[None, :] >= i[:, None]) & (j[None, :] <= i[:, None] + WINDOW)
    none_before = (np.arange(P) >= WINDOW)[:, None] | (j >= WINDOW)[None, :]
    both = np.stack([seen & none_before, seen], 1)
    return np.where(both, 0.0, MASKED).astype(np.float32)


def kernel(L0_attn_x, L0_attn_W_down, L0_attn_tokeys, L0_attn_toqueries, L0_attn_tovalues, L0_attn_W_unify,
           L0_attn_b_unify, L0_ffn_Wqkv, L0_ffn_q_scale, L0_ffn_k_scale, L0_ffn_Wo, L0_ffn_ln_g, L0_ffn_ln_b,
           L0_ffn_W1, L0_ffn_b1, L0_ffn_W2, L0_ffn_b2):
    import numpy as np
    import concourse.bacc as bacc
    from concourse.bass_utils import run_bass_kernel_spmd

    f = np.float32
    qk_pad = np.zeros((P, 2, A_GROUPS, P), f)
    v_block = np.zeros((P, P), f)
    w_unify = np.zeros((P, A_GROUPS, DIM), f)
    for h in range(A_HEADS):
        g, j = divmod(h, A_PER_GROUP)
        rows, cols = slice(h * A_DIM, (h + 1) * A_DIM), slice(j * A_ROWS, j * A_ROWS + A_DIM)
        qk_pad[rows, 0, g, cols] = np.asarray(L0_attn_toqueries)[h].T
        qk_pad[rows, 1, g, cols] = np.asarray(L0_attn_tokeys)[h].T
        v_block[rows, rows] = np.asarray(L0_attn_tovalues)[h].T
        w_unify[cols, g, :] = np.asarray(L0_attn_W_unify)[rows, :]
    columns = np.zeros((DEPTH, P, 2 * FF_BLOCKS + 3), f)
    b1 = np.asarray(L0_ffn_b1)
    for part in range(2):
        for k in range(FF_BLOCKS):
            rows = P if k < FF_BLOCKS - 1 else FF_LAST
            columns[:, 0:rows, part * FF_BLOCKS + k] = b1[:, part * FF + k * P:part * FF + k * P + rows]
    for i, a in enumerate((L0_ffn_b2, L0_ffn_ln_g, L0_ffn_ln_b)):
        columns[:, :, 2 * FF_BLOCKS + i] = np.asarray(a)
    w2 = np.zeros((DEPTH, FF_BLOCKS * P, DIM), f)
    w2[:, 0:FF, :] = np.asarray(L0_ffn_W2)
    qs, ks = np.asarray(L0_ffn_q_scale), np.asarray(L0_ffn_k_scale)
    scales = np.stack([qs, np.roll(qs, HEAD_DIM // 2, 1), ks, np.roll(ks, HEAD_DIM // 2, 1)], 1)
    spread = np.zeros((P, P), f)
    for j in range(A_PER_GROUP):
        spread[j * A_ROWS + A_DIM, j * A_ROWS:(j + 1) * A_ROWS] = 1.0

    arrays = {
        "x": np.asarray(L0_attn_x).reshape(SEQS * TOKENS, DIM), "w_down": np.asarray(L0_attn_W_down),
        "qk_pad": qk_pad, "v_block": v_block, "w_unify": w_unify,
        "b_unify": np.asarray(L0_attn_b_unify), "w_qkv": np.asarray(L0_ffn_Wqkv), "w_o": np.asarray(L0_ffn_Wo),
        "scales": scales, "w1": np.asarray(L0_ffn_W1), "w2": w2, "columns": columns,
        "rope": rope_tables(np), "ident": np.eye(P, dtype=f), "mask": window_masks(np), "spread": spread,
    }
    arrays = {f"in_{k}": np.ascontiguousarray(v) for k, v in arrays.items()}
    nc = bacc.Bacc("TRN2", target_bir_lowering=False, num_devices=1)
    args = [nc.dram_tensor(k, v.shape, mybir.dt.from_np(v.dtype), kind="ExternalInput").ap()
            for k, v in arrays.items()]
    result = nc.dram_tensor("result", (SEQS * TOKENS, DIM), mybir.dt.float32, kind="ExternalOutput").ap()
    build(nc, *args, result)
    r = run_bass_kernel_spmd(nc, [arrays], core_ids=[0])
    return r.results[0]["result"].reshape(SEQS, TOKENS, DIM)
```

```python
import concourse.bass as bass
from concourse import mybir
from contextlib import ExitStack

SEQS, TOKENS, DIM = 16, 256, 128
P = 128
TILES = TOKENS // P
A_HEADS, A_DIM = 16, 8
A_ROWS = 32
A_PER_GROUP = P // A_ROWS
A_GROUPS = A_HEADS // A_PER_GROUP
DEPTH, HEADS, HEAD_DIM, WINDOW = 6, 16, 64, 32
INNER = HEADS * HEAD_DIM
PAIRS = HEADS // 2
WINDOWS = TOKENS // WINDOW
TILE_WINDOWS = P // WINDOW
CHUNK = 512
CHUNK_HEADS = CHUNK // HEAD_DIM
UNITS = TILES * 2 * INNER // CHUNK
V_UNITS = TILES * INNER // CHUNK
FF = DIM * 4 * 2 // 3
FF_BLOCKS = -(-FF // P)
FF_LAST = FF - (FF_BLOCKS - 1) * P
FF_SEQS = 2
FF_COLS = FF_SEQS * TOKENS
FF_STEPS = SEQS // FF_SEQS
EPS = 1e-5
QK_SCALE = 8.0
LEAST_NORM = 1e-12
MASKED = -float(2 ** 100)


def nth(n, per_iteration, j):
    return n * per_iteration + (j + 1)


def nth_of_used(n, per_iteration, j):
    return nth(n, per_iteration, j) + 1


def build(nc, x, w_down, qk_pad, v_block, w_unify, b_unify, w_qkv, w_o, scales, w1, w2, columns,
          rope, ident, mask, spread, out):
    f32, bf16 = mybir.dt.float32, mybir.dt.bfloat16
    ALU = mybir.AluOpType
    ACT = mybir.ActivationFunctionType
    X = mybir.AxisListType.X

    ctx = ExitStack()
    with ctx:
        def sb(name, shape, dt=f32):
            return ctx.enter_context(nc.sbuf_tensor(name, shape, dt))

        def sem(name):
            return ctx.enter_context(nc.semaphore(name))

        resid = sb("resid", [P, SEQS * TILES, DIM])
        stream = sb("stream", [P, SEQS + FF_SEQS, TOKENS + 1])
        ident_f = sb("ident_f", [P, P])
        ident_b = sb("ident_b", [P, P], bf16)
        mask_f = sb("mask_f", [P, 2, HEAD_DIM])
        mask_b = sb("mask_b", [P, 2, CHUNK_HEADS, HEAD_DIM], bf16)
        mean_w = sb("mean_w", [P, P])
        ones_w = sb("ones_w", [P, P])
        neg_half = sb("neg_half", [P, 1])
        spread_sb = sb("spread_sb", [P, P])
        stat_sum = sb("stat_sum", [P, SEQS * TILES])
        stat_mean = sb("stat_mean", [P, SEQS * TILES])
        stat_ss = sb("stat_ss", [P, SEQS * TILES])
        stat_var = sb("stat_var", [P, SEQS * TILES])
        stat_rstd = sb("stat_rstd", [P, SEQS * TILES])
        w_down_sb = sb("w_down_sb", [P, P])
        qk_pad_sb = sb("qk_pad_sb", [P, 2, A_GROUPS, P])
        v_block_sb = sb("v_block_sb", [P, P])
        w_unify_sb = sb("w_unify_sb", [P, A_GROUPS, P])
        b_unify_sb = sb("b_unify_sb", [P, DIM])
        w_qkv_sb = sb("w_qkv_sb", [P, 3 * INNER])
        w_o_sb = sb("w_o_sb", [P, PAIRS, DIM])
        w1_sb = sb("w1_sb", [P, 2 * FF])
        w2_sb = sb("w2_sb", [P, FF_BLOCKS, DIM])
        cols_sb = sb("cols_sb", [P, 2 * FF_BLOCKS + 3])
        rope_sb = sb("rope_sb", [P, TILES, 4, HEAD_DIM])
        scales_sb = sb("scales_sb", [P, 4, HEAD_DIM])
        table = sb("table", [P, TILES, 4, HEAD_DIM])
        shifted = sb("shifted", [P, TOKENS])
        shifted_v = sb("shifted_v", [P, TOKENS])
        area_d = sb("area_d", [P, 12 * CHUNK])
        raw = area_d[:, 0:4 * CHUNK].rearrange("p (u n) -> p u n", u=4)
        squares = area_d[:, 4 * CHUNK:8 * CHUNK].rearrange("p (u n) -> p u n", u=4)
        sumsq = sb("sumsq", [P, UNITS, CHUNK_HEADS])
        clamped = sb("clamped", [P, UNITS, CHUNK_HEADS])
        rnorm = sb("rnorm", [P, UNITS, CHUNK_HEADS])
        normed = sb("normed", [P, 4, CHUNK])
        by_cos = sb("by_cos", [P, 4, CHUNK])
        by_sin = sb("by_sin", [P, 4, CHUNK])
        k_t = sb("k_t", [P, PAIRS, WINDOW + TOKENS])
        row_max = sb("row_max", [P, TILES, HEADS])
        row_sum = sb("row_sum", [P, TILES, HEADS])
        row_inv = sb("row_inv", [P, TILES, HEADS])
        area_a = sb("area_a", [P, 2 * TILES * INNER])
        area_b = sb("area_b", [P, 2 * TILES * INNER])
        area_c = sb("area_c", [P, 2 * TILES * INNER])
        half = TILES * INNER
        probs = area_a[:, 0:half].rearrange("p (t n) -> p t n", t=TILES)
        exps = area_a[:, half:].rearrange("p (t n) -> p t n", t=TILES)
        v_sb = area_b[:, 0:half].rearrange("p (t n) -> p t n", t=TILES)
        att_t = area_b[:, half:].rearrange("p (c n) -> p c n", c=PAIRS)
        q_t = area_c[:, 0:half].rearrange("p (c n) -> p c n", c=PAIRS)
        probs_t = area_c[:, half:].rearrange("p (t b n) -> p t b n", t=TILES, b=2)
        band = sb("band", [P, 2 * TILE_WINDOWS + 1, HEADS * WINDOW])
        ff_area = area_d[:, :].rearrange("p (u n) -> p u n", n=FF_COLS)
        ff_x, ff_xc, ff_sq, ff_x0, ff_xn = (ff_area[:, i, :] for i in range(5))
        ff_gate, ff_h = ff_area[:, 5:8, :], ff_area[:, 8:11, :]
        ff_diag = ff_area[:, 11, :].rearrange("p (c n) -> p c n", n=P)
        ff_var = sb("ff_var", [P, FF_COLS // P])
        ff_rstd = sb("ff_rstd", [P, FF_COLS // P])
        ln_sq = area_a[:, :].rearrange("p (n d) -> p n d", d=DIM)
        ln_xc = area_b[:, :].rearrange("p (n d) -> p n d", d=DIM)
        y_all = area_c[:, :].rearrange("p (n d) -> p n d", d=DIM)
        flat = band[:, :, :].rearrange("p a b -> p (a b)")
        side = A_GROUPS * TOKENS
        a_q = flat[:, 0:side].rearrange("p (g n) -> p g n", g=A_GROUPS)
        a_k = flat[:, side:2 * side].rearrange("p (g n) -> p g n", g=A_GROUPS)
        a_v = flat[:, 2 * side:3 * side].rearrange("p (t h r) -> p t h r", t=TILES, h=A_HEADS)
        a_on = flat[:, 3 * side:4 * side].rearrange("p (g n) -> p g n", g=A_GROUPS)
        a_x = sb("a_x", [P, TILES, DIM])
        a_xt = sb("a_xt", [P, TOKENS])
        a_xd = sb("a_xd", [P, TOKENS])
        a_nmax = sb("a_nmax", [P, A_HEADS, TILES])
        a_p = area_d[:, 0:4 * TOKENS].rearrange("p (r t n) -> p r t n", r=2, t=TILES)
        a_pt = area_d[:, 4 * TOKENS:8 * TOKENS].rearrange("p (r t n) -> p r t n", r=2, t=TILES)
        a_os = area_d[:, 8 * TOKENS:10 * TOKENS].rearrange("p (r n) -> p r n", r=2)
        a_inv = area_d[:, 10 * TOKENS:12 * TOKENS].rearrange("p (r n) -> p r n", r=2)

        bank = [ctx.enter_context(nc.psum_tensor(f"bank{i}", [P, CHUNK], f32)) for i in range(6)]
        wide = ctx.enter_context(nc.psum_tensor("wide", [P, 2 * CHUNK], f32))
        proj = bank[0:2]
        turn = [bank[2], bank[5]]
        att_o = bank[3:5]
        wo_ps = bank[3]
        score = wide[:, :].rearrange("p (h j) -> p h j", j=2 * WINDOW)
        wide_half = [wide[:, 0:CHUNK], wide[:, CHUNK:2 * CHUNK]]
        ff_mean_ps, ff_var_ps = bank[0], bank[1]
        ff_ps = [bank[2][:, :], bank[3][:, :], wide_half[0], wide_half[1]]
        ff_rstd_ps = bank[4]
        ff_y_ps = bank[5]
        a_s_ps = bank[0:3]
        a_pt_ps = bank[3:5]
        a_o_ps = [wide_half[0], wide_half[1]]
        a_m_ps = bank[5]

        in_x, in_const, in_first = sem("in_x"), sem("in_const"), sem("in_first")
        in_attn, in_ff = sem("in_attn"), sem("in_ff")
        const_ready, zero_ready, dve_step = sem("const_ready"), sem("zero_ready"), sem("dve_step")
        ln_centred, ln_squared, ln_var = sem("ln_centred"), sem("ln_squared"), sem("ln_var")
        ln_rstd, ln_scaled, ln_eps = sem("ln_rstd"), sem("ln_scaled"), sem("ln_eps")
        x_turned, stream_ready = sem("x_turned"), sem("stream_ready")
        out_turned, out_copied, out_stored = sem("out_turned"), sem("out_copied"), sem("out_stored")
        a_x_ready, a_xt_ps, a_xt_sb = sem("a_x_ready"), sem("a_xt_ps"), sem("a_xt_sb")
        a_xd_ps, a_xd_sb, a_qk_ps = sem("a_xd_ps"), sem("a_xd_sb"), sem("a_qk_ps")
        a_qk_sb, a_v_ps, a_v_sb = sem("a_qk_sb"), sem("a_v_ps"), sem("a_v_sb")
        a_scored, a_maxed, a_exped = sem("a_scored"), sem("a_maxed"), sem("a_exped")
        a_turned, a_pt_act, a_pt_dve = sem("a_turned"), sem("a_pt_act"), sem("a_pt_dve")
        a_mixed, a_o_sb, a_spread = sem("a_mixed"), sem("a_o_sb"), sem("a_spread")
        a_inv_ready, a_on_ready = sem("a_inv_ready"), sem("a_on_ready")
        a_y_ps, a_y_sb = sem("a_y_ps"), sem("a_y_sb")
        table_ready, shift_ready = sem("table_ready"), sem("shift_ready")
        projected, squared, summed = sem("projected"), sem("squared"), sem("summed")
        raw_ready, shift_v_ready = sem("raw_ready"), sem("shift_v_ready")
        clamp_done, rnorm_ready, normed_ready = sem("clamp_done"), sem("rnorm_ready"), sem("normed_ready")
        cos_done, sin_done, turned = sem("cos_done"), sem("sin_done"), sem("turned")
        qk_ready, v_projected, v_ready = sem("qk_ready"), sem("v_projected"), sem("v_ready")
        scored, maxed, lowered = sem("scored"), sem("maxed"), sem("lowered")
        exped, row_summed, inv_ready = sem("exped"), sem("row_summed"), sem("inv_ready")
        probs_ready, probs_turned, band_ready = sem("probs_ready"), sem("probs_turned"), sem("band_ready")
        mixed, att_ready, unified = sem("mixed"), sem("att_ready"), sem("unified")
        attn_added = sem("attn_added")
        ff_shifted, ff_mean, ff_centred = sem("ff_shifted"), sem("ff_mean"), sem("ff_centred")
        ff_squared, ff_var_done, ff_eps = sem("ff_squared"), sem("ff_var_done"), sem("ff_eps")
        ff_rstd_done, ff_diag_ready, ff_rstd_wide = sem("ff_rstd_done"), sem("ff_diag_ready"), sem("ff_rstd_wide")
        ff_scaled, ff_xn_ready = sem("ff_scaled"), sem("ff_xn_ready")
        ff_up, ff_gelu, ff_gated = sem("ff_up"), sem("ff_gelu"), sem("ff_gated")
        ff_down, ff_added = sem("ff_down"), sem("ff_added")

        ATTN_LOADS, FF_LOADS, CONST_LOADS, FIRST_LOADS = 3, 3, 4, 5
        BAND_COPIES = WINDOWS + WINDOWS - 1
        DONE_ATTN = SEQS
        HALF_ROWS = P // 2

        block = ctx.enter_context(nc.Block())

        @block.sync
        def _(sp):
            sp.dma_start(resid[:, :, :], x.rearrange("(n p) d -> p n d", p=P)).then_inc(in_x, 16)
            sp.dma_start(ident_f[:, :], ident).then_inc(in_const, 16)
            sp.dma_start(mask_f[:, :, :], mask).then_inc(in_const, 16)
            sp.dma_start(rope_sb[:, :, :, :], rope).then_inc(in_const, 16)
            sp.dma_start(spread_sb[:, :], spread).then_inc(in_const, 16)
            sp.dma_start(w_down_sb[:, :], w_down).then_inc(in_first, 16)
            sp.dma_start(qk_pad_sb[:, :, :, :], qk_pad).then_inc(in_first, 16)
            sp.dma_start(v_block_sb[:, :], v_block).then_inc(in_first, 16)
            sp.dma_start(w_unify_sb[:, :, :], w_unify).then_inc(in_first, 16)
            sp.dma_start(b_unify_sb[:, :], b_unify.partition_broadcast(P)).then_inc(in_first, 16)

            def spread_band(tile):
                for w in range(TILE_WINDOWS):
                    wq = tile * TILE_WINDOWS + w
                    src = slice(w * WINDOW, (w + 1) * WINDOW)
                    sp.dma_start(band[src, wq + tile, :], probs_t[src, tile, 1, :]).then_inc(band_ready, 16)
                    if wq > 0:
                        key_tile, key_w = divmod(wq - 1, TILE_WINDOWS)
                        dst = slice(key_w * WINDOW, (key_w + 1) * WINDOW)
                        sp.dma_start(band[dst, wq + key_tile, :], probs_t[src, tile, 0, :])\
                          .then_inc(band_ready, 16)

            with sp.Fori(0, DEPTH) as layer:
                sp.wait_ge(attn_added, layer * DONE_ATTN + 1)
                sp.dma_start(w_qkv_sb[:, :], w_qkv[bass.ds(layer, 1), :, :].rearrange("a p n -> (a p) n"))\
                  .then_inc(in_attn, 16)
                sp.dma_start(w_o_sb[:, :, :], w_o[bass.ds(layer, 1), :, :].rearrange("a (c p) n -> p (a c) n", p=P))\
                  .then_inc(in_attn, 16)
                sp.wait_ge(table_ready, layer * TILES + 1)
                sp.dma_start(scales_sb[:, :, :], scales[bass.ds(layer, 1), :, :].rearrange("a c d -> a (c d)")
                             .broadcast_to([P, 4 * HEAD_DIM]).rearrange("p (c d) -> p c d", c=4)).then_inc(in_attn, 16)
                sp.wait_ge(ff_added, layer * FF_STEPS + 1)
                sp.dma_start(w1_sb[:, :], w1[bass.ds(layer, 1), :, :].rearrange("a p n -> (a p) n")).then_inc(in_ff, 16)
                sp.dma_start(w2_sb[:, :, :], w2[bass.ds(layer, 1), :, :].rearrange("a (c p) n -> p (a c) n", p=P))\
                  .then_inc(in_ff, 16)
                sp.wait_ge(ff_xn_ready, layer * (FF_STEPS + 1) + 1)
                sp.dma_start(cols_sb[:, :], columns[bass.ds(layer, 1), :, :].rearrange("a p n -> (a p) n"))\
                  .then_inc(in_ff, 16)
                with sp.Fori(0, SEQS) as seq:
                    n = layer * SEQS + seq
                    for tile in range(TILES):
                        sp.wait_ge(probs_turned, nth(n, TILES, tile))
                        spread_band(tile)

            for c in range(4):
                sp.wait_ge(out_copied, c + 1)
                rows = slice(c * 8, (c + 1) * 8)
                sp.dma_start(out.rearrange("(n p) d -> p n d", p=P)[:, rows, :], resid[:, rows, :])\
                  .then_inc(out_stored, 16)
            sp.wait_ge(out_stored, 4 * 16)

        @block.tensor
        def _(pe):
            mm = nc.tensor.matmul

            pe.wait_ge(in_first, 16 * FIRST_LOADS)
            pe.wait_ge(in_const, 16 * CONST_LOADS)

            def a_scores(n, h):
                g, j = divmod(h, A_PER_GROUP)
                rows = slice(j * A_ROWS, (j + 1) * A_ROWS)
                if h >= 3:
                    pe.wait_ge(a_exped, nth(n, A_HEADS, h - 3))
                for t in range(TILES):
                    last = mm(a_s_ps[h % 3][:, t * TOKENS:(t + 1) * TOKENS], a_q[rows, g, t * P:(t + 1) * P],
                              a_k[rows, g, :], start=True, stop=True)
                last.then_inc(a_scored, 1)

            def a_spread_sums(n, g):
                pe.wait_ge(a_o_sb, nth(n, A_GROUPS, g))
                if g > 0:
                    pe.wait_ge(a_inv_ready, nth(n, A_GROUPS, g - 1))
                mm(a_m_ps[:, 0:TOKENS], spread_sb[:, :], a_os[:, g % 2, :], start=True, stop=True)\
                    .then_inc(a_spread, 1)

            with pe.Fori(0, SEQS) as n:
                pe.wait_ge(a_x_ready, nth(n, 1, 0))
                pe.wait_ge(a_y_sb, nth_of_used(n, 1, -1))
                for t in range(TILES):
                    last = mm(a_m_ps[:, t * P:(t + 1) * P], a_x[:, t, :], ident_f[:, :], start=True, stop=True,
                              is_transpose=True)
                last.then_inc(a_xt_ps, 1)
                pe.wait_ge(a_xt_sb, nth(n, 1, 0))
                mm(a_m_ps[:, 0:TOKENS], w_down_sb[:, :], a_xt[:, :], start=True, stop=True).then_inc(a_xd_ps, 1)
                pe.wait_ge(a_xd_sb, nth(n, 1, 0))
                qk_banks = [a_s_ps[0], a_s_ps[1], a_s_ps[2], a_m_ps]
                for r in range(4):
                    side_no, g0 = divmod(2 * r, A_GROUPS)
                    for i in range(2):
                        last = mm(qk_banks[r][:, i * TOKENS:(i + 1) * TOKENS], qk_pad_sb[:, side_no, g0 + i, :],
                                  a_xd[:, :], start=True, stop=True)
                    last.then_inc(a_qk_ps, 1)
                for t in range(TILES):
                    last = mm(a_pt_ps[0][:, t * P:(t + 1) * P], a_xd[:, t * P:(t + 1) * P], v_block_sb[:, :],
                              start=True, stop=True)
                last.then_inc(a_v_ps, 1)
                pe.wait_ge(a_qk_sb, nth(n, 4, 3))
                a_scores(n, 0)
                a_scores(n, 1)
                pe.wait_ge(a_v_sb, nth(n, 1, 0))
                for h in range(A_HEADS):
                    g, j = divmod(h, A_PER_GROUP)
                    if h + 2 < A_HEADS:
                        a_scores(n, h + 2)
                    pe.wait_ge(a_exped, nth(n, A_HEADS, h))
                    if h >= 2:
                        pe.wait_ge(a_pt_dve if h % 2 == 0 else a_pt_act, nth(n, A_HEADS // 2, h // 2 - 1))
                    for kb in range(TILES):
                        for t in range(TILES):
                            at = kb * TOKENS + t * P
                            last = mm(a_pt_ps[h % 2][:, at:at + P], a_p[:, h % 2, t, kb * P:(kb + 1) * P],
                                      ident_f[:, :], start=True, stop=True, is_transpose=True)
                    last.then_inc(a_turned, 1)
                    if h % A_PER_GROUP == 0 and g > 0:
                        a_spread_sums(n, g - 1)
                    pe.wait_ge(a_pt_dve if h % 2 == 0 else a_pt_act, nth(n, A_HEADS // 2, h // 2))
                    if g >= 2 and j == 0:
                        pe.wait_ge(a_on_ready, nth(n, A_GROUPS, g - 2))
                    rows = slice(j * A_ROWS, (j + 1) * A_ROWS)
                    for kb in range(TILES):
                        last = mm(a_o_ps[g % 2][rows, 0:TOKENS], a_v[:, kb, h, :], a_pt[:, h % 2, kb, :],
                                  start=kb == 0, stop=kb == TILES - 1)
                    last.then_inc(a_mixed, 1)
                a_spread_sums(n, A_GROUPS - 1)
                pe.wait_ge(a_on_ready, nth(n, A_GROUPS, A_GROUPS - 1))
                for t in range(TILES):
                    for g in range(A_GROUPS):
                        last = mm(a_m_ps[:, t * P:(t + 1) * P], a_on[:, g, t * P:(t + 1) * P], w_unify_sb[:, g, :],
                                  start=g == 0, stop=g == A_GROUPS - 1)
                last.then_inc(a_y_ps, 1)

            pe.wait_ge(ln_scaled, 3)
            for c in range(SEQS * TILES // 4):
                if c >= 2:
                    pe.wait_ge(stream_ready, c - 1)
                for i in range(4):
                    last = mm(proj[c % 2][:, i * P:(i + 1) * P], ln_xc[:, 4 * c + i, :], ident_f[:, :],
                              start=True, stop=True, is_transpose=True)
                last.then_inc(x_turned, 1)

            def project(layer, seq, first, u):
                n = layer * SEQS + seq
                tile, c = divmod(u, UNITS // TILES)
                if u == 0:
                    pe.wait_ge(shift_ready, nth_of_used(n, 1, 0))
                if u > 0 or not first:
                    pe.wait_ge(raw_ready, nth(n, UNITS, u - 1))
                mm(proj[0][:, :], shifted[:, tile * P:(tile + 1) * P], w_qkv_sb[:, c * CHUNK:(c + 1) * CHUNK],
                   start=True, stop=True).then_inc(projected, 1)

            def project_v(layer, seq, first, j):
                n = layer * SEQS + seq
                c, tile = divmod(j, TILES)
                if j == 0:
                    pe.wait_ge(shift_v_ready, nth(n, 1, 0))
                if j > 0 or not first:
                    pe.wait_ge(v_ready, nth(n, V_UNITS, j - 1))
                at = 2 * INNER + c * CHUNK
                mm(proj[1][:, :], shifted_v[:, tile * P:(tile + 1) * P], w_qkv_sb[:, at:at + CHUNK],
                   start=True, stop=True).then_inc(v_projected, 1)

            def scores(layer, seq, first, tile):
                n = layer * SEQS + seq
                pe.wait_ge(qk_ready, nth(n, UNITS, (tile + 1) * (UNITS // TILES) - 1))
                if tile > 0 or not first:
                    pe.wait_ge(lowered, nth(n, TILES, tile - 1))
                for odd in range(2):
                    mm(wide_half[odd], ident_b[:, :], mask_b[:, 0 if tile == 0 else 1, :, :]
                       .rearrange("p h j -> p (h j)"), start=True, stop=False, skip_group_check=True)
                for pair in range(PAIRS):
                    for w in range(TILE_WINDOWS):
                        for odd in range(2):
                            rows = slice(odd * HEAD_DIM, (odd + 1) * HEAD_DIM)
                            at = tile * P + w * WINDOW
                            last = mm(score[w * WINDOW:(w + 1) * WINDOW, odd * PAIRS + pair, :],
                                      q_t[rows, pair, at:at + WINDOW], k_t[rows, pair, at:at + 2 * WINDOW],
                                      start=False, stop=True, skip_group_check=True)
                last.then_inc(scored, 1)

            def turn_unit(layer, seq, first, u):
                n = layer * SEQS + seq
                pe.wait_ge(cos_done, nth(n, UNITS, u))
                pe.wait_ge(sin_done, nth(n, UNITS, u))
                if u >= 2 or not first:
                    pe.wait_ge(qk_ready, nth(n, UNITS, u - 2))
                for i in range(CHUNK // P):
                    at = slice(i * P, (i + 1) * P)
                    mm(turn[u % 2][:, at], by_cos[:, u % 4, at], ident_f[:, :], start=True, stop=False,
                       is_transpose=True)
                    last = mm(turn[u % 2][:, at], by_sin[:, u % 4, at], ident_f[:, :], start=False, stop=True,
                              is_transpose=True)
                last.then_inc(turned, 1)

            def mix(layer, seq, first, j):
                n = layer * SEQS + seq
                if j == 0:
                    pe.wait_ge(band_ready, n * (16 * BAND_COPIES) + 16 * BAND_COPIES)
                    pe.wait_ge(v_ready, nth(n, V_UNITS, V_UNITS - 1))
                    pe.wait_ge(attn_added, nth_of_used(n, 1, -1))
                if j >= 2:
                    pe.wait_ge(att_ready, nth(n, PAIRS // 2, j - 2))
                cut = (TILE_WINDOWS + 1) * WINDOW
                for i in range(2):
                    pair = 2 * j + i
                    for odd in range(2):
                        rows = slice(odd * HEAD_DIM, (odd + 1) * HEAD_DIM)
                        at = (odd * PAIRS + pair) * WINDOW
                        feats = slice((2 * pair + odd) * HEAD_DIM, (2 * pair + odd + 1) * HEAD_DIM)
                        mm(att_o[j % 2][rows, i * TOKENS:i * TOKENS + cut], v_sb[:, 0, feats],
                           band[:, 0:TILE_WINDOWS + 1, at:at + WINDOW], start=True, stop=False, skip_group_check=True)
                        last = mm(att_o[j % 2][rows, i * TOKENS + P:(i + 1) * TOKENS], v_sb[:, 1, feats],
                                  band[:, TILE_WINDOWS + 1:, at:at + WINDOW], start=False, stop=True,
                                  skip_group_check=True)
                last.then_inc(mixed, 1)

            def unify(layer, seq, first):
                n = layer * SEQS + seq
                pe.wait_ge(att_ready, nth(n, PAIRS // 2, PAIRS // 2 - 1))
                for pair in range(PAIRS):
                    product = mm(wo_ps[:, 0:TOKENS], w_o_sb[:, pair, :], att_t[:, pair, :], start=pair == 0,
                                 stop=pair == PAIRS - 1)
                product.then_inc(unified, 1)

            def attention_step(layer, seq, place=None):
                before, now, after = (place is None or 0 <= place + i < SEQS for i in (-1, 0, 1))
                old, this, new = ((layer, seq + i, place is not None and place + i == 0) for i in (-1, 0, 1))
                if before:
                    project_v(*old, 1)
                if now:
                    project(*this, 6)
                if before:
                    project_v(*old, 2)
                if now:
                    turn_unit(*this, 2)
                    turn_unit(*this, 3)
                if before:
                    project_v(*old, 3)
                if now:
                    project(*this, 7)
                    scores(*this, 0)
                if after:
                    project(*new, 0)
                if now:
                    turn_unit(*this, 4)
                    project_v(*this, 0)
                if after:
                    project(*new, 1)
                if now:
                    turn_unit(*this, 5)
                if before:
                    mix(*old, 0)
                if after:
                    project(*new, 2)
                if before:
                    mix(*old, 1)
                    mix(*old, 2)
                if after:
                    project(*new, 3)
                if now:
                    turn_unit(*this, 6)
                    turn_unit(*this, 7)
                if before:
                    mix(*old, 3)
                if after:
                    project(*new, 4)
                if now:
                    scores(*this, 1)
                if before:
                    unify(*old)
                if after:
                    project(*new, 5)
                    turn_unit(*new, 0)
                    turn_unit(*new, 1)

            def ff_mean_of(e):
                pe.wait_ge(ff_shifted, nth(e, 1, 0))
                mm(ff_mean_ps[:, :], mean_w[:, :], ff_x[:, :], start=True, stop=True).then_inc(ff_mean, 1)

            def ff_var_of(e):
                pe.wait_ge(ff_squared, nth(e, 1, 0))
                for i in range(FF_COLS // P):
                    last = mm(ff_var_ps[:, i:i + 1], ff_sq[:, i * P:(i + 1) * P], mean_w[:, 0:1], start=True, stop=True)
                last.then_inc(ff_var_done, 1)

            def ff_rstd_of(e):
                pe.wait_ge(ff_diag_ready, nth(e, 1, 0))
                mm(ff_rstd_ps[:, :], ones_w[:, :], ff_diag[:, :, :].rearrange("p c n -> p (c n)"), start=True,
                   stop=True).then_inc(ff_rstd_wide, 1)

            def ff_up_of(f, k, wait=None):
                rows = P if k < FF_BLOCKS - 1 else FF_LAST
                for i, at in enumerate((FF + k * P, k * P)):
                    b = (2 * k + i) % 4
                    if k == 2:
                        if i == 0:
                            pe.wait_ge(ff_gelu, nth(f, FF_BLOCKS, 0))
                        else:
                            pe.wait_ge(ff_gated, nth_of_used(f, FF_BLOCKS, 0))
                    mm(ff_ps[b][0:rows, :], w1_sb[:, at:at + rows], ff_xn[:, :], start=True, stop=True)\
                        .then_inc(ff_up, 1)

            with pe.Fori(0, DEPTH) as layer:
                pe.wait_ge(in_attn, (layer + 1) * (16 * ATTN_LOADS))
                for place in (-1, 0, 1):
                    attention_step(layer, place, place)
                with pe.Fori(2, SEQS - 1) as seq:
                    attention_step(layer, seq)
                for place in (SEQS - 1, SEQS):
                    attention_step(layer, place, place)

                pe.wait_ge(in_ff, (layer + 1) * (16 * FF_LOADS))
                ff_mean_of(layer * (FF_STEPS + 1))
                ff_var_of(layer * (FF_STEPS + 1))
                ff_rstd_of(layer * (FF_STEPS + 1))
                with pe.Fori(0, FF_STEPS) as step:
                    f = layer * FF_STEPS + step
                    e = layer * (FF_STEPS + 1) + step
                    pe.wait_ge(ff_xn_ready, nth_of_used(e, 1, 0))
                    pe.wait_ge(ff_gated, nth_of_used(f, FF_BLOCKS, -1))
                    ff_up_of(f, 0)
                    ff_mean_of(e + 1)
                    ff_up_of(f, 1)
                    ff_var_of(e + 1)
                    ff_up_of(f, 2)
                    ff_rstd_of(e + 1)
                    pe.wait_ge(ff_added, nth_of_used(f, 1, -1))
                    for k in range(FF_BLOCKS):
                        rows = P if k < FF_BLOCKS - 1 else FF_LAST
                        pe.wait_ge(ff_gated, nth_of_used(f, FF_BLOCKS, k))
                        last = mm(ff_y_ps[:, :], w2_sb[0:rows, k, :], ff_h[0:rows, k, :], start=k == 0,
                                  stop=k == FF_BLOCKS - 1)
                    last.then_inc(ff_down, 1)

            pe.wait_ge(ff_added, DEPTH * FF_STEPS + 1)
            for c in range(SEQS * TILES // 4):
                if c >= 2:
                    pe.wait_ge(out_turned, c - 1)
                for i in range(4):
                    seq, tile = divmod(4 * c + i, TILES)
                    last = mm(proj[c % 2][:, i * P:(i + 1) * P], stream[:, seq, 1 + tile * P:1 + (tile + 1) * P],
                              ident_f[:, :], start=True, stop=True, is_transpose=True)
                last.then_inc(x_turned, 1)

        @block.scalar
        def _(act):
            av = nc.scalar.activation

            def ln_square(i):
                act.wait_ge(ln_centred, i)
                av(ln_sq, ln_xc, ACT.Square).then_inc(ln_squared, 1)

            for used in (ff_xn_ready, shift_ready):
                act.sem_inc(used, 1)
            ln_square(1)
            with act.Fori(0, SEQS) as n:
                act.wait_ge(a_xt_ps, nth(n, 1, 0))
                av(a_xt[:, :], a_m_ps[:, 0:TOKENS], ACT.Copy).then_inc(a_xt_sb, 1)
                act.wait_ge(a_xd_ps, nth(n, 1, 0))
                av(a_xd[:, :], a_m_ps[:, 0:TOKENS], ACT.Copy).then_inc(a_xd_sb, 1)
                qk_banks = [a_s_ps[0], a_s_ps[1], a_s_ps[2], a_m_ps]
                for r in range(4):
                    act.wait_ge(a_qk_ps, nth(n, 4, r))
                    side_no, g0 = divmod(2 * r, A_GROUPS)
                    av((a_q, a_k)[side_no][:, g0:g0 + 2, :], qk_banks[r][:, :].rearrange("p (g n) -> p g n", g=2),
                       ACT.Copy, scale=float(A_DIM) ** -0.25).then_inc(a_qk_sb, 1)
                for h in range(A_HEADS + 1):
                    if h < A_HEADS:
                        act.wait_ge(a_maxed, nth(n, A_HEADS, h))
                        if h >= 2:
                            act.wait_ge(a_turned, nth(n, A_HEADS, h - 2))
                        for t in range(TILES):
                            last = av(a_p[:, h % 2, t, :], a_s_ps[h % 3][:, t * TOKENS:(t + 1) * TOKENS], ACT.Exp,
                                      bias=a_nmax[:, h, t:t + 1])
                        last.then_inc(a_exped, 1)
                    if h >= 1:
                        g, j = divmod(h - 1, A_PER_GROUP)
                        if (h - 1) % 2 == 1:
                            act.wait_ge(a_turned, nth(n, A_HEADS, h - 1))
                            if h - 1 >= 2:
                                act.wait_ge(a_mixed, nth(n, A_HEADS, h - 3))
                            av(a_pt[:, 1, :, :], a_pt_ps[1][:, :].rearrange("p (t n) -> p t n", t=TILES), ACT.Copy)\
                                .then_inc(a_pt_act, 1)
                        if j == A_PER_GROUP - 1:
                            act.wait_ge(a_mixed, nth(n, A_HEADS, h - 1))
                            if g >= 2:
                                act.wait_ge(a_on_ready, nth(n, A_GROUPS, g - 2))
                            av(a_os[:, g % 2, :], a_o_ps[g % 2][:, 0:TOKENS], ACT.Copy).then_inc(a_o_sb, 1)

            ln_square(2)
            ln_square(3)
            for c in range(SEQS * TILES // 4):
                act.wait_ge(x_turned, c + 1)
                if c == 0:
                    act.wait_ge(zero_ready, 3)
                av(stream[:, 2 * c:2 * c + 2, 1:TOKENS + 1], proj[c % 2][:, :].rearrange("p (s n) -> p s n", s=2),
                   ACT.Copy).then_inc(stream_ready, 1)

            def shift(layer, seq, first):
                n = layer * SEQS + seq
                if not first:
                    act.wait_ge(projected, nth(n, UNITS, -1))
                    act.wait_ge(shift_v_ready, nth(n, 1, -1))
                av(shifted[0:HALF_ROWS, :], stream[0:HALF_ROWS, bass.ds(seq, 1), 1:TOKENS + 1]
                   .rearrange("p a n -> p (a n)"), ACT.Copy)
                av(shifted[HALF_ROWS:P, :], stream[HALF_ROWS:P, bass.ds(seq, 1), 0:TOKENS]
                   .rearrange("p a n -> p (a n)"), ACT.Copy).then_inc(shift_ready, 1)

            def square(layer, seq, first, u):
                n = layer * SEQS + seq
                act.wait_ge(projected, nth(n, UNITS, u))
                if u >= 4 or not first:
                    act.wait_ge(summed, nth(n, UNITS, u - 4))
                av(squares[:, u % 4, :], proj[0][:, :], ACT.Square).then_inc(squared, 1)
                if u >= 4 or not first:
                    act.wait_ge(normed_ready, nth(n, UNITS, u - 4))
                av(raw[:, u % 4, :], proj[0][:, :], ACT.Copy).then_inc(raw_ready, 1)

            def keep_shifted(layer, seq, first):
                n = layer * SEQS + seq
                act.wait_ge(projected, nth(n, UNITS, 0))
                if not first:
                    act.wait_ge(v_projected, nth(n, V_UNITS, -1))
                av(shifted_v[:, :], shifted[:, :], ACT.Copy).then_inc(shift_v_ready, 1)

            def take_unit(layer, seq, first, u):
                n = layer * SEQS + seq
                if u in (0, 2) and not first:
                    act.wait_ge(scored, nth(n, TILES, -2 if u == 0 else -1))
                tile, c = divmod(u, UNITS // TILES)
                pairs = slice((c % 2) * (PAIRS // 2), (c % 2 + 1) * (PAIRS // 2))
                act.wait_ge(turned, nth(n, UNITS, u))
                dst = q_t[:, pairs, tile * P:(tile + 1) * P] if c < 2 else \
                    k_t[:, pairs, WINDOW + tile * P:WINDOW + (tile + 1) * P]
                av(dst, turn[u % 2][:, :].rearrange("p (c n) -> p c n", c=PAIRS // 2), ACT.Copy).then_inc(qk_ready, 1)

            def take_v(layer, seq, first, j):
                n = layer * SEQS + seq
                c, tile = divmod(j, TILES)
                act.wait_ge(v_projected, nth(n, V_UNITS, j))
                if j == 0 and not first:
                    act.wait_ge(mixed, nth(n, PAIRS // 2, -1))
                av(v_sb[:, tile, c * CHUNK:(c + 1) * CHUNK], proj[1][:, :], ACT.Copy).then_inc(v_ready, 1)

            def exponentials(layer, seq, first, tile):
                n = layer * SEQS + seq
                act.wait_ge(lowered, nth(n, TILES, tile))
                av(exps[:, tile, :], probs[:, tile, :], ACT.Exp, scale=QK_SCALE).then_inc(exped, 1)

            def take_out(layer, seq, first, j):
                n = layer * SEQS + seq
                act.wait_ge(mixed, nth(n, PAIRS // 2, j))
                av(att_t[:, 2 * j:2 * j + 2, :], att_o[j % 2][:, :].rearrange("p (c n) -> p c n", c=2), ACT.Copy)\
                    .then_inc(att_ready, 1)

            def attention_step(layer, seq, place=None):
                before, now, after = (place is None or 0 <= place + i < SEQS for i in (-1, 0, 1))
                old, this, new = ((layer, seq + i, place is not None and place + i == 0) for i in (-1, 0, 1))
                if now:
                    take_unit(*this, 0)
                if before:
                    take_v(*old, 1)
                if now:
                    take_unit(*this, 1)
                    square(*this, 6)
                if before:
                    take_v(*old, 2)
                if now:
                    take_unit(*this, 2)
                    take_unit(*this, 3)
                if before:
                    take_v(*old, 3)
                if now:
                    keep_shifted(*this)
                if after:
                    shift(*new)
                if now:
                    square(*this, 7)
                if after:
                    square(*new, 0)
                if now:
                    take_unit(*this, 4)
                if after:
                    square(*new, 1)
                if now:
                    take_unit(*this, 5)
                if before:
                    take_out(*old, 0)
                if after:
                    square(*new, 2)
                if before:
                    take_out(*old, 1)
                if now:
                    exponentials(*this, 0)
                if before:
                    take_out(*old, 2)
                if now:
                    take_unit(*this, 6)
                if after:
                    square(*new, 3)
                if now:
                    take_unit(*this, 7)
                if after:
                    square(*new, 4)
                if now:
                    take_v(*this, 0)
                if before:
                    take_out(*old, 3)
                if after:
                    square(*new, 5)
                if now:
                    exponentials(*this, 1)

            def ff_shift(step):
                seqs = bass.ds(step * FF_SEQS, FF_SEQS)
                for rows, start in ((slice(0, HALF_ROWS), 1), (slice(HALF_ROWS, P), 0)):
                    last = av(ff_x[rows, :].rearrange("p (s n) -> p s n", s=FF_SEQS),
                              stream[rows, seqs, start:start + TOKENS], ACT.Copy)
                last.then_inc(ff_shifted, 1)

            def ff_square(e):
                act.wait_ge(ff_centred, nth(e, 1, 0))
                av(ff_sq[:, :], ff_xc[:, :], ACT.Square).then_inc(ff_squared, 1)

            def ff_affine(e):
                act.wait_ge(ff_scaled, nth(e, 1, 0))
                av(ff_xn[:, :], ff_x0[:, :], ACT.Identity, bias=cols_sb[:, 2 * FF_BLOCKS + 2:],
                   scale=cols_sb[:, 2 * FF_BLOCKS + 1:2 * FF_BLOCKS + 2]).then_inc(ff_xn_ready, 1)

            def ff_gelu_of(f, k):
                rows = P if k < FF_BLOCKS - 1 else FF_LAST
                act.wait_ge(ff_up, nth(f, 2 * FF_BLOCKS, 2 * k))
                av(ff_gate[0:rows, k, :], ff_ps[(2 * k) % 4][0:rows, :], ACT.Gelu,
                   bias=cols_sb[0:rows, FF_BLOCKS + k:FF_BLOCKS + k + 1]).then_inc(ff_gelu, 1)

            with act.Fori(0, DEPTH) as layer:
                act.wait_ge(ff_added, layer * FF_STEPS + 1)
                act.wait_ge(stream_ready, SEQS * TILES // 4)
                for place in (-1, 0, 1):
                    attention_step(layer, place, place)
                with act.Fori(2, SEQS - 1) as seq:
                    attention_step(layer, seq)
                for place in (SEQS - 1, SEQS):
                    attention_step(layer, place, place)

                act.wait_ge(attn_added, (layer + 1) * SEQS + 1)
                act.wait_ge(in_ff, (layer + 1) * (16 * FF_LOADS))
                e0 = layer * (FF_STEPS + 1)
                ff_shift(0)
                ff_square(e0)
                ff_affine(e0)
                with act.Fori(0, FF_STEPS) as step:
                    f = layer * FF_STEPS + step
                    e = layer * (FF_STEPS + 1) + step
                    act.wait_ge(ff_centred, nth(e, 1, 0))
                    ff_shift(step + 1)
                    ff_gelu_of(f, 0)
                    ff_square(e + 1)
                    ff_gelu_of(f, 1)
                    ff_gelu_of(f, 2)
                    act.wait_ge(ff_up, nth(f, 2 * FF_BLOCKS, 2 * FF_BLOCKS - 1))
                    ff_affine(e + 1)
            ln_square(4)

        @block.gpsimd
        def _(pool):
            tt = nc.gpsimd.tensor_tensor

            nc.gpsimd.memset(mean_w[:, :], 1.0 / DIM).then_inc(const_ready, 1)
            nc.gpsimd.memset(neg_half[:, :], -0.5).then_inc(const_ready, 1)
            nc.gpsimd.memset(ones_w[:, :], 1.0).then_inc(const_ready, 1)
            pool.wait_ge(const_ready, 3)

            def power(out_, in_, width):
                return tt(out_, in_, neg_half[:, 0:1].broadcast_to([P, width]), ALU.pow)

            def ln_power(i):
                pool.wait_ge(ln_var, i)
                power(stat_rstd[:, :], stat_var[:, :], SEQS * TILES).then_inc(ln_rstd, 1)

            for i in (1, 2, 3):
                ln_power(i)

            def rnorms(layer, seq, first, u):
                n = layer * SEQS + seq
                pool.wait_ge(clamp_done, nth(n, UNITS, u))
                power(rnorm[:, u, :], clamped[:, u, :], CHUNK_HEADS).then_inc(rnorm_ready, 1)

            def sines(layer, seq, first, u):
                n = layer * SEQS + seq
                tile, c = divmod(u, UNITS // TILES)
                pool.wait_ge(normed_ready, nth(n, UNITS, u))
                if u >= 4 or not first:
                    pool.wait_ge(turned, nth(n, UNITS, u - 4))
                src = normed[:, u % 4, :].rearrange("p (h b d) -> p h b d", h=CHUNK_HEADS, b=2)
                dst = by_sin[:, u % 4, :].rearrange("p (h b d) -> p h b d", h=CHUNK_HEADS, b=2)
                tab = table[:, tile, 2 * (c // 2) + 1, :].rearrange("p (b d) -> p b d", b=2)
                for b in range(2):
                    last = tt(dst[:, :, b, :], src[:, :, 1 - b, :],
                              tab[:, b, :].unsqueeze(1).broadcast_to([P, CHUNK_HEADS, HEAD_DIM // 2]), ALU.mult)
                last.then_inc(sin_done, 1)

            def normalise(layer, seq, first, tile):
                n = layer * SEQS + seq
                pool.wait_ge(inv_ready, nth(n, TILES, tile))
                tt(probs[:, tile, :].rearrange("p (h j) -> p h j", h=HEADS),
                   exps[:, tile, :].rearrange("p (h j) -> p h j", h=HEADS),
                   row_inv[:, tile, :].unsqueeze(2).broadcast_to([P, HEADS, 2 * WINDOW]), ALU.mult)\
                    .then_inc(probs_ready, 1)

            def attention_step(layer, seq, place=None):
                before, now, after = (place is None or 0 <= place + i < SEQS for i in (-1, 0, 1))
                old, this, new = ((layer, seq + i, place is not None and place + i == 0) for i in (-1, 0, 1))
                if now:
                    rnorms(*this, 6)
                    rnorms(*this, 7)
                if after:
                    rnorms(*new, 0)
                if now:
                    sines(*this, 6)
                    sines(*this, 7)
                if after:
                    rnorms(*new, 1)
                    rnorms(*new, 2)
                    sines(*new, 0)
                    sines(*new, 1)
                if now:
                    normalise(*this, 0)
                if after:
                    rnorms(*new, 3)
                    rnorms(*new, 4)
                    sines(*new, 2)
                    sines(*new, 3)
                if now:
                    normalise(*this, 1)
                if after:
                    rnorms(*new, 5)
                    sines(*new, 4)
                    sines(*new, 5)

            def ff_power(e):
                pool.wait_ge(ff_eps, nth(e, 1, 0))
                power(ff_rstd[:, :], ff_var[:, :], FF_COLS // P).then_inc(ff_rstd_done, 1)

            with pool.Fori(0, DEPTH) as layer:
                pool.wait_ge(table_ready, (layer + 1) * TILES + 1)
                for place in (-1, 0, 1):
                    attention_step(layer, place, place)
                with pool.Fori(2, SEQS - 1) as seq:
                    attention_step(layer, seq)
                for place in (SEQS - 1, SEQS):
                    attention_step(layer, place, place)
                with pool.Fori(0, FF_STEPS + 1) as step:
                    ff_power(layer * (FF_STEPS + 1) + step)
            ln_power(4)

        @block.vector
        def _(dve):
            tt, ts, red = nc.vector.tensor_tensor, nc.vector.tensor_scalar, nc.vector.tensor_reduce
            steps = [0]

            def then(ins):
                steps[0] += 1
                ins.then_inc(dve_step, 1)
                dve.wait_ge(dve_step, steps[0])

            def tiles_wide(stat):
                return stat[:, :].unsqueeze(2).broadcast_to([P, SEQS * TILES, DIM])

            def layernorm(i, src, dst=None):
                then(red(stat_sum[:, :], src, X, ALU.add))
                then(ts(stat_mean[:, :], stat_sum[:, :], 1.0 / DIM, None, ALU.mult))
                tt(ln_xc, src, tiles_wide(stat_mean), ALU.subtract).then_inc(ln_centred, 1)
                dve.wait_ge(ln_squared, i)
                then(red(stat_ss[:, :], ln_sq, X, ALU.add))
                ts(stat_var[:, :], stat_ss[:, :], 1.0 / DIM, EPS, ALU.mult, ALU.add).then_inc(ln_var, 1)
                dve.wait_ge(ln_rstd, i)
                if dst is not None:
                    dve.wait_ge(ln_centred, i)
                    tt(dst, ln_xc, tiles_wide(stat_rstd), ALU.mult).then_inc(ln_scaled, 1)
                    dve.wait_ge(ln_scaled, i)

            for used in (attn_added, table_ready, ff_added, ff_gated, a_y_sb):
                dve.sem_inc(used, 1)
            dve.wait_ge(in_x, 16)
            layernorm(1, resid[:, :, :])
            ts(ln_sq[:, 0, 0:1], stat_rstd[:, 0:1], 1.0, None, ALU.mult).then_inc(ln_scaled, 1)
            dve.wait_ge(ln_scaled, 1)
            then(nc.vector.memset(flat[:, :], 0.0))
            then(nc.vector.memset(a_v[:, :, :, A_DIM:A_DIM + 1], 1.0))
            dve.wait_ge(in_first, 16 * FIRST_LOADS)
            with dve.Fori(0, SEQS) as n:
                tt(a_x[:, :, :], ln_xc[:, bass.ds(n * TILES, TILES), :],
                   stat_rstd[:, bass.ds(n * TILES, TILES)].unsqueeze(2).broadcast_to([P, TILES, DIM]), ALU.mult)\
                    .then_inc(a_x_ready, 1)
                dve.wait_ge(a_v_ps, nth(n, 1, 0))
                nc.vector.tensor_copy(a_v[:, :, :, 0:A_DIM],
                                      a_pt_ps[0][:, 0:TOKENS].rearrange("p (t h d) -> p t h d", t=TILES, h=A_HEADS))\
                    .then_inc(a_v_sb, 1)

                def maximum(h):
                    dve.wait_ge(a_scored, nth(n, A_HEADS, h))
                    red(a_nmax[:, h, :], a_s_ps[h % 3][:, :].rearrange("p (t n) -> p t n", t=TILES), X, ALU.max,
                        negate=True).then_inc(a_maxed, 1)

                def divide(g):
                    dve.wait_ge(a_spread, nth(n, A_GROUPS, g))
                    nc.vector.reciprocal(a_inv[:, g % 2, :], a_m_ps[:, 0:TOKENS]).then_inc(a_inv_ready, 1)
                    dve.wait_ge(a_inv_ready, nth(n, A_GROUPS, g))
                    tt(a_on[:, g, :], a_os[:, g % 2, :], a_inv[:, g % 2, :], ALU.mult).then_inc(a_on_ready, 1)

                maximum(0)
                maximum(1)
                for h in range(A_HEADS):
                    if h + 2 < A_HEADS:
                        maximum(h + 2)
                    if h % 2 == 0:
                        dve.wait_ge(a_turned, nth(n, A_HEADS, h))
                        if h >= 2:
                            dve.wait_ge(a_mixed, nth(n, A_HEADS, h - 2))
                        nc.vector.tensor_copy(a_pt[:, 0, :, :],
                                              a_pt_ps[0][:, :].rearrange("p (t n) -> p t n", t=TILES))\
                            .then_inc(a_pt_dve, 1)
                    if h % A_PER_GROUP == 1 and h > 1:
                        divide(h // A_PER_GROUP - 1)
                divide(A_GROUPS - 1)
                dve.wait_ge(a_y_ps, nth(n, 1, 0))
                tt(y_all[:, bass.ds(n * TILES, TILES), :], a_m_ps[:, 0:TOKENS].rearrange("p (t d) -> p t d", t=TILES),
                   b_unify_sb[:, :].unsqueeze(1).broadcast_to([P, TILES, DIM]), ALU.add).then_inc(a_y_sb, 1)

            dve.wait_ge(a_y_sb, SEQS + 1)
            layernorm(2, y_all, dst=ln_xc)
            then(tt(resid[:, :, :], resid[:, :, :], ln_xc, ALU.add))
            layernorm(3, resid[:, :, :], dst=ln_xc)

            nc.vector.memset(stream[:, SEQS:, :], 0.0).then_inc(zero_ready, 1)
            nc.vector.memset(stream[:, 0:SEQS, 0:1], 0.0).then_inc(zero_ready, 1)
            nc.vector.memset(k_t[:, :, 0:WINDOW], 0.0).then_inc(zero_ready, 1)
            dve.wait_ge(in_const, 16 * CONST_LOADS)
            then(nc.vector.memset(band[:, :, :], 0.0))
            then(nc.vector.tensor_copy(ident_b[:, :], ident_f[:, :]))
            for i in range(2):
                then(nc.vector.tensor_copy(mask_b[:, i, :, :],
                                           mask_f[:, i, :].unsqueeze(1).broadcast_to([P, CHUNK_HEADS, HEAD_DIM])))

            def heads_of(ap):
                return ap.rearrange("p (h d) -> p h d", h=CHUNK_HEADS)

            def sum_squares(layer, seq, first, u):
                n = layer * SEQS + seq
                dve.wait_ge(squared, nth(n, UNITS, u))
                red(sumsq[:, u, :], heads_of(squares[:, u % 4, :]), X, ALU.add).then_inc(summed, 1)
                dve.wait_ge(summed, nth(n, UNITS, u))
                ts(clamped[:, u, :], sumsq[:, u, :], LEAST_NORM ** 2, None, ALU.max).then_inc(clamp_done, 1)

            def norm_and_cosines(layer, seq, first, u):
                n = layer * SEQS + seq
                tile, c = divmod(u, UNITS // TILES)
                dve.wait_ge(rnorm_ready, nth(n, UNITS, u))
                dve.wait_ge(raw_ready, nth(n, UNITS, u))
                if u >= 4 or not first:
                    dve.wait_ge(sin_done, nth(n, UNITS, u - 4))
                    dve.wait_ge(cos_done, nth(n, UNITS, u - 4))
                tt(heads_of(normed[:, u % 4, :]), heads_of(raw[:, u % 4, :]),
                   rnorm[:, u, :].unsqueeze(2).broadcast_to([P, CHUNK_HEADS, HEAD_DIM]), ALU.mult)\
                    .then_inc(normed_ready, 1)
                dve.wait_ge(normed_ready, nth(n, UNITS, u))
                if u >= 4 or not first:
                    dve.wait_ge(turned, nth(n, UNITS, u - 4))
                tt(heads_of(by_cos[:, u % 4, :]), heads_of(normed[:, u % 4, :]),
                   table[:, tile, 2 * (c // 2), :].unsqueeze(1).broadcast_to([P, CHUNK_HEADS, HEAD_DIM]), ALU.mult)\
                    .then_inc(cos_done, 1)

            def lower(layer, seq, first, tile):
                n = layer * SEQS + seq
                dve.wait_ge(scored, nth(n, TILES, tile))
                if not first:
                    dve.wait_ge(probs_turned, nth(n, TILES, tile - TILES))
                red(row_max[:, tile, :], score, X, ALU.max).then_inc(maxed, 1)
                dve.wait_ge(maxed, nth(n, TILES, tile))
                tt(probs[:, tile, :].rearrange("p (h j) -> p h j", h=HEADS), score,
                   row_max[:, tile, :].unsqueeze(2).broadcast_to([P, HEADS, 2 * WINDOW]), ALU.subtract)\
                    .then_inc(lowered, 1)

            def row_sums(layer, seq, first, tile):
                n = layer * SEQS + seq
                dve.wait_ge(exped, nth(n, TILES, tile))
                red(row_sum[:, tile, :], exps[:, tile, :].rearrange("p (h j) -> p h j", h=HEADS), X, ALU.add)\
                    .then_inc(row_summed, 1)
                dve.wait_ge(row_summed, nth(n, TILES, tile))
                nc.vector.reciprocal(row_inv[:, tile, :], row_sum[:, tile, :]).then_inc(inv_ready, 1)

            def turn_probs(layer, seq, first, tile):
                n = layer * SEQS + seq
                if tile == 0 and not first:
                    dve.wait_ge(mixed, nth(n, PAIRS // 2, -1))
                dve.wait_ge(probs_ready, nth(n, TILES, tile))
                nc.vector.transpose(probs_t[:, tile, :, :].rearrange("p b (h i) -> p h b i", h=HEADS),
                                    probs[:, tile, :].rearrange("p (h b j) -> p h b j", h=HEADS, b=2))\
                    .then_inc(probs_turned, 1)

            def add_output(layer, seq, first):
                n = layer * SEQS + seq
                dve.wait_ge(unified, nth(n, 1, 0))
                at = stream[:, bass.ds(seq, 1), 1:TOKENS + 1].rearrange("p a n -> p (a n)")
                tt(at, at, wo_ps[:, 0:TOKENS], ALU.add).then_inc(attn_added, 1)

            def attention_step(layer, seq, place=None):
                before, now, after = (place is None or 0 <= place + i < SEQS for i in (-1, 0, 1))
                old, this, new = ((layer, seq + i, place is not None and place + i == 0) for i in (-1, 0, 1))
                if now:
                    sum_squares(*this, 6)
                    sum_squares(*this, 7)
                    lower(*this, 0)
                if after:
                    sum_squares(*new, 0)
                if now:
                    norm_and_cosines(*this, 6)
                    norm_and_cosines(*this, 7)
                if after:
                    sum_squares(*new, 1)
                    sum_squares(*new, 2)
                if now:
                    row_sums(*this, 0)
                if after:
                    norm_and_cosines(*new, 0)
                    norm_and_cosines(*new, 1)
                    sum_squares(*new, 3)
                    sum_squares(*new, 4)
                    norm_and_cosines(*new, 2)
                if now:
                    lower(*this, 1)
                if before:
                    add_output(*old)
                if now:
                    turn_probs(*this, 0)
                if after:
                    norm_and_cosines(*new, 3)
                if now:
                    row_sums(*this, 1)
                if after:
                    sum_squares(*new, 5)
                if now:
                    turn_probs(*this, 1)
                if after:
                    norm_and_cosines(*new, 4)
                    norm_and_cosines(*new, 5)

            def ff_centre(e):
                dve.wait_ge(ff_mean, nth(e, 1, 0))
                tt(ff_xc[:, :], ff_x[:, :], ff_mean_ps[:, :], ALU.subtract).then_inc(ff_centred, 1)

            def ff_epsilon(e):
                dve.wait_ge(ff_var_done, nth(e, 1, 0))
                ts(ff_var[:, :], ff_var_ps[:, 0:FF_COLS // P], EPS, None, ALU.add).then_inc(ff_eps, 1)

            def ff_diagonals(e):
                dve.wait_ge(ff_rstd_done, nth(e, 1, 0))
                tt(ff_diag[:, :, :], ident_f[:, :].unsqueeze(1).broadcast_to([P, FF_COLS // P, P]),
                   ff_rstd[:, :].unsqueeze(2).broadcast_to([P, FF_COLS // P, P]), ALU.mult).then_inc(ff_diag_ready, 1)

            def ff_scale(e):
                dve.wait_ge(ff_rstd_wide, nth(e, 1, 0))
                tt(ff_x0[:, :], ff_xc[:, :], ff_rstd_ps[:, :], ALU.mult).then_inc(ff_scaled, 1)

            def ff_gate_of(f, k):
                rows = P if k < FF_BLOCKS - 1 else FF_LAST
                dve.wait_ge(ff_up, nth(f, 2 * FF_BLOCKS, 2 * k + 1))
                dve.wait_ge(ff_gelu, nth(f, FF_BLOCKS, k))
                nc.vector.scalar_tensor_tensor(ff_h[0:rows, k, :], ff_ps[(2 * k + 1) % 4][0:rows, :],
                                               cols_sb[0:rows, k:k + 1], ff_gate[0:rows, k, :], ALU.add, ALU.mult)\
                    .then_inc(ff_gated, 1)

            with dve.Fori(0, DEPTH) as layer:
                dve.wait_ge(in_attn, (layer + 1) * (16 * ATTN_LOADS))
                for tile in range(TILES):
                    tt(table[:, tile, :, :], rope_sb[:, tile, :, :], scales_sb[:, :, :], ALU.mult)\
                        .then_inc(table_ready, 1)
                dve.wait_ge(table_ready, (layer + 1) * TILES + 1)
                for place in (-1, 0, 1):
                    attention_step(layer, place, place)
                with dve.Fori(2, SEQS - 1) as seq:
                    attention_step(layer, seq)
                for place in (SEQS - 1, SEQS):
                    attention_step(layer, place, place)

                dve.wait_ge(in_ff, (layer + 1) * (16 * FF_LOADS))
                e0 = layer * (FF_STEPS + 1)
                ff_centre(e0)
                ff_epsilon(e0)
                ff_diagonals(e0)
                ff_scale(e0)
                with dve.Fori(0, FF_STEPS) as step:
                    f = layer * FF_STEPS + step
                    e = layer * (FF_STEPS + 1) + step
                    dve.wait_ge(ff_scaled, nth(e, 1, 0))
                    ff_centre(e + 1)
                    ff_gate_of(f, 0)
                    ff_epsilon(e + 1)
                    ff_gate_of(f, 1)
                    ff_diagonals(e + 1)
                    dve.wait_ge(ff_xn_ready, nth_of_used(e, 1, 0))
                    ff_gate_of(f, 2)
                    ff_scale(e + 1)
                    dve.wait_ge(ff_down, nth(f, 1, 0))
                    at = stream[:, bass.ds(step * FF_SEQS, FF_SEQS), 1:TOKENS + 1]
                    nc.vector.scalar_tensor_tensor(
                        at, ff_y_ps[:, :].rearrange("p (s n) -> p s n", s=FF_SEQS),
                        cols_sb[:, 2 * FF_BLOCKS:2 * FF_BLOCKS + 1], at, ALU.add, ALU.add).then_inc(ff_added, 1)

            for c in range(SEQS * TILES // 4):
                dve.wait_ge(x_turned, SEQS * TILES // 4 + c + 1)
                nc.vector.tensor_copy(y_all[:, 4 * c:4 * c + 4, :],
                                      proj[c % 2][:, :].rearrange("p (n d) -> p n d", n=4)).then_inc(out_turned, 1)
            dve.wait_ge(out_turned, SEQS * TILES // 4)
            layernorm(4, y_all, dst=ln_xc)
            for c in range(4):
                rows = slice(c * 8, (c + 1) * 8)
                tt(resid[:, rows, :], resid[:, rows, :], ln_xc[:, rows, :], ALU.add).then_inc(out_copied, 1)


def rope_tables(np):
    f = np.float32
    half = np.arange(0, HEAD_DIM, 2, dtype=f)
    inv_freq = f(1.0) / np.power(f(10000.0), half / f(HEAD_DIM))
    t = np.arange(TOKENS, dtype=f)
    freqs = t[:, None] * inv_freq[None, :]
    freqs = np.concatenate([freqs, freqs], -1)
    base = (half + f(0.4 * HEAD_DIM)) / f(1.4 * HEAD_DIM)
    power = (t - f(TOKENS // 2)) / f(WINDOW // 2)
    scale = np.power(base[None, :], power[:, None])
    scale = np.concatenate([scale, scale], -1)
    sign = np.where(np.arange(HEAD_DIM) < HEAD_DIM // 2, -1, 1).astype(f)
    cos, sin = np.cos(freqs), np.sin(freqs) * sign
    tables = np.stack([cos * scale, sin * scale, cos / scale, sin / scale], 1).astype(f)
    return np.ascontiguousarray(tables.reshape(TILES, P, 4, HEAD_DIM).transpose(1, 0, 2, 3))


def window_masks(np):
    i = np.arange(P) % WINDOW
    j = np.arange(2 * WINDOW)
    seen = (j[None, :] >= i[:, None]) & (j[None, :] <= i[:, None] + WINDOW)
    none_before = (np.arange(P) >= WINDOW)[:, None] | (j >= WINDOW)[None, :]
    both = np.stack([seen & none_before, seen], 1)
    return np.where(both, 0.0, MASKED).astype(np.float32)


def kernel(L0_attn_x, L0_attn_W_down, L0_attn_tokeys, L0_attn_toqueries, L0_attn_tovalues, L0_attn_W_unify,
           L0_attn_b_unify, L0_ffn_Wqkv, L0_ffn_q_scale, L0_ffn_k_scale, L0_ffn_Wo, L0_ffn_ln_g, L0_ffn_ln_b,
           L0_ffn_W1, L0_ffn_b1, L0_ffn_W2, L0_ffn_b2):
    import numpy as np
    import concourse.bacc as bacc
    from concourse.bass_utils import run_bass_kernel_spmd

    f = np.float32
    qk_pad = np.zeros((P, 2, A_GROUPS, P), f)
    v_block = np.zeros((P, P), f)
    w_unify = np.zeros((P, A_GROUPS, DIM), f)
    for h in range(A_HEADS):
        g, j = divmod(h, A_PER_GROUP)
        rows, cols = slice(h * A_DIM, (h + 1) * A_DIM), slice(j * A_ROWS, j * A_ROWS + A_DIM)
        qk_pad[rows, 0, g, cols] = np.asarray(L0_attn_toqueries)[h].T
        qk_pad[rows, 1, g, cols] = np.asarray(L0_attn_tokeys)[h].T
        v_block[rows, rows] = np.asarray(L0_attn_tovalues)[h].T
        w_unify[cols, g, :] = np.asarray(L0_attn_W_unify)[rows, :]
    columns = np.zeros((DEPTH, P, 2 * FF_BLOCKS + 3), f)
    b1 = np.asarray(L0_ffn_b1)
    for part in range(2):
        for k in range(FF_BLOCKS):
            rows = P if k < FF_BLOCKS - 1 else FF_LAST
            columns[:, 0:rows, part * FF_BLOCKS + k] = b1[:, part * FF + k * P:part * FF + k * P + rows]
    for i, a in enumerate((L0_ffn_b2, L0_ffn_ln_g, L0_ffn_ln_b)):
        columns[:, :, 2 * FF_BLOCKS + i] = np.asarray(a)
    w2 = np.zeros((DEPTH, FF_BLOCKS * P, DIM), f)
    w2[:, 0:FF, :] = np.asarray(L0_ffn_W2)
    qs, ks = np.asarray(L0_ffn_q_scale), np.asarray(L0_ffn_k_scale)
    scales = np.stack([qs, np.roll(qs, HEAD_DIM // 2, 1), ks, np.roll(ks, HEAD_DIM // 2, 1)], 1)
    spread = np.zeros((P, P), f)
    for j in range(A_PER_GROUP):
        spread[j * A_ROWS + A_DIM, j * A_ROWS:(j + 1) * A_ROWS] = 1.0

    arrays = {
        "x": np.asarray(L0_attn_x).reshape(SEQS * TOKENS, DIM), "w_down": np.asarray(L0_attn_W_down),
        "qk_pad": qk_pad, "v_block": v_block, "w_unify": w_unify,
        "b_unify": np.asarray(L0_attn_b_unify), "w_qkv": np.asarray(L0_ffn_Wqkv), "w_o": np.asarray(L0_ffn_Wo),
        "scales": scales, "w1": np.asarray(L0_ffn_W1), "w2": w2, "columns": columns,
        "rope": rope_tables(np), "ident": np.eye(P, dtype=f), "mask": window_masks(np), "spread": spread,
    }
    arrays = {f"in_{k}": np.ascontiguousarray(v) for k, v in arrays.items()}
    nc = bacc.Bacc("TRN2", target_bir_lowering=False, num_devices=1)
    args = [nc.dram_tensor(k, v.shape, mybir.dt.from_np(v.dtype), kind="ExternalInput").ap()
            for k, v in arrays.items()]
    result = nc.dram_tensor("result", (SEQS * TOKENS, DIM), mybir.dt.float32, kind="ExternalOutput").ap()
    build(nc, *args, result)
    r = run_bass_kernel_spmd(nc, [arrays], core_ids=[0])
    return r.results[0]["result"].reshape(SEQS, TOKENS, DIM)
```

```python
import concourse.bass as bass
from concourse import mybir
from contextlib import ExitStack

SEQS, TOKENS, DIM = 16, 256, 128
P = 128
TILES = TOKENS // P
A_HEADS, A_DIM = 16, 8
A_ROWS = 32
A_PER_GROUP = P // A_ROWS
A_GROUPS = A_HEADS // A_PER_GROUP
DEPTH, HEADS, HEAD_DIM, WINDOW = 6, 16, 64, 32
INNER = HEADS * HEAD_DIM
PAIRS = HEADS // 2
WINDOWS = TOKENS // WINDOW
TILE_WINDOWS = P // WINDOW
CHUNK = 512
CHUNK_HEADS = CHUNK // HEAD_DIM
UNITS = TILES * 2 * INNER // CHUNK
V_UNITS = TILES * INNER // CHUNK
STARTERS = 6
FF = DIM * 4 * 2 // 3
FF_BLOCKS = -(-FF // P)
FF_LAST = FF - (FF_BLOCKS - 1) * P
FF_SEQS = 2
FF_COLS = FF_SEQS * TOKENS
FF_STEPS = SEQS // FF_SEQS
LN_PARTS = 4
LN_TILES = SEQS * TILES // LN_PARTS
EPS = 1e-5
QK_SCALE = 8.0
LEAST_NORM = 1e-12
MASKED = -float(2 ** 100)


def nth(n, per_iteration, j):
    return n * per_iteration + (j + 1)


def a_bank(h):
    return 1 if h == A_HEADS - 1 else h % 3


def a_bank_before(h):
    for before in range(h - 1, h - A_HEADS, -1):
        if a_bank(before % A_HEADS) == a_bank(h):
            return before


def nth_of_used(n, per_iteration, j):
    return nth(n, per_iteration, j) + 1


def build(nc, x, w_down, qk_pad, v_block, w_unify, b_unify, w_qkv, w_o, scales, w1, w2, columns,
          rope, ident, mask, spread, out):
    f32, bf16 = mybir.dt.float32, mybir.dt.bfloat16
    ALU = mybir.AluOpType
    ACT = mybir.ActivationFunctionType
    X = mybir.AxisListType.X

    ctx = ExitStack()
    with ctx:
        def sb(name, shape, dt=f32):
            return ctx.enter_context(nc.sbuf_tensor(name, shape, dt))

        def sem(name):
            return ctx.enter_context(nc.semaphore(name))

        resid = sb("resid", [P, SEQS * TILES, DIM])
        stream = sb("stream", [P, SEQS, TOKENS + 1])
        ident_f = sb("ident_f", [P, P])
        ident_b = sb("ident_b", [P, P], bf16)
        mask_f = sb("mask_f", [P, 2, HEAD_DIM])
        mask_b = sb("mask_b", [P, 2, CHUNK_HEADS, HEAD_DIM], bf16)
        mean_w = sb("mean_w", [P, P])
        ones_w = sb("ones_w", [P, P])
        neg_half = sb("neg_half", [P, 1])
        spread_sb = sb("spread_sb", [P, P])
        stat_sum = sb("stat_sum", [P, SEQS * TILES])
        stat_mean = sb("stat_mean", [P, SEQS * TILES])
        stat_ss = sb("stat_ss", [P, SEQS * TILES])
        stat_var = sb("stat_var", [P, SEQS * TILES])
        stat_rstd = sb("stat_rstd", [P, SEQS * TILES])
        w_down_sb = sb("w_down_sb", [P, P])
        qk_pad_sb = sb("qk_pad_sb", [P, 2, A_GROUPS, P])
        v_block_sb = sb("v_block_sb", [P, P])
        w_unify_sb = sb("w_unify_sb", [P, A_GROUPS, P])
        b_unify_sb = sb("b_unify_sb", [P, DIM])
        w_qkv_sb = sb("w_qkv_sb", [P, 3 * INNER])
        w_o_sb = sb("w_o_sb", [P, PAIRS, DIM])
        w1_sb = sb("w1_sb", [P, 2 * FF])
        w2_sb = sb("w2_sb", [P, FF_BLOCKS, DIM])
        cols_sb = sb("cols_sb", [P, 2 * FF_BLOCKS + 3])
        rope_sb = sb("rope_sb", [P, TILES, 4, HEAD_DIM])
        scales_sb = sb("scales_sb", [P, 4, HEAD_DIM])
        table = sb("table", [P, TILES, 4, HEAD_DIM])
        shifted = sb("shifted", [P, TOKENS])
        shifted_v = sb("shifted_v", [P, TOKENS])
        area_d = sb("area_d", [P, 12 * CHUNK])
        raw = area_d[:, 0:4 * CHUNK].rearrange("p (u n) -> p u n", u=4)
        squares = area_d[:, 4 * CHUNK:8 * CHUNK].rearrange("p (u n) -> p u n", u=4)
        sumsq = sb("sumsq", [P, UNITS, CHUNK_HEADS])
        clamped = sb("clamped", [P, UNITS, CHUNK_HEADS])
        rnorm = sb("rnorm", [P, UNITS, CHUNK_HEADS])
        normed = sb("normed", [P, 4, CHUNK])
        by_cos = sb("by_cos", [P, 4, CHUNK])
        by_sin = sb("by_sin", [P, 4, CHUNK])
        k_t = sb("k_t", [P, PAIRS, WINDOW + TOKENS])
        row_max = sb("row_max", [P, TILES, HEADS])
        row_sum = sb("row_sum", [P, TILES, HEADS])
        row_inv = sb("row_inv", [P, TILES, HEADS])
        area_a = sb("area_a", [P, 2 * TILES * INNER])
        area_b = sb("area_b", [P, 2 * TILES * INNER])
        area_c = sb("area_c", [P, 2 * TILES * INNER])
        half = TILES * INNER
        probs = area_a[:, 0:half].rearrange("p (t n) -> p t n", t=TILES)
        exps = area_a[:, half:].rearrange("p (t n) -> p t n", t=TILES)
        v_sb = area_b[:, 0:half].rearrange("p (t n) -> p t n", t=TILES)
        att_t = area_b[:, half:].rearrange("p (c n) -> p c n", c=PAIRS)
        q_t = area_c[:, 0:half].rearrange("p (c n) -> p c n", c=PAIRS)
        probs_t = area_c[:, half:].rearrange("p (t b n) -> p t b n", t=TILES, b=2)
        band = sb("band", [P, 2 * TILE_WINDOWS + 1, HEADS * WINDOW])
        ff_area = area_a[:, :].rearrange("p (u n) -> p u n", n=FF_COLS)
        ff_x, ff_xc, ff_sq, ff_x0, ff_xn = (ff_area[:, i, :] for i in range(5))
        ff_diag = ff_area[:, 5, :].rearrange("p (c n) -> p c n", n=P)
        ff_hidden = area_b[:, :].rearrange("p (u n) -> p u n", n=FF_COLS)
        ff_gate, ff_h = ff_hidden[:, 0:3, :], ff_hidden[:, 3:6, :]
        ff_var = sb("ff_var", [P, FF_COLS // P])
        ff_rstd = sb("ff_rstd", [P, FF_COLS // P])
        ln_sq = area_a[:, :].rearrange("p (n d) -> p n d", d=DIM)
        ln_xc = area_b[:, :].rearrange("p (n d) -> p n d", d=DIM)
        y_all = area_c[:, :].rearrange("p (n d) -> p n d", d=DIM)
        flat = band[:, :, :].rearrange("p a b -> p (a b)")
        side = A_GROUPS * TOKENS
        a_qk = flat[:, 0:2 * side].rearrange("p (s g n) -> p s g n", s=2, g=A_GROUPS)
        a_v = flat[:, 2 * side:3 * side].rearrange("p (t h r) -> p t h r", t=TILES, h=A_HEADS)
        a_on = flat[:, 3 * side:4 * side].rearrange("p (g n) -> p g n", g=A_GROUPS)
        a_x = sb("a_x", [P, TILES, DIM])
        a_xt = sb("a_xt", [P, TOKENS])
        a_xd = sb("a_xd", [P, TOKENS])
        a_nmax = sb("a_nmax", [P, A_HEADS, TILES])
        a_p = area_d[:, 0:4 * TOKENS].rearrange("p (r t n) -> p r t n", r=2, t=TILES)
        a_pt = area_d[:, 4 * TOKENS:8 * TOKENS].rearrange("p (r t n) -> p r t n", r=2, t=TILES)
        a_os = area_d[:, 8 * TOKENS:10 * TOKENS].rearrange("p (r n) -> p r n", r=2)
        a_inv = area_d[:, 10 * TOKENS:12 * TOKENS].rearrange("p (r n) -> p r n", r=2)

        bank = [ctx.enter_context(nc.psum_tensor(f"bank{i}", [P, CHUNK], f32)) for i in range(6)]
        wide = ctx.enter_context(nc.psum_tensor("wide", [P, 2 * CHUNK], f32))
        proj = bank[0:2]
        turn = [bank[2], bank[5]]
        att_o = bank[3:5]
        wo_ps = bank[3]
        score = wide[:, :].rearrange("p (h j) -> p h j", j=2 * WINDOW)
        wide_half = [wide[:, 0:CHUNK], wide[:, CHUNK:2 * CHUNK]]
        ff_mean_ps, ff_var_ps = bank[0], bank[1]
        ff_ps = [bank[2][:, :], bank[3][:, :], wide_half[0], wide_half[1]]
        ff_rstd_ps = bank[0]
        ff_y_ps = bank[5]
        a_s_ps = bank[0:3]
        a_pt_ps = bank[3:5]
        a_o_ps = [wide_half[0], wide_half[1]]
        a_m_ps = bank[5]

        in_x = [sem(f"in_x{c}") for c in range(LN_PARTS)]
        in_const, in_first = sem("in_const"), sem("in_first")
        in_attn, in_ff = sem("in_attn"), sem("in_ff")
        const_ready, zero_ready, dve_step = sem("const_ready"), sem("zero_ready"), sem("dve_step")
        ln_centred, ln_squared, ln_var = sem("ln_centred"), sem("ln_squared"), sem("ln_var")
        ln_rstd, ln_scaled, ln_eps = sem("ln_rstd"), sem("ln_scaled"), sem("ln_eps")
        x_turned, stream_ready = sem("x_turned"), sem("stream_ready")
        out_turned, out_copied, out_stored = sem("out_turned"), sem("out_copied"), sem("out_stored")
        a_x_ready, a_xt_ps, a_xt_sb = sem("a_x_ready"), sem("a_xt_ps"), sem("a_xt_sb")
        a_xd_ps, a_xd_sb, a_qk_ps = sem("a_xd_ps"), sem("a_xd_sb"), sem("a_qk_ps")
        a_qk_sb, a_v_ps, a_v_sb = sem("a_qk_sb"), sem("a_v_ps"), sem("a_v_sb")
        a_scored, a_maxed, a_exped = sem("a_scored"), sem("a_maxed"), sem("a_exped")
        a_turned, a_pt_act, a_pt_dve = sem("a_turned"), sem("a_pt_act"), sem("a_pt_dve")
        a_mixed, a_o_sb, a_spread = sem("a_mixed"), sem("a_o_sb"), sem("a_spread")
        a_inv_ready, a_on_ready = sem("a_inv_ready"), sem("a_on_ready")
        a_y_ps, a_y_sb = sem("a_y_ps"), sem("a_y_sb")
        table_ready, shift_ready = sem("table_ready"), sem("shift_ready")
        projected, squared, summed = sem("projected"), sem("squared"), sem("summed")
        raw_ready, shift_v_ready = sem("raw_ready"), sem("shift_v_ready")
        clamp_done, rnorm_ready, normed_ready = sem("clamp_done"), sem("rnorm_ready"), sem("normed_ready")
        cos_done, sin_done, turned = sem("cos_done"), sem("sin_done"), sem("turned")
        qk_ready, v_projected, v_ready = sem("qk_ready"), sem("v_projected"), sem("v_ready")
        scored, maxed, lowered = sem("scored"), sem("maxed"), sem("lowered")
        exped, row_summed, inv_ready = sem("exped"), sem("row_summed"), sem("inv_ready")
        probs_ready, probs_turned, band_ready = sem("probs_ready"), sem("probs_turned"), sem("band_ready")
        mixed, att_ready, unified = sem("mixed"), sem("att_ready"), sem("unified")
        attn_added = sem("attn_added")
        ff_shifted, ff_mean, ff_centred = sem("ff_shifted"), sem("ff_mean"), sem("ff_centred")
        ff_squared, ff_var_done, ff_eps = sem("ff_squared"), sem("ff_var_done"), sem("ff_eps")
        ff_rstd_done, ff_diag_ready, ff_rstd_wide = sem("ff_rstd_done"), sem("ff_diag_ready"), sem("ff_rstd_wide")
        ff_scaled, ff_xn_ready = sem("ff_scaled"), sem("ff_xn_ready")
        ff_up, ff_gelu, ff_gated = sem("ff_up"), sem("ff_gelu"), sem("ff_gated")
        ff_down, ff_added = sem("ff_down"), sem("ff_added")

        ATTN_LOADS, FF_LOADS, CONST_LOADS, FIRST_LOADS = 3, 3, 4, 5
        BAND_COPIES = WINDOWS + WINDOWS - 1
        DONE_ATTN = SEQS
        HALF_ROWS = P // 2

        block = ctx.enter_context(nc.Block())

        @block.sync
        def _(sp):
            for c in range(LN_PARTS):
                rows = slice(c * LN_TILES, (c + 1) * LN_TILES)
                sp.dma_start(resid[:, rows, :], x.rearrange("(n p) d -> p n d", p=P)[:, rows, :]).then_inc(in_x[c], 16)
            sp.dma_start(ident_f[:, :], ident).then_inc(in_const, 16)
            sp.dma_start(mask_f[:, :, :], mask).then_inc(in_const, 16)
            sp.dma_start(rope_sb[:, :, :, :], rope).then_inc(in_const, 16)
            sp.dma_start(spread_sb[:, :], spread).then_inc(in_const, 16)
            sp.dma_start(w_down_sb[:, :], w_down).then_inc(in_first, 16)
            sp.dma_start(qk_pad_sb[:, :, :, :], qk_pad).then_inc(in_first, 16)
            sp.dma_start(v_block_sb[:, :], v_block).then_inc(in_first, 16)
            sp.dma_start(w_unify_sb[:, :, :], w_unify).then_inc(in_first, 16)
            sp.dma_start(b_unify_sb[:, :], b_unify.partition_broadcast(P)).then_inc(in_first, 16)

            def spread_band(tile):
                for w in range(TILE_WINDOWS):
                    wq = tile * TILE_WINDOWS + w
                    src = slice(w * WINDOW, (w + 1) * WINDOW)
                    sp.dma_start(band[src, wq + tile, :], probs_t[src, tile, 1, :]).then_inc(band_ready, 16)
                    if wq > 0:
                        key_tile, key_w = divmod(wq - 1, TILE_WINDOWS)
                        dst = slice(key_w * WINDOW, (key_w + 1) * WINDOW)
                        sp.dma_start(band[dst, wq + key_tile, :], probs_t[src, tile, 0, :])\
                          .then_inc(band_ready, 16)

            with sp.Fori(0, DEPTH) as layer:
                sp.wait_ge(attn_added, layer * DONE_ATTN + 1)
                sp.dma_start(w_qkv_sb[:, :], w_qkv[bass.ds(layer, 1), :, :].rearrange("a p n -> (a p) n"))\
                  .then_inc(in_attn, 16)
                sp.dma_start(w_o_sb[:, :, :], w_o[bass.ds(layer, 1), :, :].rearrange("a (c p) n -> p (a c) n", p=P))\
                  .then_inc(in_attn, 16)
                sp.wait_ge(table_ready, layer * TILES + 1)
                sp.dma_start(scales_sb[:, :, :], scales[bass.ds(layer, 1), :, :].rearrange("a c d -> a (c d)")
                             .broadcast_to([P, 4 * HEAD_DIM]).rearrange("p (c d) -> p c d", c=4)).then_inc(in_attn, 16)
                sp.wait_ge(ff_added, layer * FF_STEPS + 1)
                sp.dma_start(w1_sb[:, :], w1[bass.ds(layer, 1), :, :].rearrange("a p n -> (a p) n")).then_inc(in_ff, 16)
                sp.dma_start(w2_sb[:, :, :], w2[bass.ds(layer, 1), :, :].rearrange("a (c p) n -> p (a c) n", p=P))\
                  .then_inc(in_ff, 16)
                sp.wait_ge(ff_xn_ready, layer * FF_STEPS + 1)
                sp.dma_start(cols_sb[:, :], columns[bass.ds(layer, 1), :, :].rearrange("a p n -> (a p) n"))\
                  .then_inc(in_ff, 16)
                with sp.Fori(0, SEQS) as seq:
                    n = layer * SEQS + seq
                    for tile in range(TILES):
                        sp.wait_ge(probs_turned, nth(n, TILES, tile))
                        spread_band(tile)

            for c in range(LN_PARTS):
                sp.wait_ge(out_copied, c + 1)
                rows = slice(c * LN_TILES, (c + 1) * LN_TILES)
                sp.dma_start(out.rearrange("(n p) d -> p n d", p=P)[:, rows, :], resid[:, rows, :])\
                  .then_inc(out_stored, 16)
            sp.wait_ge(out_stored, LN_PARTS * 16)

        @block.tensor
        def _(pe):
            mm = nc.tensor.matmul

            pe.wait_ge(in_first, 16 * FIRST_LOADS)
            pe.wait_ge(in_const, 16 * CONST_LOADS)

            def a_turn_x(n, place):
                pe.wait_ge(a_x_ready, nth(n, 1, 0))
                if place != 0:
                    pe.wait_ge(a_y_sb, nth_of_used(n, 1, -2))
                for t in range(TILES):
                    last = mm(a_m_ps[:, t * P:(t + 1) * P], a_x[:, t, :], ident_f[:, :], start=True, stop=True,
                              is_transpose=True)
                last.then_inc(a_xt_ps, 1)

            def a_narrow(n, place):
                pe.wait_ge(a_xt_sb, nth(n, 1, 0))
                mm(a_m_ps[:, 0:TOKENS], w_down_sb[:, :], a_xt[:, :], start=True, stop=True).then_inc(a_xd_ps, 1)

            def a_project(n, place, g):
                if g == 0:
                    pe.wait_ge(a_xd_sb, nth(n, 1, 0))
                elif place != 0:
                    pe.wait_ge(a_on_ready, nth(n, A_GROUPS, g - 1 - A_GROUPS))
                else:
                    pe.wait_ge(a_qk_sb, nth(n, A_GROUPS, g - 1))
                for i in range(2):
                    last = mm(a_m_ps[:, i * TOKENS:(i + 1) * TOKENS], qk_pad_sb[:, i, g, :], a_xd[:, :],
                              start=True, stop=True)
                last.then_inc(a_qk_ps, 1)

            def a_scores(n, place, h):
                g, j = divmod(h, A_PER_GROUP)
                rows = slice(j * A_ROWS, (j + 1) * A_ROWS)
                pe.wait_ge(a_qk_sb, nth(n, A_GROUPS, g))
                reader = a_bank_before(h)
                if reader >= 0 or place != 0:
                    pe.wait_ge(a_exped, nth(n, A_HEADS, reader))
                for t in range(TILES):
                    last = mm(a_s_ps[a_bank(h)][:, t * TOKENS:(t + 1) * TOKENS], a_qk[rows, 0, g, t * P:(t + 1) * P],
                              a_qk[rows, 1, g, :], start=True, stop=True)
                last.then_inc(a_scored, 1)

            def a_turn_probs(n, place, h):
                pe.wait_ge(a_exped, nth(n, A_HEADS, h))
                if h >= 2 or place != 0:
                    pe.wait_ge(a_pt_dve if h % 2 == 0 else a_pt_act, nth(n, A_HEADS // 2, h // 2 - 1))
                for kb in range(TILES):
                    for t in range(TILES):
                        at = kb * TOKENS + t * P
                        last = mm(a_pt_ps[h % 2][:, at:at + P], a_p[:, h % 2, t, kb * P:(kb + 1) * P],
                                  ident_f[:, :], start=True, stop=True, is_transpose=True)
                last.then_inc(a_turned, 1)

            def a_mix(n, place, h):
                g, j = divmod(h, A_PER_GROUP)
                pe.wait_ge(a_pt_dve if h % 2 == 0 else a_pt_act, nth(n, A_HEADS // 2, h // 2))
                if h == 0:
                    pe.wait_ge(a_v_sb, nth(n, 1, 0))
                if j == 0 and (g >= 2 or place != 0):
                    pe.wait_ge(a_o_sb, nth(n, A_GROUPS, g - 2))
                rows = slice(j * A_ROWS, (j + 1) * A_ROWS)
                for kb in range(TILES):
                    last = mm(a_o_ps[g % 2][rows, 0:TOKENS], a_v[:, kb, h, :], a_pt[:, h % 2, kb, :],
                              start=kb == 0, stop=kb == TILES - 1)
                last.then_inc(a_mixed, 1)

            def a_spread_sums(n, place, g):
                pe.wait_ge(a_o_sb, nth(n, A_GROUPS, g))
                if place != SEQS - 1:
                    pe.wait_ge(a_qk_sb, nth(n + 1, A_GROUPS, g))
                elif g > 0:
                    pe.wait_ge(a_on_ready, nth(n, A_GROUPS, g - 1))
                mm(a_m_ps[:, 0:TOKENS], spread_sb[:, :], a_os[:, g % 2, :], start=True, stop=True)\
                    .then_inc(a_spread, 1)

            def a_project_v(n, place):
                if place != 0:
                    pe.wait_ge(a_on_ready, nth(n, A_GROUPS, -1))
                else:
                    pe.wait_ge(a_qk_sb, nth(n, A_GROUPS, A_GROUPS - 1))
                for t in range(TILES):
                    last = mm(a_m_ps[:, t * P:(t + 1) * P], a_xd[:, t * P:(t + 1) * P], v_block_sb[:, :],
                              start=True, stop=True)
                last.then_inc(a_v_ps, 1)

            def a_unify(n, place):
                pe.wait_ge(a_on_ready, nth(n, A_GROUPS, A_GROUPS - 1))
                if place != SEQS - 1:
                    pe.wait_ge(a_v_sb, nth(n + 1, 1, 0))
                for t in range(TILES):
                    for g in range(A_GROUPS):
                        last = mm(a_m_ps[:, t * P:(t + 1) * P], a_on[:, g, t * P:(t + 1) * P], w_unify_sb[:, g, :],
                                  start=g == 0, stop=g == A_GROUPS - 1)
                last.then_inc(a_y_ps, 1)

            def a_step(seq, place=None):
                before, now, after = (place is None or 0 <= place + i < SEQS for i in (-1, 0, 1))
                old, this, new = ((seq + i, None if place is None else place + i) for i in (-1, 0, 1))
                if before:
                    a_mix(*old, 6)
                    a_turn_probs(*old, 7)
                    a_scores(*old, 11)
                    a_turn_probs(*old, 8)
                    a_scores(*old, 12)
                    a_turn_probs(*old, 9)
                    a_mix(*old, 7)
                if now:
                    a_project(*this, 1)
                if before:
                    a_scores(*old, 13)
                    a_mix(*old, 8)
                    a_turn_probs(*old, 10)
                    a_mix(*old, 9)
                    a_spread_sums(*old, 1)
                    a_turn_probs(*old, 11)
                    a_scores(*old, 14)
                    a_turn_probs(*old, 12)
                    a_mix(*old, 10)
                    a_mix(*old, 11)
                    a_turn_probs(*old, 13)
                    a_scores(*old, 15)
                if now:
                    a_project(*this, 2)
                    a_scores(*this, 0)
                if before:
                    a_spread_sums(*old, 2)
                    a_mix(*old, 12)
                    a_mix(*old, 13)
                    a_turn_probs(*old, 14)
                if now:
                    a_scores(*this, 1)
                if before:
                    a_turn_probs(*old, 15)
                if now:
                    a_scores(*this, 2)
                    a_project(*this, 3)
                if before:
                    a_mix(*old, 14)
                    a_mix(*old, 15)
                if now:
                    a_turn_probs(*this, 0)
                    a_scores(*this, 3)
                if before:
                    a_spread_sums(*old, 3)
                if now:
                    a_turn_probs(*this, 1)
                    a_turn_probs(*this, 2)
                    a_scores(*this, 4)
                    a_scores(*this, 5)
                    a_turn_probs(*this, 3)
                    a_project_v(*this)
                    a_scores(*this, 6)
                    a_mix(*this, 0)
                if before:
                    a_unify(*old)
                if now:
                    a_scores(*this, 7)
                if after:
                    a_turn_x(*new)
                if now:
                    a_turn_probs(*this, 4)
                    a_mix(*this, 1)
                    a_scores(*this, 8)
                if after:
                    a_narrow(*new)
                if now:
                    a_mix(*this, 2)
                    a_turn_probs(*this, 5)
                    a_mix(*this, 3)
                    a_scores(*this, 9)
                    a_turn_probs(*this, 6)
                    a_mix(*this, 4)
                if after:
                    a_project(*new, 0)
                if now:
                    a_mix(*this, 5)
                    a_scores(*this, 10)
                    a_spread_sums(*this, 0)

            for place in (-1, 0, 1):
                a_step(place, place)
            with pe.Fori(2, SEQS - 2) as seq:
                a_step(seq)
            for place in (SEQS - 2, SEQS - 1, SEQS):
                a_step(place, place)

            for c in range(SEQS * TILES // 4):
                pe.wait_ge(ln_scaled, nth(1, LN_PARTS, 4 * c // LN_TILES))
                if c >= 2:
                    pe.wait_ge(stream_ready, c - 1)
                for i in range(4):
                    last = mm(proj[c % 2][:, i * P:(i + 1) * P], ln_xc[:, 4 * c + i, :], ident_f[:, :],
                              start=True, stop=True, is_transpose=True)
                last.then_inc(x_turned, 1)

            def project(layer, seq, first, u):
                n = layer * SEQS + seq
                tile, c = divmod(u, UNITS // TILES)
                if u == 0:
                    pe.wait_ge(shift_ready, nth_of_used(n, 1, 0))
                starts = first and u < STARTERS
                if not starts:
                    pe.wait_ge(raw_ready, nth(n, UNITS, u - 1))
                elif u >= 2:
                    pe.wait_ge(raw_ready, nth(n, UNITS, u - 2))
                mm(proj[u % 2 if starts else 0][:, :], shifted[:, tile * P:(tile + 1) * P], w_qkv_sb[:, c * CHUNK:(c + 1) * CHUNK],
                   start=True, stop=True).then_inc(projected, 1)

            def project_v(layer, seq, first, j):
                n = layer * SEQS + seq
                c, tile = divmod(j, TILES)
                if j == 0:
                    pe.wait_ge(shift_v_ready, nth(n, 1, 0))
                if j > 0 or not first:
                    pe.wait_ge(v_ready, nth(n, V_UNITS, j - 1))
                at = 2 * INNER + c * CHUNK
                mm(proj[1][:, :], shifted_v[:, tile * P:(tile + 1) * P], w_qkv_sb[:, at:at + CHUNK],
                   start=True, stop=True).then_inc(v_projected, 1)

            def scores(layer, seq, first, tile):
                n = layer * SEQS + seq
                pe.wait_ge(qk_ready, nth(n, UNITS, (tile + 1) * (UNITS // TILES) - 1))
                if tile > 0 or not first:
                    pe.wait_ge(lowered, nth(n, TILES, tile - 1))
                for odd in range(2):
                    mm(wide_half[odd], ident_b[:, :], mask_b[:, 0 if tile == 0 else 1, :, :]
                       .rearrange("p h j -> p (h j)"), start=True, stop=False, skip_group_check=True)
                for pair in range(PAIRS):
                    for w in range(TILE_WINDOWS):
                        for odd in range(2):
                            rows = slice(odd * HEAD_DIM, (odd + 1) * HEAD_DIM)
                            at = tile * P + w * WINDOW
                            last = mm(score[w * WINDOW:(w + 1) * WINDOW, odd * PAIRS + pair, :],
                                      q_t[rows, pair, at:at + WINDOW], k_t[rows, pair, at:at + 2 * WINDOW],
                                      start=False, stop=True, skip_group_check=True)
                last.then_inc(scored, 1)

            def turn_unit(layer, seq, first, u):
                n = layer * SEQS + seq
                pe.wait_ge(cos_done, nth(n, UNITS, u))
                pe.wait_ge(sin_done, nth(n, UNITS, u))
                if u >= 2 or not first:
                    pe.wait_ge(qk_ready, nth(n, UNITS, u - 2))
                for i in range(CHUNK // P):
                    at = slice(i * P, (i + 1) * P)
                    mm(turn[u % 2][:, at], by_cos[:, u % 4, at], ident_f[:, :], start=True, stop=False,
                       is_transpose=True)
                    last = mm(turn[u % 2][:, at], by_sin[:, u % 4, at], ident_f[:, :], start=False, stop=True,
                              is_transpose=True)
                last.then_inc(turned, 1)

            def mix(layer, seq, first, j):
                n = layer * SEQS + seq
                if j == 0:
                    pe.wait_ge(band_ready, n * (16 * BAND_COPIES) + 16 * BAND_COPIES)
                    pe.wait_ge(v_ready, nth(n, V_UNITS, V_UNITS - 1))
                    pe.wait_ge(attn_added, nth_of_used(n, 1, -1))
                if j >= 2:
                    pe.wait_ge(att_ready, nth(n, PAIRS // 2, j - 2))
                cut = (TILE_WINDOWS + 1) * WINDOW
                for i in range(2):
                    pair = 2 * j + i
                    for odd in range(2):
                        rows = slice(odd * HEAD_DIM, (odd + 1) * HEAD_DIM)
                        at = (odd * PAIRS + pair) * WINDOW
                        feats = slice((2 * pair + odd) * HEAD_DIM, (2 * pair + odd + 1) * HEAD_DIM)
                        mm(att_o[j % 2][rows, i * TOKENS:i * TOKENS + cut], v_sb[:, 0, feats],
                           band[:, 0:TILE_WINDOWS + 1, at:at + WINDOW], start=True, stop=False, skip_group_check=True)
                        last = mm(att_o[j % 2][rows, i * TOKENS + P:(i + 1) * TOKENS], v_sb[:, 1, feats],
                                  band[:, TILE_WINDOWS + 1:, at:at + WINDOW], start=False, stop=True,
                                  skip_group_check=True)
                last.then_inc(mixed, 1)

            def unify(layer, seq, first):
                n = layer * SEQS + seq
                pe.wait_ge(att_ready, nth(n, PAIRS // 2, PAIRS // 2 - 1))
                for pair in range(PAIRS):
                    product = mm(wo_ps[:, 0:TOKENS], w_o_sb[:, pair, :], att_t[:, pair, :], start=pair == 0,
                                 stop=pair == PAIRS - 1)
                product.then_inc(unified, 1)

            def attention_step(layer, seq, place=None):
                before, now, after = (place is None or 0 <= place + i < SEQS for i in (-1, 0, 1))
                old, this, new = ((layer, seq + i, place is not None and place + i == 0) for i in (-1, 0, 1))
                if before:
                    project_v(*old, 1)
                if now:
                    project(*this, 6)
                if before:
                    project_v(*old, 2)
                if now:
                    turn_unit(*this, 2)
                    turn_unit(*this, 3)
                if before:
                    project_v(*old, 3)
                if place == SEQS:
                    pe.wait_ge(in_ff, (layer + 1) * (16 * FF_LOADS))
                    ff_mean_of(layer * FF_STEPS)
                    ff_var_of(layer * FF_STEPS)
                    ff_rstd_of(layer * FF_STEPS)
                if now:
                    project(*this, 7)
                    scores(*this, 0)
                if after:
                    project(*new, 0)
                if now:
                    turn_unit(*this, 4)
                    project_v(*this, 0)
                if after:
                    project(*new, 1)
                if now:
                    turn_unit(*this, 5)
                if before:
                    mix(*old, 0)
                if after:
                    project(*new, 2)
                if before:
                    mix(*old, 1)
                    mix(*old, 2)
                if after:
                    project(*new, 3)
                if now:
                    turn_unit(*this, 6)
                    turn_unit(*this, 7)
                if before:
                    mix(*old, 3)
                if after:
                    project(*new, 4)
                if now:
                    scores(*this, 1)
                if before:
                    unify(*old)
                if after:
                    project(*new, 5)
                    turn_unit(*new, 0)
                    turn_unit(*new, 1)

            def ff_mean_of(e):
                pe.wait_ge(ff_shifted, nth(e, 1, 0))
                mm(ff_mean_ps[:, :], mean_w[:, :], ff_x[:, :], start=True, stop=True).then_inc(ff_mean, 1)

            def ff_var_of(e):
                pe.wait_ge(ff_squared, nth(e, 1, 0))
                for i in range(FF_COLS // P):
                    last = mm(ff_var_ps[:, i:i + 1], ff_sq[:, i * P:(i + 1) * P], mean_w[:, 0:1], start=True, stop=True)
                last.then_inc(ff_var_done, 1)

            def ff_rstd_of(e):
                pe.wait_ge(ff_diag_ready, nth(e, 1, 0))
                mm(ff_rstd_ps[:, :], ones_w[:, :], ff_diag[:, :, :].rearrange("p c n -> p (c n)"), start=True,
                   stop=True).then_inc(ff_rstd_wide, 1)

            def ff_up_of(f, k, wait=None):
                rows = P if k < FF_BLOCKS - 1 else FF_LAST
                for i, at in enumerate((FF + k * P, k * P)):
                    b = (2 * k + i) % 4
                    if k == 2:
                        if i == 0:
                            pe.wait_ge(ff_gelu, nth(f, FF_BLOCKS, 0))
                        else:
                            pe.wait_ge(ff_gated, nth_of_used(f, FF_BLOCKS, 0))
                    mm(ff_ps[b][0:rows, :], w1_sb[:, at:at + rows], ff_xn[:, :], start=True, stop=True)\
                        .then_inc(ff_up, 1)

            def ff_step(layer, step, last=False):
                f = layer * FF_STEPS + step
                pe.wait_ge(attn_added, (layer + 1) * SEQS + 1)
                pe.wait_ge(ff_xn_ready, nth_of_used(f, 1, 0))
                pe.wait_ge(ff_gated, nth_of_used(f, FF_BLOCKS, -1))
                ff_up_of(f, 0)
                if not last:
                    ff_mean_of(f + 1)
                ff_up_of(f, 1)
                if not last:
                    ff_var_of(f + 1)
                ff_up_of(f, 2)
                if not last:
                    ff_rstd_of(f + 1)
                pe.wait_ge(ff_added, nth_of_used(f, 1, -1))
                for k in range(FF_BLOCKS):
                    rows = P if k < FF_BLOCKS - 1 else FF_LAST
                    pe.wait_ge(ff_gated, nth_of_used(f, FF_BLOCKS, k))
                    product = mm(ff_y_ps[:, :], w2_sb[0:rows, k, :], ff_h[0:rows, k, :], start=k == 0,
                                 stop=k == FF_BLOCKS - 1)
                product.then_inc(ff_down, 1)

            with pe.Fori(0, DEPTH) as layer:
                pe.wait_ge(in_attn, (layer + 1) * (16 * ATTN_LOADS))
                for place in (-1, 0, 1):
                    attention_step(layer, place, place)
                with pe.Fori(2, SEQS - 1) as seq:
                    attention_step(layer, seq)
                for place in (SEQS - 1, SEQS):
                    attention_step(layer, place, place)

                with pe.Fori(0, FF_STEPS - 1) as step:
                    ff_step(layer, step)
                ff_step(layer, FF_STEPS - 1, last=True)

            pe.wait_ge(ff_added, DEPTH * FF_STEPS + 1)
            for c in range(SEQS * TILES // 4):
                if c >= 2:
                    pe.wait_ge(out_turned, c - 1)
                for i in range(4):
                    seq, tile = divmod(4 * c + i, TILES)
                    last = mm(proj[c % 2][:, i * P:(i + 1) * P], stream[:, seq, 1 + tile * P:1 + (tile + 1) * P],
                              ident_f[:, :], start=True, stop=True, is_transpose=True)
                last.then_inc(x_turned, 1)

        @block.scalar
        def _(act):
            av = nc.scalar.activation

            def ln_square(i):
                for c in range(LN_PARTS):
                    act.wait_ge(ln_centred, nth(i, LN_PARTS, c))
                    rows = slice(c * LN_TILES, (c + 1) * LN_TILES)
                    av(ln_sq[:, rows, :], ln_xc[:, rows, :], ACT.Square).then_inc(ln_squared, 1)

            for used in (ff_xn_ready, shift_ready):
                act.sem_inc(used, 1)
            ln_square(0)
            def a_take_x(n, place):
                act.wait_ge(a_xt_ps, nth(n, 1, 0))
                av(a_xt[:, :], a_m_ps[:, 0:TOKENS], ACT.Copy).then_inc(a_xt_sb, 1)

            def a_take_narrow(n, place):
                act.wait_ge(a_xd_ps, nth(n, 1, 0))
                av(a_xd[:, :], a_m_ps[:, 0:TOKENS], ACT.Copy).then_inc(a_xd_sb, 1)

            def a_take_qk(n, place, g):
                act.wait_ge(a_qk_ps, nth(n, A_GROUPS, g))
                if place != 0:
                    act.wait_ge(a_scored, nth(n, A_HEADS, (g + 1) * A_PER_GROUP - 1 - A_HEADS))
                av(a_qk[:, :, g, :], a_m_ps[:, :].rearrange("p (s n) -> p s n", s=2), ACT.Copy,
                   scale=float(A_DIM) ** -0.25).then_inc(a_qk_sb, 1)

            def a_exponentials(n, place, h):
                act.wait_ge(a_maxed, nth(n, A_HEADS, h))
                if h >= 2 or place != 0:
                    act.wait_ge(a_turned, nth(n, A_HEADS, h - 2))
                for t in range(TILES):
                    last = av(a_p[:, h % 2, t, :], a_s_ps[a_bank(h)][:, t * TOKENS:(t + 1) * TOKENS], ACT.Exp,
                              bias=a_nmax[:, h, t:t + 1])
                last.then_inc(a_exped, 1)

            def a_take_odd(n, place, h):
                act.wait_ge(a_turned, nth(n, A_HEADS, h))
                if h >= 2 or place != 0:
                    act.wait_ge(a_mixed, nth(n, A_HEADS, h - 2))
                av(a_pt[:, 1, :, :], a_pt_ps[1][:, :].rearrange("p (t n) -> p t n", t=TILES), ACT.Copy)\
                    .then_inc(a_pt_act, 1)

            def a_take_out(n, place, g):
                act.wait_ge(a_mixed, nth(n, A_HEADS, (g + 1) * A_PER_GROUP - 1))
                if g >= 2 or place != 0:
                    act.wait_ge(a_on_ready, nth(n, A_GROUPS, g - 2))
                av(a_os[:, g % 2, :], a_o_ps[g % 2][:, 0:TOKENS], ACT.Copy).then_inc(a_o_sb, 1)

            def a_step(seq, place=None):
                before, now, after = (place is None or 0 <= place + i < SEQS for i in (-1, 0, 1))
                old, this, new = ((seq + i, None if place is None else place + i) for i in (-1, 0, 1))
                if before:
                    a_exponentials(*old, 8)
                if now:
                    a_take_qk(*this, 0)
                if before:
                    a_exponentials(*old, 9)
                    a_take_odd(*old, 7)
                    a_exponentials(*old, 10)
                    a_take_out(*old, 1)
                    a_take_odd(*old, 9)
                if now:
                    a_take_qk(*this, 1)
                if before:
                    a_exponentials(*old, 11)
                    a_exponentials(*old, 12)
                    a_take_odd(*old, 11)
                    a_exponentials(*old, 13)
                    a_take_out(*old, 2)
                    a_take_odd(*old, 13)
                    a_exponentials(*old, 14)
                if now:
                    a_take_qk(*this, 2)
                if before:
                    a_exponentials(*old, 15)
                    a_take_odd(*old, 15)
                if now:
                    a_exponentials(*this, 0)
                    a_exponentials(*this, 1)
                    a_take_qk(*this, 3)
                if before:
                    a_take_out(*old, 3)
                if now:
                    a_exponentials(*this, 2)
                    a_take_odd(*this, 1)
                    a_exponentials(*this, 3)
                    a_exponentials(*this, 4)
                    a_exponentials(*this, 5)
                if after:
                    a_take_x(*new)
                if now:
                    a_take_odd(*this, 3)
                    a_exponentials(*this, 6)
                if after:
                    a_take_narrow(*new)
                if now:
                    a_take_odd(*this, 5)
                    a_exponentials(*this, 7)
                    a_take_out(*this, 0)

            for place in (-1, 0, 1):
                a_step(place, place)
            with act.Fori(2, SEQS - 2) as seq:
                a_step(seq)
            for place in (SEQS - 2, SEQS - 1, SEQS):
                a_step(place, place)

            ln_square(1)
            ln_square(2)
            for c in range(SEQS * TILES // 4):
                act.wait_ge(x_turned, c + 1)
                if c == 0:
                    act.wait_ge(zero_ready, 2)
                av(stream[:, 2 * c:2 * c + 2, 1:TOKENS + 1], proj[c % 2][:, :].rearrange("p (s n) -> p s n", s=2),
                   ACT.Copy).then_inc(stream_ready, 1)

            def shift(layer, seq, first):
                n = layer * SEQS + seq
                if not first:
                    act.wait_ge(projected, nth(n, UNITS, -1))
                    act.wait_ge(shift_v_ready, nth(n, 1, -1))
                av(shifted[0:HALF_ROWS, :], stream[0:HALF_ROWS, bass.ds(seq, 1), 1:TOKENS + 1]
                   .rearrange("p a n -> p (a n)"), ACT.Copy)
                av(shifted[HALF_ROWS:P, :], stream[HALF_ROWS:P, bass.ds(seq, 1), 0:TOKENS]
                   .rearrange("p a n -> p (a n)"), ACT.Copy).then_inc(shift_ready, 1)

            def square(layer, seq, first, u):
                n = layer * SEQS + seq
                act.wait_ge(projected, nth(n, UNITS, u))
                if u >= 4 or not first:
                    act.wait_ge(summed, nth(n, UNITS, u - 4))
                source = proj[u % 2 if first and u < STARTERS else 0]
                av(squares[:, u % 4, :], source[:, :], ACT.Square).then_inc(squared, 1)
                if u >= 4 or not first:
                    act.wait_ge(normed_ready, nth(n, UNITS, u - 4))
                av(raw[:, u % 4, :], source[:, :], ACT.Copy).then_inc(raw_ready, 1)

            def keep_shifted(layer, seq, first):
                n = layer * SEQS + seq
                act.wait_ge(projected, nth(n, UNITS, 0))
                if not first:
                    act.wait_ge(v_projected, nth(n, V_UNITS, -1))
                av(shifted_v[:, :], shifted[:, :], ACT.Copy).then_inc(shift_v_ready, 1)

            def take_unit(layer, seq, first, u):
                n = layer * SEQS + seq
                if u in (0, 2) and not first:
                    act.wait_ge(scored, nth(n, TILES, -2 if u == 0 else -1))
                tile, c = divmod(u, UNITS // TILES)
                pairs = slice((c % 2) * (PAIRS // 2), (c % 2 + 1) * (PAIRS // 2))
                act.wait_ge(turned, nth(n, UNITS, u))
                dst = q_t[:, pairs, tile * P:(tile + 1) * P] if c < 2 else \
                    k_t[:, pairs, WINDOW + tile * P:WINDOW + (tile + 1) * P]
                av(dst, turn[u % 2][:, :].rearrange("p (c n) -> p c n", c=PAIRS // 2), ACT.Copy).then_inc(qk_ready, 1)

            def take_v(layer, seq, first, j):
                n = layer * SEQS + seq
                c, tile = divmod(j, TILES)
                act.wait_ge(v_projected, nth(n, V_UNITS, j))
                if j == 0 and not first:
                    act.wait_ge(mixed, nth(n, PAIRS // 2, -1))
                av(v_sb[:, tile, c * CHUNK:(c + 1) * CHUNK], proj[1][:, :], ACT.Copy).then_inc(v_ready, 1)

            def exponentials(layer, seq, first, tile):
                n = layer * SEQS + seq
                act.wait_ge(lowered, nth(n, TILES, tile))
                av(exps[:, tile, :], probs[:, tile, :], ACT.Exp, scale=QK_SCALE).then_inc(exped, 1)

            def take_out(layer, seq, first, j):
                n = layer * SEQS + seq
                act.wait_ge(mixed, nth(n, PAIRS // 2, j))
                av(att_t[:, 2 * j:2 * j + 2, :], att_o[j % 2][:, :].rearrange("p (c n) -> p c n", c=2), ACT.Copy)\
                    .then_inc(att_ready, 1)

            def attention_step(layer, seq, place=None):
                before, now, after = (place is None or 0 <= place + i < SEQS for i in (-1, 0, 1))
                old, this, new = ((layer, seq + i, place is not None and place + i == 0) for i in (-1, 0, 1))
                if now:
                    take_unit(*this, 0)
                if before:
                    take_v(*old, 1)
                if now:
                    take_unit(*this, 1)
                    square(*this, 6)
                if before:
                    take_v(*old, 2)
                if now:
                    take_unit(*this, 2)
                    take_unit(*this, 3)
                if before:
                    take_v(*old, 3)
                if place == SEQS:
                    act.wait_ge(attn_added, nth_of_used(layer * SEQS, 1, FF_SEQS - 1))
                    act.wait_ge(probs_turned, (layer + 1) * (SEQS * TILES))
                    ff_shift(0)
                    ff_square(layer * FF_STEPS)
                    act.wait_ge(in_ff, (layer + 1) * (16 * FF_LOADS))
                    ff_affine(layer * FF_STEPS)
                if now:
                    keep_shifted(*this)
                if after:
                    shift(*new)
                if now:
                    square(*this, 7)
                if after:
                    square(*new, 0)
                if now:
                    take_unit(*this, 4)
                if after:
                    square(*new, 1)
                if now:
                    take_unit(*this, 5)
                if before:
                    take_out(*old, 0)
                if after:
                    square(*new, 2)
                if before:
                    take_out(*old, 1)
                if now:
                    exponentials(*this, 0)
                if before:
                    take_out(*old, 2)
                if now:
                    take_unit(*this, 6)
                if after:
                    square(*new, 3)
                if now:
                    take_unit(*this, 7)
                if after:
                    square(*new, 4)
                if now:
                    take_v(*this, 0)
                if before:
                    take_out(*old, 3)
                if after:
                    square(*new, 5)
                if now:
                    exponentials(*this, 1)

            def ff_shift(step):
                seqs = bass.ds(step * FF_SEQS, FF_SEQS)
                for rows, start in ((slice(0, HALF_ROWS), 1), (slice(HALF_ROWS, P), 0)):
                    last = av(ff_x[rows, :].rearrange("p (s n) -> p s n", s=FF_SEQS),
                              stream[rows, seqs, start:start + TOKENS], ACT.Copy)
                last.then_inc(ff_shifted, 1)

            def ff_square(e):
                act.wait_ge(ff_centred, nth(e, 1, 0))
                av(ff_sq[:, :], ff_xc[:, :], ACT.Square).then_inc(ff_squared, 1)

            def ff_affine(e):
                act.wait_ge(ff_scaled, nth(e, 1, 0))
                av(ff_xn[:, :], ff_x0[:, :], ACT.Identity, bias=cols_sb[:, 2 * FF_BLOCKS + 2:],
                   scale=cols_sb[:, 2 * FF_BLOCKS + 1:2 * FF_BLOCKS + 2]).then_inc(ff_xn_ready, 1)

            def ff_gelu_of(f, k):
                rows = P if k < FF_BLOCKS - 1 else FF_LAST
                act.wait_ge(ff_up, nth(f, 2 * FF_BLOCKS, 2 * k))
                av(ff_gate[0:rows, k, :], ff_ps[(2 * k) % 4][0:rows, :], ACT.Gelu,
                   bias=cols_sb[0:rows, FF_BLOCKS + k:FF_BLOCKS + k + 1]).then_inc(ff_gelu, 1)

            def ff_step(f, step, last=False):
                if not last:
                    act.wait_ge(ff_centred, nth(f, 1, 0))
                    ff_shift(step + 1)
                ff_gelu_of(f, 0)
                if not last:
                    ff_square(f + 1)
                ff_gelu_of(f, 1)
                ff_gelu_of(f, 2)
                if not last:
                    act.wait_ge(ff_up, nth(f, 2 * FF_BLOCKS, 2 * FF_BLOCKS - 1))
                    ff_affine(f + 1)

            with act.Fori(0, DEPTH) as layer:
                act.wait_ge(stream_ready, SEQS * TILES // 4)
                for place in (-1, 0, 1):
                    attention_step(layer, place, place)
                with act.Fori(2, SEQS - 1) as seq:
                    attention_step(layer, seq)
                for place in (SEQS - 1, SEQS):
                    attention_step(layer, place, place)

                act.wait_ge(attn_added, (layer + 1) * SEQS + 1)
                with act.Fori(0, FF_STEPS - 1) as step:
                    ff_step(layer * FF_STEPS + step, step)
                ff_step(layer * FF_STEPS + FF_STEPS - 1, FF_STEPS - 1, last=True)
            ln_square(3)

        @block.gpsimd
        def _(pool):
            tt = nc.gpsimd.tensor_tensor

            nc.gpsimd.memset(mean_w[:, :], 1.0 / DIM).then_inc(const_ready, 1)
            nc.gpsimd.memset(neg_half[:, :], -0.5).then_inc(const_ready, 1)
            nc.gpsimd.memset(ones_w[:, :], 1.0).then_inc(const_ready, 1)
            pool.wait_ge(const_ready, 3)

            def power(out_, in_, width):
                return tt(out_, in_, neg_half[:, 0:1].broadcast_to([P, width]), ALU.pow)

            def ln_power(i):
                for c in range(LN_PARTS):
                    pool.wait_ge(ln_var, nth(i, LN_PARTS, c))
                    rows = slice(c * LN_TILES, (c + 1) * LN_TILES)
                    power(stat_rstd[:, rows], stat_var[:, rows], LN_TILES).then_inc(ln_rstd, 1)

            for i in range(3):
                ln_power(i)

            def rnorms(layer, seq, first, u):
                n = layer * SEQS + seq
                pool.wait_ge(clamp_done, nth(n, UNITS, u))
                power(rnorm[:, u, :], clamped[:, u, :], CHUNK_HEADS).then_inc(rnorm_ready, 1)

            def sines(layer, seq, first, u):
                n = layer * SEQS + seq
                tile, c = divmod(u, UNITS // TILES)
                pool.wait_ge(normed_ready, nth(n, UNITS, u))
                if u >= 4 or not first:
                    pool.wait_ge(turned, nth(n, UNITS, u - 4))
                src = normed[:, u % 4, :].rearrange("p (h b d) -> p h b d", h=CHUNK_HEADS, b=2)
                dst = by_sin[:, u % 4, :].rearrange("p (h b d) -> p h b d", h=CHUNK_HEADS, b=2)
                tab = table[:, tile, 2 * (c // 2) + 1, :].rearrange("p (b d) -> p b d", b=2)
                for b in range(2):
                    last = tt(dst[:, :, b, :], src[:, :, 1 - b, :],
                              tab[:, b, :].unsqueeze(1).broadcast_to([P, CHUNK_HEADS, HEAD_DIM // 2]), ALU.mult)
                last.then_inc(sin_done, 1)

            def normalise(layer, seq, first, tile):
                n = layer * SEQS + seq
                pool.wait_ge(inv_ready, nth(n, TILES, tile))
                tt(probs[:, tile, :].rearrange("p (h j) -> p h j", h=HEADS),
                   exps[:, tile, :].rearrange("p (h j) -> p h j", h=HEADS),
                   row_inv[:, tile, :].unsqueeze(2).broadcast_to([P, HEADS, 2 * WINDOW]), ALU.mult)\
                    .then_inc(probs_ready, 1)

            def attention_step(layer, seq, place=None):
                before, now, after = (place is None or 0 <= place + i < SEQS for i in (-1, 0, 1))
                old, this, new = ((layer, seq + i, place is not None and place + i == 0) for i in (-1, 0, 1))
                if now:
                    rnorms(*this, 6)
                    rnorms(*this, 7)
                if after:
                    rnorms(*new, 0)
                if now:
                    sines(*this, 6)
                    sines(*this, 7)
                if after:
                    rnorms(*new, 1)
                    rnorms(*new, 2)
                    sines(*new, 0)
                    sines(*new, 1)
                if now:
                    normalise(*this, 0)
                if after:
                    rnorms(*new, 3)
                    rnorms(*new, 4)
                    sines(*new, 2)
                    sines(*new, 3)
                if now:
                    normalise(*this, 1)
                if after:
                    rnorms(*new, 5)
                    sines(*new, 4)
                    sines(*new, 5)

            def ff_power(e):
                pool.wait_ge(ff_eps, nth(e, 1, 0))
                power(ff_rstd[:, :], ff_var[:, :], FF_COLS // P).then_inc(ff_rstd_done, 1)

            with pool.Fori(0, DEPTH) as layer:
                pool.wait_ge(table_ready, (layer + 1) * TILES + 1)
                for place in (-1, 0, 1):
                    attention_step(layer, place, place)
                with pool.Fori(2, SEQS - 1) as seq:
                    attention_step(layer, seq)
                for place in (SEQS - 1, SEQS):
                    attention_step(layer, place, place)
                with pool.Fori(0, FF_STEPS) as step:
                    ff_power(layer * FF_STEPS + step)
            ln_power(3)

        @block.vector
        def _(dve):
            tt, ts, red = nc.vector.tensor_tensor, nc.vector.tensor_scalar, nc.vector.tensor_reduce
            steps = [0]

            def then(ins):
                steps[0] += 1
                ins.then_inc(dve_step, 1)
                dve.wait_ge(dve_step, steps[0])

            def layernorm(i, src, ready=None, scale=True, use=None):
                parts = [slice(c * LN_TILES, (c + 1) * LN_TILES) for c in range(LN_PARTS)]

                def wide(stat, rows):
                    return stat[:, rows].unsqueeze(2).broadcast_to([P, LN_TILES, DIM])

                for c, rows in enumerate(parts):
                    if ready is not None:
                        ready(c)
                    then(red(stat_sum[:, rows], src[:, rows, :], X, ALU.add))
                    then(ts(stat_mean[:, rows], stat_sum[:, rows], 1.0 / DIM, None, ALU.mult))
                    tt(ln_xc[:, rows, :], src[:, rows, :], wide(stat_mean, rows), ALU.subtract).then_inc(ln_centred, 1)
                for c, rows in enumerate(parts):
                    dve.wait_ge(ln_squared, nth(i, LN_PARTS, c))
                    then(red(stat_ss[:, rows], ln_sq[:, rows, :], X, ALU.add))
                    ts(stat_var[:, rows], stat_ss[:, rows], 1.0 / DIM, EPS, ALU.mult, ALU.add).then_inc(ln_var, 1)
                for c, rows in enumerate(parts):
                    dve.wait_ge(ln_rstd, nth(i, LN_PARTS, c))
                    if scale:
                        dve.wait_ge(ln_centred, nth(i, LN_PARTS, c))
                        tt(ln_xc[:, rows, :], ln_xc[:, rows, :], wide(stat_rstd, rows), ALU.mult).then_inc(ln_scaled, 1)
                    if use is not None:
                        dve.wait_ge(ln_scaled, nth(i - 1, LN_PARTS, c))
                        use(c, rows)

            for used in (attn_added, table_ready, ff_added, ff_gated, a_y_sb):
                dve.sem_inc(used, 1)
            layernorm(0, resid, ready=lambda c: dve.wait_ge(in_x[c], 16), scale=False)
            dve.wait_ge(ln_centred, LN_PARTS)
            then(nc.vector.memset(flat[:, :], 0.0))
            then(nc.vector.memset(a_v[:, :, :, A_DIM:A_DIM + 1], 1.0))
            dve.wait_ge(in_first, 16 * FIRST_LOADS)
            def a_scale_x(n, place):
                if place != 0:
                    dve.wait_ge(a_xt_ps, nth(n, 1, -1))
                tt(a_x[:, :, :], ln_xc[:, bass.ds(n * TILES, TILES), :],
                   stat_rstd[:, bass.ds(n * TILES, TILES)].unsqueeze(2).broadcast_to([P, TILES, DIM]), ALU.mult)\
                    .then_inc(a_x_ready, 1)

            def a_take_v(n, place):
                dve.wait_ge(a_v_ps, nth(n, 1, 0))
                if place != 0:
                    dve.wait_ge(a_mixed, nth(n, A_HEADS, -1))
                nc.vector.tensor_copy(a_v[:, :, :, 0:A_DIM],
                                      a_m_ps[:, 0:TOKENS].rearrange("p (t h d) -> p t h d", t=TILES, h=A_HEADS))\
                    .then_inc(a_v_sb, 1)

            def a_maximum(n, place, h):
                dve.wait_ge(a_scored, nth(n, A_HEADS, h))
                red(a_nmax[:, h, :], a_s_ps[a_bank(h)][:, :].rearrange("p (t n) -> p t n", t=TILES), X, ALU.max,
                    negate=True).then_inc(a_maxed, 1)

            def a_take_even(n, place, h):
                dve.wait_ge(a_turned, nth(n, A_HEADS, h))
                if h >= 2 or place != 0:
                    dve.wait_ge(a_mixed, nth(n, A_HEADS, h - 2))
                nc.vector.tensor_copy(a_pt[:, 0, :, :], a_pt_ps[0][:, :].rearrange("p (t n) -> p t n", t=TILES))\
                    .then_inc(a_pt_dve, 1)

            def a_divide(n, place, g):
                dve.wait_ge(a_spread, nth(n, A_GROUPS, g))
                nc.vector.reciprocal(a_inv[:, g % 2, :], a_m_ps[:, 0:TOKENS]).then_inc(a_inv_ready, 1)
                dve.wait_ge(a_inv_ready, nth(n, A_GROUPS, g))
                if g == 0 and place != 0:
                    dve.wait_ge(a_y_ps, nth(n, 1, -1))
                tt(a_on[:, g, :], a_os[:, g % 2, :], a_inv[:, g % 2, :], ALU.mult).then_inc(a_on_ready, 1)

            def a_add_bias(n, place):
                dve.wait_ge(a_y_ps, nth(n, 1, 0))
                tt(y_all[:, bass.ds(n * TILES, TILES), :], a_m_ps[:, 0:TOKENS].rearrange("p (t d) -> p t d", t=TILES),
                   b_unify_sb[:, :].unsqueeze(1).broadcast_to([P, TILES, DIM]), ALU.add).then_inc(a_y_sb, 1)

            def a_step(seq, place=None):
                before, now, after = (place is None or 0 <= place + i < SEQS for i in (-1, 0, 1))
                old, this, new = ((seq + i, None if place is None else place + i) for i in (-1, 0, 1))
                if before:
                    a_take_even(*old, 8)
                if after:
                    a_scale_x(*new)
                if before:
                    a_maximum(*old, 12)
                    a_maximum(*old, 13)
                    a_take_even(*old, 10)
                    a_divide(*old, 1)
                    a_maximum(*old, 14)
                    a_take_even(*old, 12)
                    a_maximum(*old, 15)
                if now:
                    a_maximum(*this, 0)
                if before:
                    a_divide(*old, 2)
                if now:
                    a_maximum(*this, 1)
                if before:
                    a_take_even(*old, 14)
                if now:
                    a_maximum(*this, 2)
                    a_take_even(*this, 0)
                    a_maximum(*this, 3)
                if before:
                    a_divide(*old, 3)
                if now:
                    a_maximum(*this, 4)
                    a_take_v(*this)
                    a_maximum(*this, 5)
                    a_take_even(*this, 2)
                if before:
                    a_add_bias(*old)
                if now:
                    a_maximum(*this, 6)
                    a_maximum(*this, 7)
                    a_maximum(*this, 8)
                    a_take_even(*this, 4)
                    a_maximum(*this, 9)
                    a_take_even(*this, 6)
                    a_maximum(*this, 10)
                    a_divide(*this, 0)
                    a_maximum(*this, 11)

            for place in (-1, 0, 1):
                a_step(place, place)
            with dve.Fori(2, SEQS - 2) as seq:
                a_step(seq)
            for place in (SEQS - 2, SEQS - 1, SEQS):
                a_step(place, place)

            dve.wait_ge(a_y_sb, SEQS + 1)
            layernorm(1, y_all, use=lambda c, rows: then(
                tt(resid[:, rows, :], resid[:, rows, :], ln_xc[:, rows, :], ALU.add)))
            layernorm(2, resid)

            nc.vector.memset(stream[:, 0:SEQS, 0:1], 0.0).then_inc(zero_ready, 1)
            nc.vector.memset(k_t[:, :, 0:WINDOW], 0.0).then_inc(zero_ready, 1)
            dve.wait_ge(in_const, 16 * CONST_LOADS)
            then(nc.vector.memset(band[:, :, :], 0.0))
            then(nc.vector.tensor_copy(ident_b[:, :], ident_f[:, :]))
            for i in range(2):
                then(nc.vector.tensor_copy(mask_b[:, i, :, :],
                                           mask_f[:, i, :].unsqueeze(1).broadcast_to([P, CHUNK_HEADS, HEAD_DIM])))

            def heads_of(ap):
                return ap.rearrange("p (h d) -> p h d", h=CHUNK_HEADS)

            def sum_squares(layer, seq, first, u):
                n = layer * SEQS + seq
                dve.wait_ge(squared, nth(n, UNITS, u))
                red(sumsq[:, u, :], heads_of(squares[:, u % 4, :]), X, ALU.add).then_inc(summed, 1)
                dve.wait_ge(summed, nth(n, UNITS, u))
                ts(clamped[:, u, :], sumsq[:, u, :], LEAST_NORM ** 2, None, ALU.max).then_inc(clamp_done, 1)

            def norm_and_cosines(layer, seq, first, u):
                n = layer * SEQS + seq
                tile, c = divmod(u, UNITS // TILES)
                dve.wait_ge(rnorm_ready, nth(n, UNITS, u))
                dve.wait_ge(raw_ready, nth(n, UNITS, u))
                if u >= 4 or not first:
                    dve.wait_ge(sin_done, nth(n, UNITS, u - 4))
                    dve.wait_ge(cos_done, nth(n, UNITS, u - 4))
                tt(heads_of(normed[:, u % 4, :]), heads_of(raw[:, u % 4, :]),
                   rnorm[:, u, :].unsqueeze(2).broadcast_to([P, CHUNK_HEADS, HEAD_DIM]), ALU.mult)\
                    .then_inc(normed_ready, 1)
                dve.wait_ge(normed_ready, nth(n, UNITS, u))
                if u >= 4 or not first:
                    dve.wait_ge(turned, nth(n, UNITS, u - 4))
                tt(heads_of(by_cos[:, u % 4, :]), heads_of(normed[:, u % 4, :]),
                   table[:, tile, 2 * (c // 2), :].unsqueeze(1).broadcast_to([P, CHUNK_HEADS, HEAD_DIM]), ALU.mult)\
                    .then_inc(cos_done, 1)

            def lower(layer, seq, first, tile):
                n = layer * SEQS + seq
                dve.wait_ge(scored, nth(n, TILES, tile))
                if not first:
                    dve.wait_ge(probs_turned, nth(n, TILES, tile - TILES))
                red(row_max[:, tile, :], score, X, ALU.max).then_inc(maxed, 1)
                dve.wait_ge(maxed, nth(n, TILES, tile))
                tt(probs[:, tile, :].rearrange("p (h j) -> p h j", h=HEADS), score,
                   row_max[:, tile, :].unsqueeze(2).broadcast_to([P, HEADS, 2 * WINDOW]), ALU.subtract)\
                    .then_inc(lowered, 1)

            def row_sums(layer, seq, first, tile):
                n = layer * SEQS + seq
                dve.wait_ge(exped, nth(n, TILES, tile))
                red(row_sum[:, tile, :], exps[:, tile, :].rearrange("p (h j) -> p h j", h=HEADS), X, ALU.add)\
                    .then_inc(row_summed, 1)
                dve.wait_ge(row_summed, nth(n, TILES, tile))
                nc.vector.reciprocal(row_inv[:, tile, :], row_sum[:, tile, :]).then_inc(inv_ready, 1)

            def turn_probs(layer, seq, first, tile):
                n = layer * SEQS + seq
                if tile == 0 and not first:
                    dve.wait_ge(mixed, nth(n, PAIRS // 2, -1))
                dve.wait_ge(probs_ready, nth(n, TILES, tile))
                nc.vector.transpose(probs_t[:, tile, :, :].rearrange("p b (h i) -> p h b i", h=HEADS),
                                    probs[:, tile, :].rearrange("p (h b j) -> p h b j", h=HEADS, b=2))\
                    .then_inc(probs_turned, 1)

            def add_output(layer, seq, first):
                n = layer * SEQS + seq
                dve.wait_ge(unified, nth(n, 1, 0))
                at = stream[:, bass.ds(seq, 1), 1:TOKENS + 1].rearrange("p a n -> p (a n)")
                tt(at, at, wo_ps[:, 0:TOKENS], ALU.add).then_inc(attn_added, 1)

            def attention_step(layer, seq, place=None):
                before, now, after = (place is None or 0 <= place + i < SEQS for i in (-1, 0, 1))
                old, this, new = ((layer, seq + i, place is not None and place + i == 0) for i in (-1, 0, 1))
                if now:
                    sum_squares(*this, 6)
                    sum_squares(*this, 7)
                    lower(*this, 0)
                if after:
                    sum_squares(*new, 0)
                if now:
                    norm_and_cosines(*this, 6)
                    norm_and_cosines(*this, 7)
                if after:
                    sum_squares(*new, 1)
                    sum_squares(*new, 2)
                if now:
                    row_sums(*this, 0)
                if after:
                    norm_and_cosines(*new, 0)
                    norm_and_cosines(*new, 1)
                    sum_squares(*new, 3)
                    sum_squares(*new, 4)
                    norm_and_cosines(*new, 2)
                if now:
                    lower(*this, 1)
                if place == SEQS:
                    dve.wait_ge(in_ff, (layer + 1) * (16 * FF_LOADS))
                    ff_centre(layer * FF_STEPS)
                    ff_epsilon(layer * FF_STEPS)
                    ff_diagonals(layer * FF_STEPS)
                    ff_scale(layer * FF_STEPS)
                if before:
                    add_output(*old)
                if now:
                    turn_probs(*this, 0)
                if after:
                    norm_and_cosines(*new, 3)
                if now:
                    row_sums(*this, 1)
                if after:
                    sum_squares(*new, 5)
                if now:
                    turn_probs(*this, 1)
                if after:
                    norm_and_cosines(*new, 4)
                    norm_and_cosines(*new, 5)

            def ff_centre(e):
                dve.wait_ge(ff_mean, nth(e, 1, 0))
                tt(ff_xc[:, :], ff_x[:, :], ff_mean_ps[:, :], ALU.subtract).then_inc(ff_centred, 1)

            def ff_epsilon(e):
                dve.wait_ge(ff_var_done, nth(e, 1, 0))
                ts(ff_var[:, :], ff_var_ps[:, 0:FF_COLS // P], EPS, None, ALU.add).then_inc(ff_eps, 1)

            def ff_diagonals(e):
                dve.wait_ge(ff_rstd_done, nth(e, 1, 0))
                tt(ff_diag[:, :, :], ident_f[:, :].unsqueeze(1).broadcast_to([P, FF_COLS // P, P]),
                   ff_rstd[:, :].unsqueeze(2).broadcast_to([P, FF_COLS // P, P]), ALU.mult).then_inc(ff_diag_ready, 1)

            def ff_scale(e):
                dve.wait_ge(ff_rstd_wide, nth(e, 1, 0))
                tt(ff_x0[:, :], ff_xc[:, :], ff_rstd_ps[:, :], ALU.mult).then_inc(ff_scaled, 1)

            def ff_gate_of(f, k):
                rows = P if k < FF_BLOCKS - 1 else FF_LAST
                dve.wait_ge(ff_up, nth(f, 2 * FF_BLOCKS, 2 * k + 1))
                dve.wait_ge(ff_gelu, nth(f, FF_BLOCKS, k))
                nc.vector.scalar_tensor_tensor(ff_h[0:rows, k, :], ff_ps[(2 * k + 1) % 4][0:rows, :],
                                               cols_sb[0:rows, k:k + 1], ff_gate[0:rows, k, :], ALU.add, ALU.mult)\
                    .then_inc(ff_gated, 1)

            def ff_step(f, step, last=False):
                if not last:
                    dve.wait_ge(ff_scaled, nth(f, 1, 0))
                    ff_centre(f + 1)
                ff_gate_of(f, 0)
                if not last:
                    ff_epsilon(f + 1)
                ff_gate_of(f, 1)
                if not last:
                    ff_diagonals(f + 1)
                    dve.wait_ge(ff_xn_ready, nth_of_used(f, 1, 0))
                ff_gate_of(f, 2)
                if not last:
                    ff_scale(f + 1)
                dve.wait_ge(ff_down, nth(f, 1, 0))
                at = stream[:, bass.ds(step * FF_SEQS, FF_SEQS), 1:TOKENS + 1]
                nc.vector.scalar_tensor_tensor(
                    at, ff_y_ps[:, :].rearrange("p (s n) -> p s n", s=FF_SEQS),
                    cols_sb[:, 2 * FF_BLOCKS:2 * FF_BLOCKS + 1], at, ALU.add, ALU.add).then_inc(ff_added, 1)

            with dve.Fori(0, DEPTH) as layer:
                dve.wait_ge(in_attn, (layer + 1) * (16 * ATTN_LOADS))
                for tile in range(TILES):
                    tt(table[:, tile, :, :], rope_sb[:, tile, :, :], scales_sb[:, :, :], ALU.mult)\
                        .then_inc(table_ready, 1)
                dve.wait_ge(table_ready, (layer + 1) * TILES + 1)
                for place in (-1, 0, 1):
                    attention_step(layer, place, place)
                with dve.Fori(2, SEQS - 1) as seq:
                    attention_step(layer, seq)
                for place in (SEQS - 1, SEQS):
                    attention_step(layer, place, place)

                with dve.Fori(0, FF_STEPS - 1) as step:
                    ff_step(layer * FF_STEPS + step, step)
                ff_step(layer * FF_STEPS + FF_STEPS - 1, FF_STEPS - 1, last=True)

            def take_output(part):
                for c in range(part * LN_TILES // 4, (part + 1) * LN_TILES // 4):
                    dve.wait_ge(x_turned, SEQS * TILES // 4 + c + 1)
                    nc.vector.tensor_copy(y_all[:, 4 * c:4 * c + 4, :],
                                          proj[c % 2][:, :].rearrange("p (n d) -> p n d", n=4)).then_inc(out_turned, 1)
                dve.wait_ge(out_turned, (part + 1) * LN_TILES // 4)

            layernorm(3, y_all, ready=take_output, use=lambda c, rows: tt(
                resid[:, rows, :], resid[:, rows, :], ln_xc[:, rows, :], ALU.add).then_inc(out_copied, 1))


def rope_tables(np):
    f = np.float32
    half = np.arange(0, HEAD_DIM, 2, dtype=f)
    inv_freq = f(1.0) / np.power(f(10000.0), half / f(HEAD_DIM))
    t = np.arange(TOKENS, dtype=f)
    freqs = t[:, None] * inv_freq[None, :]
    freqs = np.concatenate([freqs, freqs], -1)
    base = (half + f(0.4 * HEAD_DIM)) / f(1.4 * HEAD_DIM)
    power = (t - f(TOKENS // 2)) / f(WINDOW // 2)
    scale = np.power(base[None, :], power[:, None])
    scale = np.concatenate([scale, scale], -1)
    sign = np.where(np.arange(HEAD_DIM) < HEAD_DIM // 2, -1, 1).astype(f)
    cos, sin = np.cos(freqs), np.sin(freqs) * sign
    tables = np.stack([cos * scale, sin * scale, cos / scale, sin / scale], 1).astype(f)
    return np.ascontiguousarray(tables.reshape(TILES, P, 4, HEAD_DIM).transpose(1, 0, 2, 3))


def window_masks(np):
    i = np.arange(P) % WINDOW
    j = np.arange(2 * WINDOW)
    seen = (j[None, :] >= i[:, None]) & (j[None, :] <= i[:, None] + WINDOW)
    none_before = (np.arange(P) >= WINDOW)[:, None] | (j >= WINDOW)[None, :]
    both = np.stack([seen & none_before, seen], 1)
    return np.where(both, 0.0, MASKED).astype(np.float32)


def kernel(L0_attn_x, L0_attn_W_down, L0_attn_tokeys, L0_attn_toqueries, L0_attn_tovalues, L0_attn_W_unify,
           L0_attn_b_unify, L0_ffn_Wqkv, L0_ffn_q_scale, L0_ffn_k_scale, L0_ffn_Wo, L0_ffn_ln_g, L0_ffn_ln_b,
           L0_ffn_W1, L0_ffn_b1, L0_ffn_W2, L0_ffn_b2):
    import numpy as np
    import concourse.bacc as bacc
    from concourse.bass_utils import run_bass_kernel_spmd

    f = np.float32
    qk_pad = np.zeros((P, 2, A_GROUPS, P), f)
    v_block = np.zeros((P, P), f)
    w_unify = np.zeros((P, A_GROUPS, DIM), f)
    for h in range(A_HEADS):
        g, j = divmod(h, A_PER_GROUP)
        rows, cols = slice(h * A_DIM, (h + 1) * A_DIM), slice(j * A_ROWS, j * A_ROWS + A_DIM)
        qk_pad[rows, 0, g, cols] = np.asarray(L0_attn_toqueries)[h].T
        qk_pad[rows, 1, g, cols] = np.asarray(L0_attn_tokeys)[h].T
        v_block[rows, rows] = np.asarray(L0_attn_tovalues)[h].T
        w_unify[cols, g, :] = np.asarray(L0_attn_W_unify)[rows, :]
    columns = np.zeros((DEPTH, P, 2 * FF_BLOCKS + 3), f)
    b1 = np.asarray(L0_ffn_b1)
    for part in range(2):
        for k in range(FF_BLOCKS):
            rows = P if k < FF_BLOCKS - 1 else FF_LAST
            columns[:, 0:rows, part * FF_BLOCKS + k] = b1[:, part * FF + k * P:part * FF + k * P + rows]
    for i, a in enumerate((L0_ffn_b2, L0_ffn_ln_g, L0_ffn_ln_b)):
        columns[:, :, 2 * FF_BLOCKS + i] = np.asarray(a)
    w2 = np.zeros((DEPTH, FF_BLOCKS * P, DIM), f)
    w2[:, 0:FF, :] = np.asarray(L0_ffn_W2)
    qs, ks = np.asarray(L0_ffn_q_scale), np.asarray(L0_ffn_k_scale)
    scales = np.stack([qs, np.roll(qs, HEAD_DIM // 2, 1), ks, np.roll(ks, HEAD_DIM // 2, 1)], 1)
    spread = np.zeros((P, P), f)
    for j in range(A_PER_GROUP):
        spread[j * A_ROWS + A_DIM, j * A_ROWS:(j + 1) * A_ROWS] = 1.0

    arrays = {
        "x": np.asarray(L0_attn_x).reshape(SEQS * TOKENS, DIM), "w_down": np.asarray(L0_attn_W_down),
        "qk_pad": qk_pad, "v_block": v_block, "w_unify": w_unify,
        "b_unify": np.asarray(L0_attn_b_unify), "w_qkv": np.asarray(L0_ffn_Wqkv), "w_o": np.asarray(L0_ffn_Wo),
        "scales": scales, "w1": np.asarray(L0_ffn_W1), "w2": w2, "columns": columns,
        "rope": rope_tables(np), "ident": np.eye(P, dtype=f), "mask": window_masks(np), "spread": spread,
    }
    arrays = {f"in_{k}": np.ascontiguousarray(v) for k, v in arrays.items()}
    nc = bacc.Bacc("TRN2", target_bir_lowering=False, num_devices=1)
    args = [nc.dram_tensor(k, v.shape, mybir.dt.from_np(v.dtype), kind="ExternalInput").ap()
            for k, v in arrays.items()]
    result = nc.dram_tensor("result", (SEQS * TOKENS, DIM), mybir.dt.float32, kind="ExternalOutput").ap()
    build(nc, *args, result)
    r = run_bass_kernel_spmd(nc, [arrays], core_ids=[0])
    return r.results[0]["result"].reshape(SEQS, TOKENS, DIM)
```
